# Optimizing a Trainium2 kernel written in Bass

```python
import numpy as np
import jax
import jax.numpy as jnp

def _softmax(x, axis=-1):
    return jax.nn.softmax(x, axis=axis)

def _gelu(x):
    return jax.nn.gelu(x, approximate=True)

def _silu(x):
    return jax.nn.silu(x)

def _sigmoid(x):
    return jax.nn.sigmoid(x)

def _layernorm(x, axis=-1, eps=1e-05):
    m = jnp.mean(x, axis=axis, keepdims=True)
    v = jnp.var(x, axis=axis, keepdims=True)
    return (x - m) / jnp.sqrt(v + eps)

def _scatter_add(tgt, idx, src, axis=0):
    return tgt.at[idx].add(src)

def _segment_sum(src, seg, n):
    return jax.ops.segment_sum(src, seg, n)
kernel_name = 'mk_recurrent_d2_jaxref_r8_7e23df'

def setup_inputs(seed: int=0):
    np.random.seed(seed)
    _w = jnp.asarray

    def _L0_attn_setup():
        import jax, jax.numpy as jnp
        import numpy as np
        key = jax.random.key(seed)
        B, N, D = (32, 128, 128)
        x = jax.random.normal(key, (B, N, D), dtype=jnp.float32)
        return {'x': x}
    _L0_attn_in = _L0_attn_setup()

    def _L0_ffn_setup():
        import jax, jax.numpy as jnp
        import numpy as np
        D_MODEL = 128
        NUM_TILES = 64
        TPC = 8
        NUM_CLUSTERS = NUM_TILES // TPC
        GRID = 16
        COMP_H = 32
        NUM_KNOTS = 8
        EPS_LN = 1e-05

        def _calibrate(scores, knots, temperature):
            K = knots.shape[0]
            normalized = jax.nn.sigmoid(scores / (temperature[0] + 1e-06))
            idx_float = normalized * (K - 1)
            idx_low = jnp.clip(idx_float.astype(jnp.int32), 0, K - 2)
            idx_high = idx_low + 1
            t = idx_float - idx_low.astype(scores.dtype)
            val_low = knots[idx_low]
            val_high = knots[idx_high]
            return val_low + t * (val_high - val_low)

        def _forward(x, signatures_raw, knot_values, temperature, compress_w1, compress_b1, compress_w2, compress_b2, spline_w1, spline_b1, spline_w2, spline_b2, directions, norm_gamma, norm_beta, output_scale):
            B, T, D = x.shape
            xf = x.reshape(-1, D)
            q = jnp.where(signatures_raw > 0.3, 1.0, jnp.where(signatures_raw < -0.3, -1.0, 0.0)).astype(signatures_raw.dtype)
            sigs = signatures_raw + jax.lax.stop_gradient(q - signatures_raw)
            cluster_sigs = jnp.sign(sigs.reshape(NUM_CLUSTERS, TPC, D).mean(axis=1))
            cluster_scores = xf @ cluster_sigs.T
            cluster_gates = _calibrate(cluster_scores, knot_values, temperature)
            cluster_idx = jnp.argmax(cluster_gates, axis=-1)
            tile_scores = xf @ sigs.T
            tile_gates = _calibrate(tile_scores, knot_values, temperature)
            gates_by_cluster = tile_gates.reshape(-1, NUM_CLUSTERS, TPC)
            sel_gates = jnp.take_along_axis(gates_by_cluster, cluster_idx[:, None, None], axis=1)[:, 0, :]
            local_idx = jnp.argmax(sel_gates, axis=-1)
            tile_idx = cluster_idx * TPC + local_idx
            h = jax.nn.gelu(xf @ compress_w1 + compress_b1, approximate=False)
            comp = jnp.tanh(h @ compress_w2 + compress_b2)
            w1 = spline_w1[tile_idx]
            b1 = spline_b1[tile_idx]
            hh = jax.nn.relu(jnp.einsum('ni,nig->ng', comp, w1) + b1)
            w2 = spline_w2[tile_idx]
            b2 = spline_b2[tile_idx]
            mag = jnp.einsum('ng,ngo->no', hh, w2) + b2
            ffn_out = mag * directions[tile_idx] * output_scale[0]
            y = xf + ffn_out
            mu = y.mean(axis=-1, keepdims=True)
            var = ((y - mu) ** 2).mean(axis=-1, keepdims=True)
            y = (y - mu) / jnp.sqrt(var + EPS_LN) * norm_gamma + norm_beta
            return y.reshape(B, T, D)
        key = jax.random.key(seed)
        ks = jax.random.split(key, 12)
        B, T = (4, 512)
        x = jax.random.normal(ks[0], (B, T, D_MODEL), dtype=jnp.float32)
        signatures_raw = jax.random.normal(ks[1], (NUM_TILES, D_MODEL), dtype=jnp.float32) * 0.5
        knot_values = jax.nn.sigmoid(jnp.linspace(-3.0, 3.0, NUM_KNOTS).astype(jnp.float32))
        temperature = jnp.ones((1,), dtype=jnp.float32)
        compress_w1 = jax.random.normal(ks[2], (D_MODEL, COMP_H), dtype=jnp.float32) * (1.0 / np.sqrt(D_MODEL))
        compress_b1 = jnp.zeros((COMP_H,), dtype=jnp.float32)
        compress_w2 = jax.random.normal(ks[3], (COMP_H, 2), dtype=jnp.float32) * (1.0 / np.sqrt(COMP_H))
        compress_b2 = jnp.zeros((2,), dtype=jnp.float32)
        spline_w1 = jax.random.normal(ks[4], (NUM_TILES, 2, GRID), dtype=jnp.float32) * (1.0 / np.sqrt(2.0))
        spline_b1 = jnp.zeros((NUM_TILES, GRID), dtype=jnp.float32)
        spline_w2 = jax.random.normal(ks[5], (NUM_TILES, GRID, 1), dtype=jnp.float32) * (1.0 / np.sqrt(GRID))
        spline_b2 = jnp.zeros((NUM_TILES, 1), dtype=jnp.float32)
        directions = jax.random.normal(ks[6], (NUM_TILES, D_MODEL), dtype=jnp.float32) * 0.02
        norm_gamma = jnp.ones((D_MODEL,), dtype=jnp.float32)
        norm_beta = jnp.zeros((D_MODEL,), dtype=jnp.float32)
        output_scale = jnp.ones((1,), dtype=jnp.float32) * 0.1
        return dict(x=x, signatures_raw=signatures_raw, knot_values=knot_values, temperature=temperature, compress_w1=compress_w1, compress_b1=compress_b1, compress_w2=compress_w2, compress_b2=compress_b2, spline_w1=spline_w1, spline_b1=spline_b1, spline_w2=spline_w2, spline_b2=spline_b2, directions=directions, norm_gamma=norm_gamma, norm_beta=norm_beta, output_scale=output_scale)
    _L0_ffn_in = _L0_ffn_setup()

    def _L1_attn_setup():
        import jax, jax.numpy as jnp
        import numpy as np
        D_MODEL = 128
        N_HEADS = 16
        D_HEAD = D_MODEL // N_HEADS
        B, T = (2, 256)
        EPS = 1e-05
        key = jax.random.key(seed)
        ks = jax.random.split(key, 5)
        s = 1.0 / np.sqrt(D_MODEL)
        return {'x': jax.random.normal(ks[0], (B, T, D_MODEL), dtype=jnp.float32), 'W_q': jax.random.normal(ks[1], (D_MODEL, D_MODEL), dtype=jnp.float32) * s, 'W_k': jax.random.normal(ks[2], (D_MODEL, D_MODEL), dtype=jnp.float32) * s, 'W_v': jax.random.normal(ks[3], (D_MODEL, D_MODEL), dtype=jnp.float32) * s, 'W_o': jax.random.normal(ks[4], (D_MODEL, D_MODEL), dtype=jnp.float32) * s, 'gn_weight': jnp.ones((D_MODEL,), dtype=jnp.float32), 'gn_bias': jnp.zeros((D_MODEL,), dtype=jnp.float32)}
    _L1_attn_in = _L1_attn_setup()

    def _L1_ffn_setup():
        import jax, jax.numpy as jnp
        import numpy as np
        NUM_EXPERTS = 8
        CAPACITY = 80
        key = jax.random.key(seed)
        ks = jax.random.split(key, 5)
        D, E, F = (128, NUM_EXPERTS, 512)
        inputs = jax.random.normal(ks[0], (2, 256, D), dtype=jnp.float32)
        gate_w = jax.random.normal(ks[1], (D, E), dtype=jnp.float32) * 0.02
        gate_b = jnp.zeros((E,), dtype=jnp.float32)
        w1 = jax.random.normal(ks[2], (E, D, F), dtype=jnp.float32) * 0.02
        b1 = jnp.zeros((E, F), dtype=jnp.float32)
        w2 = jax.random.normal(ks[3], (E, F, D), dtype=jnp.float32) * 0.02
        b2 = jnp.zeros((E, D), dtype=jnp.float32)
        return {'inputs': inputs, 'gate_w': gate_w, 'gate_b': gate_b, 'w1': w1, 'b1': b1, 'w2': w2, 'b2': b2}
    _L1_ffn_in = _L1_ffn_setup()
    _d = {'L0_attn_x': _L0_attn_in['x'], 'L0_ffn_signatures_raw': _L0_ffn_in['signatures_raw'], 'L0_ffn_knot_values': _L0_ffn_in['knot_values'], 'L0_ffn_temperature': _L0_ffn_in['temperature'], 'L0_ffn_compress_w1': _L0_ffn_in['compress_w1'], 'L0_ffn_compress_b1': _L0_ffn_in['compress_b1'], 'L0_ffn_compress_w2': _L0_ffn_in['compress_w2'], 'L0_ffn_compress_b2': _L0_ffn_in['compress_b2'], 'L0_ffn_spline_w1': _L0_ffn_in['spline_w1'], 'L0_ffn_spline_b1': _L0_ffn_in['spline_b1'], 'L0_ffn_spline_w2': _L0_ffn_in['spline_w2'], 'L0_ffn_spline_b2': _L0_ffn_in['spline_b2'], 'L0_ffn_directions': _L0_ffn_in['directions'], 'L0_ffn_norm_gamma': _L0_ffn_in['norm_gamma'], 'L0_ffn_norm_beta': _L0_ffn_in['norm_beta'], 'L0_ffn_output_scale': _L0_ffn_in['output_scale'], 'L1_attn_W_q': _L1_attn_in['W_q'], 'L1_attn_W_k': _L1_attn_in['W_k'], 'L1_attn_W_v': _L1_attn_in['W_v'], 'L1_attn_W_o': _L1_attn_in['W_o'], 'L1_attn_gn_weight': _L1_attn_in['gn_weight'], 'L1_attn_gn_bias': _L1_attn_in['gn_bias'], 'L1_ffn_gate_w': _L1_ffn_in['gate_w'], 'L1_ffn_gate_b': _L1_ffn_in['gate_b'], 'L1_ffn_w1': _L1_ffn_in['w1'], 'L1_ffn_b1': _L1_ffn_in['b1'], 'L1_ffn_w2': _L1_ffn_in['w2'], 'L1_ffn_b2': _L1_ffn_in['b2']}
    _x0 = _d['L0_attn_x']
    _d['L0_attn_x'] = jax.random.normal(jax.random.fold_in(jax.random.key(seed), 1), (2, 1024, 128), dtype=_x0.dtype)
    del _x0
    return _d

def reference(L0_attn_x, L0_ffn_signatures_raw, L0_ffn_knot_values, L0_ffn_temperature, L0_ffn_compress_w1, L0_ffn_compress_b1, L0_ffn_compress_w2, L0_ffn_compress_b2, L0_ffn_spline_w1, L0_ffn_spline_b1, L0_ffn_spline_w2, L0_ffn_spline_b2, L0_ffn_directions, L0_ffn_norm_gamma, L0_ffn_norm_beta, L0_ffn_output_scale, L1_attn_W_q, L1_attn_W_k, L1_attn_W_v, L1_attn_W_o, L1_attn_gn_weight, L1_attn_gn_bias, L1_ffn_gate_w, L1_ffn_gate_b, L1_ffn_w1, L1_ffn_b1, L1_ffn_w2, L1_ffn_b2):

    def _L0_attn_ref(x):
        import jax, jax.numpy as jnp
        import numpy as np
        logp = jax.nn.log_softmax(x, axis=-1)
        p = jnp.exp(logp)
        neg_ent = jnp.sum(p * logp, axis=-1)
        cross = jnp.einsum('bid,bjd->bij', p, logp)
        kl = neg_ent[:, :, None] - cross
        attn = jax.nn.softmax(-kl, axis=-1)
        out = jnp.einsum('bij,bjd->bid', attn, x)
        return out

    def _L0_ffn_ref(x, signatures_raw, knot_values, temperature, compress_w1, compress_b1, compress_w2, compress_b2, spline_w1, spline_b1, spline_w2, spline_b2, directions, norm_gamma, norm_beta, output_scale):
        import jax, jax.numpy as jnp
        import numpy as np
        D_MODEL = 128
        NUM_TILES = 64
        TPC = 8
        NUM_CLUSTERS = NUM_TILES // TPC
        GRID = 16
        COMP_H = 32
        NUM_KNOTS = 8
        EPS_LN = 1e-05

        def _calibrate(scores, knots, temperature):
            K = knots.shape[0]
            normalized = jax.nn.sigmoid(scores / (temperature[0] + 1e-06))
            idx_float = normalized * (K - 1)
            idx_low = jnp.clip(idx_float.astype(jnp.int32), 0, K - 2)
            idx_high = idx_low + 1
            t = idx_float - idx_low.astype(scores.dtype)
            val_low = knots[idx_low]
            val_high = knots[idx_high]
            return val_low + t * (val_high - val_low)

        def _forward(x, signatures_raw, knot_values, temperature, compress_w1, compress_b1, compress_w2, compress_b2, spline_w1, spline_b1, spline_w2, spline_b2, directions, norm_gamma, norm_beta, output_scale):
            B, T, D = x.shape
            xf = x.reshape(-1, D)
            q = jnp.where(signatures_raw > 0.3, 1.0, jnp.where(signatures_raw < -0.3, -1.0, 0.0)).astype(signatures_raw.dtype)
            sigs = signatures_raw + jax.lax.stop_gradient(q - signatures_raw)
            cluster_sigs = jnp.sign(sigs.reshape(NUM_CLUSTERS, TPC, D).mean(axis=1))
            cluster_scores = xf @ cluster_sigs.T
            cluster_gates = _calibrate(cluster_scores, knot_values, temperature)
            cluster_idx = jnp.argmax(cluster_gates, axis=-1)
            tile_scores = xf @ sigs.T
            tile_gates = _calibrate(tile_scores, knot_values, temperature)
            gates_by_cluster = tile_gates.reshape(-1, NUM_CLUSTERS, TPC)
            sel_gates = jnp.take_along_axis(gates_by_cluster, cluster_idx[:, None, None], axis=1)[:, 0, :]
            local_idx = jnp.argmax(sel_gates, axis=-1)
            tile_idx = cluster_idx * TPC + local_idx
            h = jax.nn.gelu(xf @ compress_w1 + compress_b1, approximate=False)
            comp = jnp.tanh(h @ compress_w2 + compress_b2)
            w1 = spline_w1[tile_idx]
            b1 = spline_b1[tile_idx]
            hh = jax.nn.relu(jnp.einsum('ni,nig->ng', comp, w1) + b1)
            w2 = spline_w2[tile_idx]
            b2 = spline_b2[tile_idx]
            mag = jnp.einsum('ng,ngo->no', hh, w2) + b2
            ffn_out = mag * directions[tile_idx] * output_scale[0]
            y = xf + ffn_out
            mu = y.mean(axis=-1, keepdims=True)
            var = ((y - mu) ** 2).mean(axis=-1, keepdims=True)
            y = (y - mu) / jnp.sqrt(var + EPS_LN) * norm_gamma + norm_beta
            return y.reshape(B, T, D)
        return _forward(x, signatures_raw, knot_values, temperature, compress_w1, compress_b1, compress_w2, compress_b2, spline_w1, spline_b1, spline_w2, spline_b2, directions, norm_gamma, norm_beta, output_scale)

    def _L1_attn_ref(x, W_q, W_k, W_v, W_o, gn_weight, gn_bias):
        import jax, jax.numpy as jnp
        import numpy as np
        D_MODEL = 128
        N_HEADS = 16
        D_HEAD = D_MODEL // N_HEADS
        B, T = (2, 256)
        EPS = 1e-05
        b, t, dm = x.shape
        h, dh = (N_HEADS, D_HEAD)
        gammas = 1.0 - 2.0 ** (-5.0 - jnp.arange(h, dtype=jnp.float32))
        q = (x @ W_q.T).reshape(b, t, h, dh)
        k = (x @ W_k.T).reshape(b, t, h, dh)
        v = (x @ W_v.T).reshape(b, t, h, dh)
        idx = jnp.arange(t)
        diff = idx[:, None] - idx[None, :]
        pow_ = jnp.maximum(diff, 0).astype(jnp.float32)
        decay = jnp.where(diff >= 0, gammas[:, None, None] ** pow_, 0.0)
        scale = jnp.sqrt(jnp.float32(dh))
        attn = jnp.einsum('bihd,bjhd->bhij', q, k) * decay[None] / scale
        y = jnp.einsum('bhij,bjhd->bihd', attn, v)
        mean = y.mean(axis=(1, 3), keepdims=True)
        var = y.var(axis=(1, 3), keepdims=True)
        yn = (y - mean) / jnp.sqrt(var + EPS)
        yn = yn.reshape(b, t, dm) * gn_weight + gn_bias
        return yn @ W_o.T

    def _L1_ffn_ref(inputs, gate_w, gate_b, w1, b1, w2, b2):
        import jax, jax.numpy as jnp
        import numpy as np
        NUM_EXPERTS = 8
        CAPACITY = 80
        D = inputs.shape[-1]
        tokens = inputs.reshape(-1, D)
        logits = tokens @ gate_w + gate_b
        probs = jax.nn.softmax(logits, axis=-1)
        expert_idx = jnp.argmax(probs, axis=-1)
        mask1 = jax.nn.one_hot(expert_idx, NUM_EXPERTS, dtype=jnp.float32)
        pos = jnp.sum(jnp.cumsum(mask1, axis=0) * mask1, axis=-1) - 1.0
        pos = pos.astype(jnp.int32)
        keep = (pos < CAPACITY).astype(jnp.float32)
        gate_prob = jnp.sum(probs * mask1, axis=-1)
        pos_oh = jax.nn.one_hot(pos, CAPACITY, dtype=jnp.float32)
        sec_mask = mask1[:, :, None] * pos_oh[:, None, :] * keep[:, None, None]
        combine_weights = sec_mask * gate_prob[:, None, None]
        dispatch = jnp.einsum('nec,nd->ecd', sec_mask, tokens)
        h = jax.nn.gelu(jnp.einsum('ecd,edf->ecf', dispatch, w1) + b1[:, None, :])
        expert_out = jnp.einsum('ecf,efd->ecd', h, w2) + b2[:, None, :]
        out = jnp.einsum('nec,ecd->nd', combine_weights, expert_out)
        return out.reshape(inputs.shape)
    x = L0_attn_x
    xn = _layernorm(x, axis=-1)
    s = _L0_attn_ref(xn)
    g = _silu(_L0_ffn_ref(xn, L0_ffn_signatures_raw, L0_ffn_knot_values, L0_ffn_temperature, L0_ffn_compress_w1, L0_ffn_compress_b1, L0_ffn_compress_w2, L0_ffn_compress_b2, L0_ffn_spline_w1, L0_ffn_spline_b1, L0_ffn_spline_w2, L0_ffn_spline_b2, L0_ffn_directions, L0_ffn_norm_gamma, L0_ffn_norm_beta, L0_ffn_output_scale))
    x = x + s * g
    xn = _layernorm(x, axis=-1)
    s = _L1_attn_ref(xn, L1_attn_W_q, L1_attn_W_k, L1_attn_W_v, L1_attn_W_o, L1_attn_gn_weight, L1_attn_gn_bias)
    g = _silu(_L1_ffn_ref(xn, L1_ffn_gate_w, L1_ffn_gate_b, L1_ffn_w1, L1_ffn_b1, L1_ffn_w2, L1_ffn_b2))
    x = x + s * g
    return x

_drawn_inputs = setup_inputs


def setup_inputs(seed=0):
    import zlib

    import numpy as np

    out = dict(_drawn_inputs(seed))
    spreads = {'L0_ffn_compress_b1': (0.0, 0.8),
     'L0_ffn_compress_b2': (0.0, 0.8),
     'L0_ffn_spline_b1': (0.0, 0.8),
     'L0_ffn_spline_b2': (0.0, 0.8),
     'L0_ffn_norm_gamma': (1.0, 0.6),
     'L0_ffn_norm_beta': (0.0, 0.8),
     'L1_attn_gn_weight': (1.0, 0.6),
     'L1_attn_gn_bias': (0.0, 0.8),
     'L1_ffn_gate_b': (0.0, 0.8),
     'L1_ffn_b1': (0.0, 0.8),
     'L1_ffn_b2': (0.0, 0.8)}
    factors = {'L0_ffn_signatures_raw': 8.0,
     'L0_ffn_knot_values': 8.0,
     'L0_ffn_compress_w1': 8.0,
     'L0_ffn_compress_w2': 8.0,
     'L0_ffn_spline_w1': 8.0,
     'L0_ffn_spline_w2': 8.0,
     'L0_ffn_directions': 8.0,
     'L1_attn_W_q': 8.0,
     'L1_attn_W_k': 8.0,
     'L1_attn_W_v': 8.0,
     'L1_attn_W_o': 8.0,
     'L1_ffn_gate_w': 8.0,
     'L1_ffn_w1': 8.0,
     'L1_ffn_w2': 8.0}
    for name, (base, spread) in spreads.items():
        noise = np.random.default_rng([zlib.crc32(name.encode()), seed]).standard_normal(out[name].shape)
        drawn = base * np.exp(spread * noise) if base else spread * noise
        out[name] = jnp.asarray(drawn.astype(out[name].dtype))
    for name, factor in factors.items():
        out[name] = (out[name] * factor).astype(out[name].dtype)
    return out
```

```python
from contextlib import ExitStack

import concourse.bass as bass
from concourse import mybir

F32 = mybir.dt.float32
BF16 = mybir.dt.bfloat16
U32 = mybir.dt.uint32
ALU = mybir.AluOpType
ACT = mybir.ActivationFunctionType
AX = mybir.AxisListType

P = 128
D = 128
NB, SEQ = 2, 1024
N = NB * SEQ
NT = N // P
TB = SEQ // P
QT = 4
NQ = NT // QT
QW = QT * P
EPS = 1e-5

NTILES, TPC = 64, 8
NCL = NTILES // TPC
NKNOT = 8
COMP, GRID = 32, 16
NSC = NTILES + NCL
TW1, TB1, TW2, TB2, TDIR = 0, 2 * GRID, 3 * GRID, 4 * GRID, 4 * GRID + 1
TABW = TDIR + D

H, DH = 16, 8
C = 32
CT, CQ, CB = P // C, QW // C, SEQ // C
NG, GH = 4, 4

NE, CAP, F = 8, 80, 512
FT = F // P
SLOTS = NE * CAP
NOWHERE = 2 * N

CONST_COLS = {}


def _layout():
    at = 0
    for name, width in (("ident", P), ("tri", P), ("ones", P), ("avg8", P), ("decay_s", NG * C),
                        ("mask_v", P), ("mask_kv", C), ("mask_k", GH), ("decay_k", P), ("decay_q", C),
                        ("gamma_c", 1), ("thr", NKNOT), ("rev", NE), ("slot0", NE), ("iota", SLOTS),
                        ("ids", NT * 2), ("neghalf", NT), ("oob", NE), ("reset", NE * NT), ("repeat", CT * P)):
        CONST_COLS[name] = (at, width)
        at += width
    return at


CONST_W = _layout()


def kernel_program(nc, L0_attn_x, L0_ffn_signatures_raw, L0_ffn_knot_values, L0_ffn_temperature,
                   L0_ffn_compress_w1, L0_ffn_compress_b1, L0_ffn_compress_w2, L0_ffn_compress_b2,
                   L0_ffn_spline_w1, L0_ffn_spline_b1, L0_ffn_spline_w2, L0_ffn_spline_b2,
                   L0_ffn_directions, L0_ffn_norm_gamma, L0_ffn_norm_beta, L0_ffn_output_scale,
                   L1_attn_W_q, L1_attn_W_k, L1_attn_W_v, L1_attn_W_o, L1_attn_gn_weight, L1_attn_gn_bias,
                   L1_ffn_gate_w, L1_ffn_gate_b, L1_ffn_w1, L1_ffn_b1, L1_ffn_w2, L1_ffn_b2, consts, out):
    rows_x2 = nc.dram_tensor("rows_x2", (N, 2 * D), F32, kind="Internal").ap()
    rows_s = nc.dram_tensor("rows_s", (N, D), F32, kind="Internal").ap()
    out_rows = out.rearrange("b t d -> (b t) d")

    with ExitStack() as ctx:
        def sb(name, shape, dt=F32):
            return ctx.enter_context(nc.sbuf_tensor(name, shape, dt))

        def sem(name):
            return ctx.enter_context(nc.semaphore(name))

        bank = [ctx.enter_context(nc.psum_tensor(f"bank{i}", [P, 512], F32)) for i in range(8)]
        bank_filled = [sem(f"bank{i}_filled") for i in range(8)]
        bank_emptied = [sem(f"bank{i}_emptied") for i in range(8)]

        cst = sb("cst", [P, CONST_W])

        def K(name, parts=P):
            at, w = CONST_COLS[name]
            return cst[0:parts, at:at + w]

        x = sb("x", [P, NT, D])
        xn = sb("xn", [P, NT, D + 1])
        prob = sb("prob", [P, NT, D])
        xnT = sb("xnT", [P, N])
        pT = sb("pT", [P, N])
        ebuf = sb("ebuf", [P, 2, TB, QW])
        stats = sb("stats", [P, NT, 6])
        mv = sb("mv", [P, NT, 2])
        veps = sb("veps", [P, NT])
        rstd = sb("rstd", [P, NT])
        sumexp = sb("sumexp", [P, NT])
        rsum = sb("rsum", [P, NT])
        lse = sb("lse", [P, NT])
        nlse = sb("nlse", [P, NT])
        negent = sb("negent", [P, NT])
        nexp = sb("nexp", [P, NT])
        s0 = sb("s0", [P, NT, D + 1])
        ratio = sb("ratio", [P, NT])
        sig = sb("sig", [NTILES, 3, D])
        sigT = sb("sigT", [P, NSC])
        clsum = sb("clsum", [P, 2 * NCL])
        sc = sb("sc", [P, NT, NSC])
        knots = sb("knots", [P, NKNOT])
        dknots = sb("dknots", [P, NKNOT])
        temp = sb("temp", [P, 2])
        cw1 = sb("cw1", [P, COMP])
        cb1 = sb("cb1", [COMP, 1])
        cw2 = sb("cw2", [COMP, 2])
        cb2 = sb("cb2", [P, 2])
        hT_room = sb("hT_room", [P, N])
        hT = hT_room[0:COMP, :]
        comp = sb("comp", [P, NT, 2])
        table = sb("table", [NTILES, TABW])
        gamma = sb("gamma", [P, D])
        beta = sb("beta", [P, D])
        oscale = sb("oscale", [P, 1])
        picked_room = sb("picked_room", [P, NT * SLOTS // 2])
        picked = picked_room[:, 0:NT * TABW].rearrange("p (t w) -> p t w", t=NT)
        oneT_room = sb("oneT_room", [P, N])
        oneT = oneT_room[0:NTILES, :]
        cal_b = oneT_room[:, 0:NT * 8 * 7].rearrange("p (t a b) -> p t a b", t=NT, a=8)
        onehot = sb("onehot", [P, NT, NTILES])
        sel8 = sb("sel8", [P, NT, 8])
        gate8 = sb("gate8", [P, NT, 8])
        ohc = sb("ohc", [P, NT, 8])
        ohl = sb("ohl", [P, NT, 8])
        cal_a = sb("cal_a", [P, NT, 8, 8])
        small = sb("small", [P, 6, NT * 8])
        row16 = sb("row16", [P, 4, NT])
        spl = sb("spl", [P, 2, NT, GRID])
        y = sb("y", [P, NT, D])
        xn2 = sb("xn2", [P, NT, D])
        wT = sb("wT", [P, 4, P])
        wraw = xn2[:, 0:4, :]
        gnw = sb("gnw", [P, 2])
        gate_w = sb("gate_w", [P, NE])
        gate_b = sb("gate_b", [P, NE])
        b1raw = sb("b1raw", [NE * FT, P])
        b1T = sb("b1T", [P, NE * FT])
        b2r = sb("b2r", [CAP, NE, D])
        slotv = sb("slotv", [P, NT])
        info = sb("info", [P, NT, 6], BF16)
        gpt = sb("gpt", [P, 3, NT])
        idx_f = sb("idx_f", [CAP, NE, 6])
        idx_t = sb("idx_t", [CAP, 3, NE])
        idx_load = sb("idx_load", [CAP, NE], U32)
        idx_store = sb("idx_store", [CAP, NE], U32)
        gprob = sb("gprob", [CAP, NE])
        gns = sb("gns", [P, NB, 16])
        gnst = sb("gnst", [P, NQ, 6])

        xn2T = xnT
        w1 = sb("w1", [P, NE, F])
        w2 = sb("w2", [P, NE, FT, D])
        kexp = pT[:, :].rearrange("p (c a) -> p c a", c=CQ)
        vexp = hT_room[:, :].rearrange("p (c a) -> p c a", c=CQ)
        smask = ebuf[:, 0].rearrange("p a b -> p (a b)")[:, 0:NG * QW].rearrange("p (g w) -> p g w", g=NG)
        xg = ebuf[:, 1].rearrange("p a b -> p (a b)")[0:CAP, 0:NE * 2 * D].rearrange("p (e d) -> p e d", e=NE)
        xgT = ebuf[:, 1].rearrange("p a b -> p (a b)")[:, NE * 2 * D:NE * 2 * D + SLOTS].rearrange("p (e c) -> p e c", e=NE)
        sg = ebuf[:, 1].rearrange("p a b -> p (a b)")[0:CAP, 2688:2688 + NE * D].rearrange("p (e d) -> p e d", e=NE)
        q_plain = cal_a[:, :, :, :].rearrange("p a b c -> p (a b c)")[:, 0:QW]
        q_dec = cal_a[:, :, :, :].rearrange("p a b c -> p (a b c)")[:, QW:2 * QW]
        kd = y[:, 0:TB, :]
        vtok = y[:, TB:NT, :]
        kvm = prob[:, 0:TB, :].rearrange("p a b -> p (a b)").rearrange("p (e c) -> p e c", e=C)
        state = prob[:, TB:NT, :].rearrange("p a b -> p (a b)").rearrange("p (e c) -> p e c", e=C)
        dtab = s0[:, :, :].rearrange("p a b -> p (a b)")[:, 0:C * CB]
        yT = oneT_room
        s2 = s0[:, :, :].rearrange("p a b -> p (a b)")[:, C * CB:C * CB + 2 * QW].rearrange("p (h a d) -> p h a d", h=2, a=QT)
        slot_mask = picked_room[:, :].bitcast(BF16).rearrange("p (t s) -> p t s", t=NT)
        hb = xn[:, :, :].rearrange("p a b -> p (a b)")[:, 0:2 * FT * CAP * 2].rearrange("p (n f c) -> p n f c", n=4, f=FT)
        eo = sc[:, :, :].rearrange("p a b -> p (a b)")[0:CAP, 0:NE * D].rearrange("p (e d) -> p e d", e=NE)

        ident_in = sem("ident_in")
        consts_in = sem("consts_in")
        x_in = [sem(f"x_in{q}") for q in range(NQ)]
        sig_in = sem("sig_in")
        ffn_in = sem("ffn_in")
        w_in = sem("w_in")
        moe_in = sem("moe_in")
        dve_step = sem("dve_step")
        pool_step = sem("pool_step")
        var_ready = sem("var_ready")
        rstd_ready = sem("rstd_ready")
        xn_ready = sem("xn_ready")
        exp_ready = sem("exp_ready")
        sum_ready = sem("sum_ready")
        lse_ready = sem("lse_ready")
        p_ready = sem("p_ready")
        negent_ready = sem("negent_ready")
        nexp_ready = sem("nexp_ready")
        sig_ready = sem("sig_ready")
        sigT_ready = sem("sigT_ready")
        comp_ready = sem("comp_ready")
        cal_in = sem("cal_in")
        cal_exp = sem("cal_exp")
        onehot_ready = sem("onehot_ready")
        yhat_ready = sem("yhat_ready")
        yaff_ready = sem("yaff_ready")
        silu_ready = sem("silu_ready")
        x2_ready = sem("x2_ready")
        xn2_ready = sem("xn2_ready")
        rows_stored = sem("rows_stored")
        base_stored = sem("base_stored")
        lg_ready = sem("lg_ready")
        lgexp_ready = sem("lgexp_ready")
        exp_mask_ready = sem("exp_mask_ready")
        slotmask_ready = sem("slotmask_ready")
        info_ready = sem("info_ready")
        idx_ready = sem("idx_ready")
        xg_in = sem("xg_in")
        state_ready = sem("state_ready")
        gn_mean = sem("gn_mean")
        gn_dev = sem("gn_dev")
        yn_ready = sem("yn_ready")
        s2_stored = [sem(f"s2_stored{q}") for q in range(NQ)]
        sg_in = sem("sg_in")
        h_ready = sem("h_ready")
        h_used = sem("h_used")
        eo_ready = sem("eo_ready")
        silu2_ready = sem("silu2_ready")
        fin_ready = sem("fin_ready")
        out_stored = sem("out_stored")

        quarters = range(NQ)
        turns = {
            0: [f"xnT{q}" for q in quarters] + ["sigT"] + [f"oneT{q}" for q in quarters]
               + [f"xn2T{q}" for q in quarters] + ["b1T"]
               + [f"vrep{q}.{i}" for q in quarters for i in (0, 2)] + ["xgT0", "h0", "h4"],
            1: [f"pT{q}" for q in quarters] + ["wT"] + [f"pick{i}" for i in range(0, NT // 2, 2)]
               + ["ktok0", "ktok1", "KT0", "QT0", "KT1", "QT1", "ktok2", "ktok3", "KT2", "QT2", "KT3", "QT3"]
               + ["xgT1", "h1", "h5"],
            6: [f"sc{q}" for q in quarters] + ["comp", "lg", "cum"]
               + [f"vrep{q}.{i}" for q in (0, 1) for i in (1, 3)] + ["idx"]
               + [f"vrep{q}.{i}" for q in (2, 3) for i in (1, 3)] + ["s2_0", "s2_2"],
            7: [f"h0_{q}" for q in quarters] + [f"pick{i}" for i in range(1, NT // 2, 2)] + ["tot"]
               + ["vtok0", "vtok1", "y0", "y1", "vtok2", "vtok3", "y2", "y3", "s2_1", "s2_3"],
        }
        last = {2: ["h2", "h6"], 3: ["h3", "h7"], 4: ["gn0", "gn1", "eo0"], 5: ["gd0", "gd1", "eo1"]}
        for i in range(NG):
            if i < 2:
                head = [f"S{b}.{h}.{j}" for b in range(NB) for h in range(2) for j in range(i, TB, 2)]
            else:
                head = [f"A{t}" for t in range(i - 2, NT, 2)]
            turns[2 + i] = head + [f"KV0.{i}", f"R0.{i}", f"R1.{i}", f"KV1.{i}", f"R2.{i}", f"R3.{i}"] + last[2 + i]
        turn = {name: (b, n) for b, names in turns.items() for n, name in enumerate(names)}
        in_order = {b: list(names) for b, names in turns.items()}

        def psum(name):
            return bank[turn[name][0]]

        def free(pe, name):
            b, n = turn[name]
            assert in_order[b].pop(0) == name, name
            if n:
                pe.wait_ge(bank_emptied[b], n)
            return bank[b]

        def filled(eng, name):
            b, n = turn[name]
            eng.wait_ge(bank_filled[b], n + 1)
            return bank[b]

        def moved(eng, name):
            b, n = turn[name]
            eng.wait_ge(bank_emptied[b], n + 1)

        block = ctx.enter_context(nc.Block())

        def bc(ap, shape):
            return ap.to_broadcast(shape)

        @block.sync
        def _(sp):
            i0, iw = CONST_COLS["ident"]
            sp.dma_start(cst[:, i0:i0 + iw], consts[:, i0:i0 + iw]).then_inc(ident_in, 16)
            xr = L0_attn_x.rearrange("b (t p) d -> p (b t) d", p=P)
            for q in range(NQ):
                sp.dma_start(x[:, QT * q:QT * q + QT, :], xr[:, QT * q:QT * q + QT, :]).then_inc(x_in[q], 16)
            sp.dma_start(cst[:, iw:], consts[:, iw:]).then_inc(consts_in, 16)
            for j, w in enumerate((L1_attn_W_q, L1_attn_W_k, L1_attn_W_v, L1_attn_W_o)):
                sp.dma_start(wraw[:, j, :], w).then_inc(w_in, 16)
            sp.dma_start(gnw[:, 0:1], L1_attn_gn_weight.unsqueeze(1)).then_inc(w_in, 16)
            sp.dma_start(gnw[:, 1:2], L1_attn_gn_bias.unsqueeze(1)).then_inc(w_in, 16)
            sp.dma_start(gate_w[:, :], L1_ffn_gate_w).then_inc(w_in, 16)
            sp.dma_start(gate_b[:, :], L1_ffn_gate_b.partition_broadcast(P)).then_inc(w_in, 16)
            sp.dma_start(b1raw[:, :], L1_ffn_b1.rearrange("e (f p) -> (e f) p", p=P)).then_inc(w_in, 16)
            sp.dma_start(b2r[:, :, :], L1_ffn_b2.partition_broadcast(CAP)).then_inc(moe_in, 16)
            sp.dma_start(w1[:, :, :], L1_ffn_w1.rearrange("e d f -> d e f")).then_inc(moe_in, 16)
            sp.dma_start(w2[:, :, :, :], L1_ffn_w2.rearrange("e (f p) d -> p e f d", p=P)).then_inc(moe_in, 16)
            rows = rows_x2.rearrange("(t p) w -> p t w", p=P)
            outr = out_rows.rearrange("(t p) d -> p t d", p=P)
            for b in range(NB):
                ts = slice(TB * b, TB * b + TB)
                sp.wait_ge(x2_ready, b + 1)
                sp.dma_start(rows[:, ts, 0:D], x[:, ts, :]).then_inc(rows_stored, 16)
                sp.dma_start(outr[:, ts, :], x[:, ts, :]).then_inc(base_stored, 16)
                sp.wait_ge(xn2_ready, b + 1)
                sp.dma_start(rows[:, ts, D:2 * D], xn2[:, ts, :]).then_inc(rows_stored, 16)
            srow = rows_s.rearrange("(t p) d -> p t d", p=P)
            for q in range(NQ):
                moved(sp, f"s2_{q}")
                sp.dma_start(srow[:, QT * q:QT * q + QT, :], s2[:, q % 2]).then_inc(s2_stored[q], 16)

        @block.gpsimd
        def _(pool):
            n_step = [0]

            def link(ins):
                n_step[0] += 1
                ins.then_inc(pool_step, 1)
                pool.wait_ge(pool_step, n_step[0])

            uses = [0]

            def inv_sqrt(out_ap, var_ap, n, parts=P):
                uses[0] += 1
                pool.wait_ge(var_ready, uses[0])
                link(pool.tensor_scalar(veps[0:parts, 0:n], var_ap, EPS, None, ALU.add))
                pool.tensor_tensor(out_ap, veps[0:parts, 0:n], K("neghalf")[0:parts, 0:n], ALU.pow).then_inc(rstd_ready, 1)
                pool.wait_ge(rstd_ready, uses[0])

            pool.memset(xn[:, :, D:D + 1], 1.0).then_inc(xn_ready, 1)
            pool.wait_ge(consts_in, 16)
            for q in range(NQ):
                ts = slice(QT * q, QT * q + QT)
                inv_sqrt(rstd[:, ts], mv[:, ts, 1], QT)
            for b in range(NB):
                ts = slice(TB * b, TB * b + TB)
                inv_sqrt(rstd[:, ts], mv[:, ts, 1], TB)
                pool.wait_ge(yhat_ready, b + 1)
                link(pool.tensor_tensor(y[:, ts, :], y[:, ts, :], bc(gamma[:, :].unsqueeze(1), [P, TB, D]), ALU.mult))
                pool.tensor_tensor(y[:, ts, :], y[:, ts, :], bc(beta[:, :].unsqueeze(1), [P, TB, D]), ALU.add)\
                    .then_inc(yaff_ready, 1)
            for b in range(NB):
                ts = slice(TB * b, TB * b + TB)
                inv_sqrt(rstd[:, ts], mv[:, ts, 1], TB)
            pool.wait_ge(idx_ready, 1)
            pool.wait_ge(rows_stored, 16 * 2 * NB)
            for e in range(NE):
                pool.indirect_dma_start(xg[:, e, :], None, rows_x2, bass.IndirectOffsetOnAxis(ap=idx_load[:, e:e + 1], axis=0))\
                    .then_inc(xg_in, 16)
            for b in range(NB):
                inv_sqrt(gns[:, b, 6:7], gns[:, b, 5:6], 1)
            for q in range(NQ):
                pool.wait_ge(s2_stored[q], 16)
            for e in range(NE):
                pool.indirect_dma_start(sg[:, e, :], None, rows_s, bass.IndirectOffsetOnAxis(ap=idx_load[:, e:e + 1], axis=0))\
                    .then_inc(sg_in, 16)
            pool.wait_ge(base_stored, 16 * NB)
            for h in range(2):
                pool.wait_ge(fin_ready, h + 1)
                for e in range(4 * h, 4 * h + 4):
                    pool.indirect_dma_start(out_rows, bass.IndirectOffsetOnAxis(ap=idx_store[:, e:e + 1], axis=0),
                                            eo[:, e, :], None, bounds_check=N - 1, oob_is_err=False).then_inc(out_stored, 16)
            pool.wait_ge(out_stored, 16 * NE)

        @block.scalar
        def _(act):
            act.dma_start(sig[:, 0, :], L0_ffn_signatures_raw).then_inc(sig_in, 16)
            for dst, src in ((cw1[:, :], L0_ffn_compress_w1), (cb1[:, :], L0_ffn_compress_b1.unsqueeze(1)),
                             (cw2[:, :], L0_ffn_compress_w2), (cb2[:, :], L0_ffn_compress_b2.partition_broadcast(P)),
                             (knots[:, :], L0_ffn_knot_values.partition_broadcast(P)),
                             (temp[:, 0:1], L0_ffn_temperature.partition_broadcast(P)),
                             (oscale[:, :], L0_ffn_output_scale.partition_broadcast(P)),
                             (gamma[:, :], L0_ffn_norm_gamma.partition_broadcast(P)),
                             (beta[:, :], L0_ffn_norm_beta.partition_broadcast(P)),
                             (table[:, TW1:TB1], L0_ffn_spline_w1.rearrange("t i g -> t (i g)")),
                             (table[:, TB1:TW2], L0_ffn_spline_b1),
                             (table[:, TW2:TB2], L0_ffn_spline_w2.rearrange("t g o -> t (g o)")),
                             (table[:, TB2:TDIR], L0_ffn_spline_b2),
                             (table[:, TDIR:TABW], L0_ffn_directions)):
                act.dma_start(dst, src).then_inc(ffn_in, 16)
            act.preload_act_table(ACT.Ln)
            for q in range(NQ):
                ts = slice(QT * q, QT * q + QT)
                act.wait_ge(xn_ready, q + 2)
                act.activation(prob[:, ts, :], xn[:, ts, 0:D], ACT.Exp).then_inc(exp_ready, 1)
                filled(act, f"xnT{q}")
                act.activation(xnT[:, QW * q:QW * q + QW], psum(f"xnT{q}")[:, :], ACT.Copy).then_inc(bank_emptied[0], 1)
                act.wait_ge(sum_ready, q + 1)
                act.activation(lse[:, ts], sumexp[:, ts], ACT.Ln).then_inc(lse_ready, 1)
            act.wait_ge(negent_ready, NQ)
            act.activation(nexp[:, :], negent[:, :], ACT.Exp, scale=-1.0).then_inc(nexp_ready, 1)
            filled(act, "sigT")
            act.activation(sigT[:, 0:NTILES], psum("sigT")[:, 0:NTILES], ACT.Copy).then_inc(bank_emptied[0], 1)
            filled(act, "wT")
            act.activation(wT[:, :, :].rearrange("p a b -> p (a b)"), psum("wT")[:, :], ACT.Copy).then_inc(bank_emptied[1], 1)
            act.wait_ge(ffn_in, 16 * 14)
            for q in range(NQ):
                filled(act, f"h0_{q}")
                act.activation(hT[:, QW * q:QW * q + QW], psum(f"h0_{q}")[0:COMP, :], ACT.Gelu, bias=cb1[:, 0:1])\
                    .then_inc(bank_emptied[7], 1)
            moved(act, "comp")
            cflat = comp[:, :, :].rearrange("p a b -> p (a b)")
            act.activation(cflat, cflat, ACT.Tanh).then_inc(comp_ready, 1)

            def calibrate_exp(n):
                act.wait_ge(cal_in, n + 1)
                act.activation(small[:, 0, :], sel8[:, :, :].rearrange("p a b -> p (a b)"), ACT.Exp,
                               scale=temp[:, 1:2]).then_inc(cal_exp, 1)

            calibrate_exp(0)

            def attention_exps(b, h):
                half = 2 * b + h
                if half >= 2:
                    filled(act, f"A{QT * (half - 1) - 1}")
                for j in range(TB):
                    filled(act, f"S{b}.{h}.{j}")
                    act.activation(ebuf[:, half % 2, j, :], psum(f"S{b}.{h}.{j}")[:, :], ACT.Exp,
                                   bias=nlse[:, TB * b + j:TB * b + j + 1]).then_inc(bank_emptied[2 + j % 2], 1)
                    if half == 0 and j == 5:
                        calibrate_exp(1)

            def attention_copy(h):
                for i in range(QT):
                    t = QT * h + i
                    filled(act, f"A{t}")
                    act.activation(s0[:, t, :], psum(f"A{t}")[:, 0:D + 1], ACT.Copy).then_inc(bank_emptied[4 + t % 2], 1)

            act.wait_ge(p_ready, NQ)
            attention_exps(0, 0)
            attention_exps(0, 1)
            attention_copy(0)
            for i in range(8):
                filled(act, f"pick{i}")
                act.activation(picked[:, 2 * i:2 * i + 2, :], psum(f"pick{i}")[:, 0:2 * TABW].rearrange("p (a b) -> p a b", a=2),
                               ACT.Copy).then_inc(bank_emptied[turn[f"pick{i}"][0]], 1)
            attention_copy(1)
            attention_exps(1, 0)
            attention_exps(1, 1)
            attention_copy(2)
            attention_copy(3)
            for b in range(NB):
                act.wait_ge(yaff_ready, b + 1)
                ts = slice(TB * b, TB * b + TB)
                act.activation(y[:, ts, :], y[:, ts, :], ACT.Silu).then_inc(silu_ready, 1)
            for q in range(NQ):
                filled(act, f"xn2T{q}")
                act.activation(xn2T[:, QW * q:QW * q + QW], psum(f"xn2T{q}")[:, :], ACT.Copy).then_inc(bank_emptied[0], 1)
            filled(act, "b1T")
            act.activation(b1T[:, :], psum("b1T")[:, 0:NE * FT], ACT.Copy).then_inc(bank_emptied[0], 1)
            act.wait_ge(lg_ready, 1)
            act.activation(small[:, 1, :], small[:, 0, :], ACT.Exp).then_inc(lgexp_ready, 1)

            def output_copy(q):
                filled(act, f"y{q}")
                act.activation(yT[:, QW * q:QW * q + QW], psum(f"y{q}")[:, :], ACT.Copy).then_inc(bank_emptied[7], 1)

            for b in range(NB):
                for k in range(2):
                    q = 2 * b + k
                    filled(act, f"vtok{q}")
                    act.activation(vtok[:, QT * k:QT * k + QT, :], psum(f"vtok{q}")[:, :].rearrange("p (a b) -> p a b", a=QT),
                                   ACT.Copy).then_inc(bank_emptied[7], 1)
                for k in range(2):
                    q = 2 * b + k
                    filled(act, f"KT{q}")
                    if q:
                        filled(act, f"R{q - 1}.{NG - 1}")
                    for m in range(GH):
                        ins = act.activation(kexp[:, :, C * m:C * m + C], psum(f"KT{q}")[:, :].rearrange("p (c j) -> p c j", c=CQ),
                                             ACT.Copy, scale=K("mask_k")[:, m:m + 1])
                    ins.then_inc(bank_emptied[1], 1)
                    if k:
                        output_copy(q - 1)
                output_copy(q)
            def hidden_gelu(e):
                moved(act, f"h{e}")
                hv = hb[:, e % 4].rearrange("p f c -> p (f c)")
                act.activation(hv, hv, ACT.Gelu_apprx_tanh).then_inc(h_ready, 1)

            for e in range(4):
                hidden_gelu(e)
            for q in range(NQ):
                filled(act, f"s2_{q}")
                if q >= 2:
                    act.wait_ge(s2_stored[q - 2], 16)
                act.activation(s2[:, q % 2].rearrange("p a b -> p (a b)"), psum(f"s2_{q}")[:, :], ACT.Copy)\
                    .then_inc(bank_emptied[6 + q % 2], 1)
            for e in range(4, NE):
                hidden_gelu(e)
            for h in range(2):
                act.wait_ge(eo_ready, h + 1)
                ev = eo[:, 4 * h:4 * h + 4, :].rearrange("p e d -> p (e d)")
                act.activation(ev, ev, ACT.Silu).then_inc(silu2_ready, 1)

        @block.tensor
        def _(pe):
            idt = K("ident")
            pe.wait_ge(ident_in, 16)

            def done(ins, name):
                ins.then_inc(bank_filled[turn[name][0]], 1)

            def transposes(name, srcs, rows=P):
                out_bank = free(pe, name)
                for i, src in enumerate(srcs):
                    ins = pe.transpose(out_bank[0:src.shape[1], P * i:P * i + src.shape[0]], src, idt[0:src.shape[0], 0:src.shape[0]])
                done(ins, name)

            for q in range(NQ):
                pe.wait_ge(xn_ready, q + 2)
                transposes(f"xnT{q}", [xn[:, QT * q + i, 0:D] for i in range(QT)])
                pe.wait_ge(p_ready, q + 1)
                transposes(f"pT{q}", [prob[:, QT * q + i, :] for i in range(QT)])
            pe.wait_ge(sig_ready, 1)
            transposes("sigT", [sig[:, 2, :]])
            pe.wait_ge(w_in, 16 * 9)
            transposes("wT", [wraw[:, j, :] for j in range(4)])
            pe.wait_ge(ffn_in, 16 * 14)
            pe.wait_ge(sigT_ready, 1)
            for q in range(NQ):
                moved(pe, f"xnT{q}")
                ob = free(pe, f"h0_{q}")
                done(pe.matmul(ob[0:COMP, :], cw1[:, :], xnT[:, QW * q:QW * q + QW], start=True, stop=True), f"h0_{q}")
                ob = free(pe, f"sc{q}")
                for i in range(QT):
                    t = QT * q + i
                    ins = pe.matmul(ob[:, P * i:P * i + NSC], xnT[:, P * t:P * t + P], sigT[:, :], start=True, stop=True)
                done(ins, f"sc{q}")
            ob = free(pe, "comp")
            for t in range(NT):
                if t % QT == 0:
                    moved(pe, f"h0_{t // QT}")
                ins = pe.matmul(ob[:, 2 * t:2 * t + 2], hT[:, P * t:P * t + P], cw2[:, :], start=True, stop=True)
            done(ins, "comp")

            moved(pe, f"pT{NQ - 1}")

            def scores(b, h):
                for j in range(TB):
                    name = f"S{b}.{h}.{j}"
                    ob = free(pe, name)
                    t = TB * b + j
                    done(pe.matmul(ob[:, :], xnT[:, P * t:P * t + P], pT[:, SEQ * b + QW * h:SEQ * b + QW * h + QW],
                                   start=True, stop=True), name)

            def values(b, h):
                half = 2 * b + h
                for i in range(QT):
                    t = QT * half + i
                    ob = free(pe, f"A{t}")
                    for j in range(TB):
                        if i == 0:
                            moved(pe, f"S{b}.{h}.{j}")
                        ins = pe.matmul(ob[:, 0:D + 1], ebuf[:, half % 2, j, P * i:P * i + P], xn[:, TB * b + j, :],
                                        start=(j == 0), stop=(j == TB - 1))
                    done(ins, f"A{t}")

            def pick_rows():
                for q in range(NQ):
                    pe.wait_ge(onehot_ready, 1)
                    transposes(f"oneT{q}", [onehot[:, QT * q + i, :] for i in range(QT)])
                for i in range(NT // 2):
                    name = f"pick{i}"
                    ob = free(pe, name)
                    moved(pe, f"oneT{2 * i // QT}")
                    for k in range(2):
                        t = 2 * i + k
                        ins = pe.matmul(ob[:, TABW * k:TABW * k + TABW], oneT[:, P * t:P * t + P], table[:, :], start=True, stop=True)
                    done(ins, name)

            scores(0, 0)
            scores(0, 1)
            values(0, 0)
            pick_rows()
            values(0, 1)
            scores(1, 0)
            scores(1, 1)
            values(1, 0)
            values(1, 1)

            for q in range(NQ):
                pe.wait_ge(xn2_ready, q // 2 + 1)
                transposes(f"xn2T{q}", [xn2[:, QT * q + i, :] for i in range(QT)])
            transposes("b1T", [b1raw[:, :]])
            ob = free(pe, "lg")
            for t in range(NT):
                if t % QT == 0:
                    moved(pe, f"xn2T{t // QT}")
                ins = pe.matmul(ob[:, NE * t:NE * t + NE], xn2T[:, P * t:P * t + P], gate_w[:, :], start=True, stop=True)
            done(ins, "lg")

            def key_value_states(b):
                for name, w in (("ktok", 1), ("vtok", 2)):
                    for k in range(2):
                        q = 2 * b + k
                        ob = free(pe, f"{name}{q}")
                        for i in range(QT):
                            t = QT * q + i
                            ins = pe.matmul(ob[:, P * i:P * i + P], xn2T[:, P * t:P * t + P], wT[:, w, :], start=True, stop=True)
                        done(ins, f"{name}{q}")
                moved(pe, f"ktok{2 * b + 1}")
                moved(pe, f"vtok{2 * b + 1}")
                for c in range(CT):
                    ob = free(pe, f"KV{b}.{c}")
                    rows = slice(C * c, C * c + C)
                    for t in range(TB):
                        for g in range(NG):
                            cols = slice(C * g, C * g + C)
                            ins = pe.matmul(ob[cols, C * t:C * t + C], kd[rows, t, cols], vtok[rows, t, cols],
                                            start=True, stop=True, tile_position=(C * c, C * g))
                    done(ins, f"KV{b}.{c}")

            def chunk_inputs(q):
                for name, w in (("KT", 1), ("QT", 0)):
                    ob = free(pe, f"{name}{q}")
                    done(pe.matmul(ob[:, :], wT[:, w, :], xn2T[:, QW * q:QW * q + QW], start=True, stop=True), f"{name}{q}")
                for i in range(QT):
                    ob = free(pe, f"vrep{q}.{i}")
                    for c in range(CT):
                        ins = pe.matmul(ob[:, P * c:P * c + P], K("repeat")[:, P * c:P * c + P],
                                        vtok[:, QT * (q % 2) + i, :], start=True, stop=True)
                    done(ins, f"vrep{q}.{i}")

            def chunk_scores(q):
                moved(pe, f"KT{q}")
                moved(pe, f"QT{q}")
                for g in range(NG):
                    rows = slice(C * g, C * g + C)
                    ob = free(pe, f"R{q}.{g}")
                    for c in range(CQ):
                        ins = pe.matmul(ob[:, C * c:C * c + C], kexp[rows, c, :], q_plain[rows, C * c:C * c + C], start=True, stop=True)
                    done(ins, f"R{q}.{g}")

            def chunk_outputs(q):
                b = q // 2
                moved(pe, f"vrep{q}.2")
                moved(pe, f"vrep{q}.3")
                pe.wait_ge(state_ready, b + 1)
                ob = free(pe, f"y{q}")
                for g in range(NG):
                    moved(pe, f"R{q}.{g}")
                    rows = slice(C * g, C * g + C)
                    for c in range(CQ):
                        cb = CQ * (q % 2) + c
                        cols = slice(C * c, C * c + C)
                        ins = pe.matmul(ob[rows, cols], vexp[:, c, rows], smask[:, g, cols], start=True, stop=(cb == 0))
                        if cb:
                            ins = pe.matmul(ob[rows, cols], state[rows, :, cb - 1], q_dec[rows, cols], start=False, stop=True,
                                            tile_position=(C * g, C * g))
                done(ins, f"y{q}")

            def count_experts():
                pe.wait_ge(exp_mask_ready, 1)
                m8 = ohc[:, :, :].rearrange("p a b -> p (a b)")
                ob = free(pe, "cum")
                done(pe.matmul(ob[:, 0:NT * NE], K("tri"), m8, start=True, stop=True), "cum")
                ob = free(pe, "tot")
                done(pe.matmul(ob[:, 0:NT * NE], K("ones"), m8, start=True, stop=True), "tot")

            def slot_tokens():
                pe.wait_ge(slotmask_ready, NT)
                pe.wait_ge(info_ready, 1)
                ob = free(pe, "idx")
                for e in range(NE):
                    for t in range(NT):
                        ins = pe.matmul(ob[0:CAP, 8 * e:8 * e + 6], slot_mask[:, t, CAP * e:CAP * e + CAP], info[:, t, :],
                                        start=(t == 0), stop=(t == NT - 1))
                done(ins, "idx")

            count_experts()
            key_value_states(0)
            chunk_inputs(0)
            chunk_scores(0)
            chunk_outputs(0)
            chunk_inputs(1)
            chunk_scores(1)
            chunk_outputs(1)
            slot_tokens()
            key_value_states(1)
            for q in (2, 3):
                chunk_inputs(q)
                chunk_scores(q)
                chunk_outputs(q)

            def norm_sums(name, srcs, b):
                ob = free(pe, name)
                done(pe.matmul(ob[:, 0:srcs.shape[1]], K("avg8"), srcs, start=True, stop=True), name)

            for b in range(NB):
                pe.wait_ge(gn_mean, b + 1)
                norm_sums(f"gn{b}", gns[:, b, 0:2], b)
                pe.wait_ge(gn_dev, b + 1)
                norm_sums(f"gd{b}", gns[:, b, 4:5], b)

            pe.wait_ge(xg_in, 16 * NE)
            for h in range(2):
                ob = free(pe, f"xgT{h}")
                for k in range(4):
                    ins = pe.transpose(ob[:, CAP * k:CAP * k + CAP], xg[:, 4 * h + k, D:2 * D], idt[0:CAP, 0:CAP])
                done(ins, f"xgT{h}")
            pe.wait_ge(moe_in, 16 * 3)

            def expert_hidden(e):
                ob = free(pe, f"h{e}")
                moved(pe, f"xgT{e // 4}")
                for f in range(FT):
                    ins = pe.matmul(ob[:, CAP * f:CAP * f + CAP], w1[:, e, P * f:P * f + P], xgT[:, e, :], start=True, stop=True)
                done(ins, f"h{e}")

            def expert_out(e):
                name = f"eo{e // 4}"
                ob = free(pe, name) if e % 4 == 0 else psum(name)
                pe.wait_ge(h_ready, e + 1)
                for f in range(FT):
                    ins = pe.matmul(ob[0:CAP, D * (e % 4):D * (e % 4) + D], hb[:, e % 4, f, :], w2[:, e, f, :],
                                    start=(f == 0), stop=(f == FT - 1))
                if e % 4 == 3:
                    done(ins, name)
                else:
                    ins.then_inc(h_used, 1)

            for e in range(4):
                expert_hidden(e)
            for q in quarters:
                pe.wait_ge(yn_ready, q // 2 + 1)
                ob = free(pe, f"s2_{q}")
                for i in range(QT):
                    t = QT * q + i
                    ins = pe.matmul(ob[:, P * i:P * i + P], yT[:, P * t:P * t + P], wT[:, 3, :], start=True, stop=True)
                done(ins, f"s2_{q}")
            for e in range(NE):
                expert_out(e)
                if e + 4 < NE:
                    expert_hidden(e + 4)
            assert not any(in_order.values())

        @block.vector
        def _(dve):
            n_step = [0]

            def link(ins):
                n_step[0] += 1
                ins.then_inc(dve_step, 1)
                dve.wait_ge(dve_step, n_step[0])

            n_var = [0]

            def variances(ins):
                n_var[0] += 1
                ins.then_inc(var_ready, 1)
                return n_var[0]

            def tile_stats(src, ts):
                for t in ts:
                    ins = dve.bn_stats(stats[:, t, :], src[:, t, 0:D])
                link(ins)
                for t in ts:
                    ins = dve.bn_aggr(mv[:, t, :], stats[:, t, :])
                return variances(ins)

            dve.wait_ge(sig_in, 16)
            raw = sig[:, 0, :]
            dve.tensor_scalar(sig[:, 1, :], raw, 0.3, None, ALU.is_gt)
            link(dve.tensor_scalar(sig[:, 2, :], raw, -0.3, None, ALU.is_lt))
            link(dve.tensor_tensor(sig[:, 1, :], sig[:, 1, :], sig[:, 2, :], ALU.subtract))
            link(dve.tensor_tensor(sig[:, 1, :], sig[:, 1, :], raw, ALU.subtract))
            dve.tensor_tensor(sig[:, 2, :], sig[:, 1, :], raw, ALU.add).then_inc(sig_ready, 1)

            for q in quarters:
                dve.wait_ge(x_in[q], 16)
                tile_stats(x, range(QT * q, QT * q + QT))
            for q in quarters:
                dve.wait_ge(rstd_ready, q + 1)
                for t in range(QT * q, QT * q + QT):
                    ins = dve.tensor_scalar(xn[:, t, 0:D], x[:, t, :], mv[:, t, 0:1], rstd[:, t:t + 1], ALU.subtract, ALU.mult)
                ins.then_inc(xn_ready, 1)
            for q in quarters:
                ts = slice(QT * q, QT * q + QT)
                dve.wait_ge(exp_ready, q + 1)
                dve.tensor_reduce(sumexp[:, ts], prob[:, ts, :], AX.X, ALU.add).then_inc(sum_ready, 1)
                dve.wait_ge(sum_ready, q + 1)
                link(dve.reciprocal(rsum[:, ts], sumexp[:, ts]))
                link(dve.tensor_tensor(prob[:, ts, :], prob[:, ts, :], bc(rsum[:, ts].unsqueeze(2), [P, QT, D]), ALU.mult))
                dve.wait_ge(lse_ready, q + 1)
                dve.tensor_scalar(nlse[:, ts], lse[:, ts], -1.0, None, ALU.mult).then_inc(p_ready, 1)
                for t in range(QT * q, QT * q + QT):
                    ins = dve.scalar_tensor_tensor(out=y[:, t, :], in0=xn[:, t, 0:D], scalar=lse[:, t:t + 1], in1=prob[:, t, :],
                                                   op0=ALU.subtract, op1=ALU.mult, accum_out=negent[:, t:t + 1])
                ins.then_inc(negent_ready, 1)
                filled(dve, f"pT{q}")
                dve.tensor_copy(pT[:, QW * q:QW * q + QW], psum(f"pT{q}")[:, :]).then_inc(bank_emptied[1], 1)

            moved(dve, "sigT")
            link(dve.tensor_reduce(clsum[:, 0:NCL], sigT[:, 0:NTILES].rearrange("p (c l) -> p c l", c=NCL), AX.X, ALU.add))
            link(dve.tensor_scalar(clsum[:, NCL:2 * NCL], clsum[:, 0:NCL], 0.0, None, ALU.is_lt))
            dve.scalar_tensor_tensor(out=sigT[:, NTILES:NSC], in0=clsum[:, 0:NCL], scalar=0.0, in1=clsum[:, NCL:2 * NCL],
                                     op0=ALU.is_gt, op1=ALU.subtract).then_inc(sigT_ready, 1)
            dve.wait_ge(ffn_in, 16 * 14)
            link(dve.tensor_scalar(temp[:, 0:1], temp[:, 0:1], 1e-6, None, ALU.add))
            link(dve.reciprocal(temp[:, 1:2], temp[:, 0:1]))
            link(dve.tensor_scalar(temp[:, 1:2], temp[:, 1:2], -1.0, None, ALU.mult))
            link(dve.tensor_tensor(dknots[:, 0:7], knots[:, 1:8], knots[:, 0:7], ALU.subtract))

            for q in quarters:
                filled(dve, f"sc{q}")
                dve.tensor_copy(sc[:, QT * q:QT * q + QT, :],
                                psum(f"sc{q}")[:, :].rearrange("p (a b) -> p a b", a=QT)[:, :, 0:NSC]).then_inc(bank_emptied[6], 1)
            filled(dve, "comp")
            dve.tensor_tensor(comp[:, :, :], psum("comp")[:, 0:2 * NT].rearrange("p (a b) -> p a b", b=2),
                              bc(cb2[:, :].unsqueeze(1), [P, NT, 2]), ALU.add).then_inc(bank_emptied[6], 1)
            moved(dve, "sc3")
            dve.tensor_copy(sel8[:, :, :], sc[:, :, NTILES:NSC]).then_inc(cal_in, 1)

            W = NT * 8
            rows = lambda i: small[:, i, :]
            r3 = lambda i: small[:, i, :].rearrange("p (a b) -> p a b", b=8)

            def calibrate(n):
                dve.wait_ge(cal_exp, n + 1)
                link(dve.tensor_scalar(rows(1), rows(0), 1.0, None, ALU.add))
                link(dve.reciprocal(rows(1), rows(1)))
                link(dve.tensor_scalar(rows(1), rows(1), float(NKNOT - 1), None, ALU.mult))
                ge = cal_a[:, :, :, :].rearrange("p t a b -> p (t a) b")
                hot = cal_b[:, :, :, :].rearrange("p t a b -> p (t a) b")
                part = cal_a[:, :, :, :].rearrange("p t a b -> p (t a) b")[:, :, 0:7]
                link(dve.tensor_tensor(ge, bc(rows(1).unsqueeze(2), [P, W, 8]), bc(K("thr").unsqueeze(1), [P, W, 8]), ALU.is_ge))
                link(dve.tensor_tensor(hot, ge[:, :, 0:7], ge[:, :, 1:8], ALU.subtract))
                link(dve.tensor_reduce(rows(2), ge[:, :, 1:7], AX.X, ALU.add))
                link(dve.tensor_tensor(rows(1), rows(1), rows(2), ALU.subtract))
                link(dve.tensor_tensor(part, hot, bc(dknots[:, 0:7].unsqueeze(1), [P, W, 7]), ALU.mult))
                link(dve.tensor_reduce(rows(2), part, AX.X, ALU.add))
                link(dve.tensor_tensor(part, hot, bc(knots[:, 0:7].unsqueeze(1), [P, W, 7]), ALU.mult))
                link(dve.tensor_reduce(rows(3), part, AX.X, ALU.add))
                link(dve.tensor_tensor(rows(1), rows(1), rows(2), ALU.mult))
                link(dve.tensor_tensor(gate8[:, :, :].rearrange("p a b -> p (a b)"), rows(1), rows(3), ALU.add))

            def first_max(out8, values):
                link(dve.tensor_reduce(row16[:, 0, :], values, AX.X, ALU.max))
                link(dve.tensor_tensor(r3(4), values, bc(row16[:, 0, :].unsqueeze(2), [P, NT, 8]), ALU.is_equal))
                link(dve.tensor_tensor(r3(4), r3(4), bc(K("rev").unsqueeze(1), [P, NT, 8]), ALU.mult))
                link(dve.tensor_reduce(row16[:, 0, :], r3(4), AX.X, ALU.max))
                return dve.tensor_tensor(out8, r3(4), bc(row16[:, 0, :].unsqueeze(2), [P, NT, 8]), ALU.is_equal)

            calibrate(0)
            link(first_max(ohc[:, :, :], gate8[:, :, :]))
            link(dve.tensor_tensor(cal_a[:, :, :, :], sc[:, :, 0:NTILES].rearrange("p t (c l) -> p t c l", c=NCL),
                                   bc(ohc[:, :, :].unsqueeze(3), [P, NT, NCL, TPC]), ALU.mult))
            dve.tensor_reduce(sel8[:, :, :], cal_a[:, :, :, :].rearrange("p t c l -> p t l c"), AX.X, ALU.add).then_inc(cal_in, 1)
            calibrate(1)
            link(first_max(ohl[:, :, :], gate8[:, :, :]))
            dve.tensor_tensor(onehot[:, :, :].rearrange("p t (c l) -> p t c l", c=NCL),
                              bc(ohc[:, :, :].unsqueeze(3), [P, NT, NCL, TPC]),
                              bc(ohl[:, :, :].unsqueeze(2), [P, NT, NCL, TPC]), ALU.mult).then_inc(onehot_ready, 1)
            for q in quarters:
                filled(dve, f"oneT{q}")
                dve.tensor_copy(oneT[:, QW * q:QW * q + QW], psum(f"oneT{q}")[0:NTILES, :]).then_inc(bank_emptied[0], 1)

            for i in (6, 7):
                moved(dve, f"pick{i}")
            dve.wait_ge(comp_ready, 1)
            col = lambda at: picked[:, :, at:at + GRID]
            dve.tensor_tensor(spl[:, 0], col(TW1), bc(comp[:, :, 0:1], [P, NT, GRID]), ALU.mult)
            link(dve.tensor_tensor(spl[:, 1], col(TW1 + GRID), bc(comp[:, :, 1:2], [P, NT, GRID]), ALU.mult))
            link(dve.tensor_tensor(spl[:, 0], spl[:, 0], spl[:, 1], ALU.add))
            link(dve.tensor_tensor(spl[:, 0], spl[:, 0], col(TB1), ALU.add))
            link(dve.scalar_tensor_tensor(out=spl[:, 1], in0=spl[:, 0], scalar=0.0, in1=col(TW2), op0=ALU.max, op1=ALU.mult))
            link(dve.tensor_reduce(row16[:, 1, :], spl[:, 1], AX.X, ALU.add))
            link(dve.tensor_tensor(row16[:, 1, :], row16[:, 1, :], picked[:, :, TB2], ALU.add))
            link(dve.tensor_scalar(row16[:, 1, :], row16[:, 1, :], oscale[:, 0:1], None, ALU.mult))
            dve.wait_ge(negent_ready, NQ)
            for b in range(NB):
                tr = range(TB * b, TB * b + TB)
                for t in tr:
                    ins = dve.scalar_tensor_tensor(out=y[:, t, :], in0=picked[:, t, TDIR:TABW], scalar=row16[:, 1, t:t + 1],
                                                   in1=xn[:, t, 0:D], op0=ALU.mult, op1=ALU.add)
                link(ins)
                n = tile_stats(y, tr)
                dve.wait_ge(rstd_ready, n)
                for t in tr:
                    ins = dve.tensor_scalar(y[:, t, :], y[:, t, :], mv[:, t, 0:1], rstd[:, t:t + 1], ALU.subtract, ALU.mult)
                ins.then_inc(yhat_ready, 1)

            dve.wait_ge(nexp_ready, 1)
            for b in range(NB):
                ts = slice(TB * b, TB * b + TB)
                for t in (TB * b + TB - 2, TB * b + TB - 1):
                    moved(dve, f"A{t}")
                link(dve.tensor_tensor(ratio[:, ts], s0[:, ts, D], nexp[:, ts], ALU.mult))
                link(dve.reciprocal(ratio[:, ts], ratio[:, ts]))
                link(dve.tensor_tensor(ratio[:, ts], ratio[:, ts], nexp[:, ts], ALU.mult))
                link(dve.tensor_tensor(s0[:, ts, 0:D], s0[:, ts, 0:D], bc(ratio[:, ts].unsqueeze(2), [P, TB, D]), ALU.mult))
                dve.wait_ge(silu_ready, b + 1)
                link(dve.tensor_tensor(s0[:, ts, 0:D], s0[:, ts, 0:D], y[:, ts, :], ALU.mult))
                dve.tensor_tensor(x[:, ts, :], x[:, ts, :], s0[:, ts, 0:D], ALU.add).then_inc(x2_ready, 1)
                dve.wait_ge(x2_ready, b + 1)
                n = tile_stats(x, range(TB * b, TB * b + TB))
                dve.wait_ge(rstd_ready, n)
                for t in range(TB * b, TB * b + TB):
                    ins = dve.tensor_scalar(xn2[:, t, :], x[:, t, :], mv[:, t, 0:1], rstd[:, t:t + 1], ALU.subtract, ALU.mult)
                ins.then_inc(xn2_ready, 1)

            filled(dve, "lg")
            dve.tensor_tensor(r3(2), psum("lg")[:, 0:W].rearrange("p (a b) -> p a b", b=NE),
                              bc(gate_b[:, :].unsqueeze(1), [P, NT, NE]), ALU.add).then_inc(bank_emptied[6], 1)
            moved(dve, "lg")
            link(dve.tensor_reduce(row16[:, 2, :], r3(2), AX.X, ALU.max))
            dve.tensor_tensor(r3(0), r3(2), bc(row16[:, 2, :].unsqueeze(2), [P, NT, NE]), ALU.subtract).then_inc(lg_ready, 1)
            dve.wait_ge(lg_ready, 1)
            first_max(ohc[:, :, :], r3(0)).then_inc(exp_mask_ready, 1)
            filled(dve, "tot")
            dve.tensor_copy(rows(3).rearrange("p (e t) -> p e t", e=NE),
                            psum("tot")[:, 0:W].rearrange("p (t e) -> p e t", e=NE)).then_inc(bank_emptied[7], 1)
            moved(dve, "tot")
            link(dve.tensor_tensor_scan(rows(4), K("reset"), rows(3), 0.0, ALU.mult, ALU.add))
            link(dve.tensor_tensor(rows(5), rows(4), rows(3), ALU.subtract))
            filled(dve, "cum")
            dve.tensor_tensor(r3(2), psum("cum")[:, 0:W].rearrange("p (t e) -> p t e", e=NE),
                              rows(5).rearrange("p (e t) -> p t e", e=NE), ALU.add).then_inc(bank_emptied[6], 1)
            moved(dve, "cum")
            link(dve.tensor_tensor(r3(2), r3(2), ohc[:, :, :], ALU.mult))
            link(dve.tensor_reduce(row16[:, 3, :], r3(2), AX.X, ALU.add))
            link(dve.tensor_tensor(r3(3), ohc[:, :, :], bc(K("slot0").unsqueeze(1), [P, NT, NE]), ALU.mult))
            link(dve.tensor_reduce(slotv[:, :], r3(3), AX.X, ALU.add))
            link(dve.tensor_tensor(slotv[:, :], slotv[:, :], row16[:, 3, :], ALU.add))
            link(dve.tensor_scalar(row16[:, 3, :], row16[:, 3, :], float(CAP), float(NOWHERE), ALU.is_gt, ALU.mult))
            link(dve.tensor_tensor(slotv[:, :], slotv[:, :], row16[:, 3, :], ALU.add))
            for t in range(NT):
                dve.tensor_scalar(slot_mask[:, t, :], K("iota"), slotv[:, t:t + 1], None, ALU.is_equal).then_inc(slotmask_ready, 1)
            dve.wait_ge(lgexp_ready, 1)
            link(dve.tensor_reduce(gpt[:, 0, :], r3(1), AX.X, ALU.add))
            link(dve.reciprocal(gpt[:, 0, :], gpt[:, 0, :]))
            dve.tensor_copy(info[:, :, 0:2], K("ids").rearrange("p (t k) -> p t k", k=2))
            dve.memset(info[:, :, 2:3], 1.0)
            link(dve.tensor_copy(info[:, :, 3], gpt[:, 0, :]))
            link(dve.tensor_tensor(gpt[:, 1, :], gpt[:, 0, :], info[:, :, 3], ALU.subtract))
            link(dve.tensor_copy(info[:, :, 4], gpt[:, 1, :]))
            link(dve.tensor_tensor(gpt[:, 2, :], gpt[:, 1, :], info[:, :, 4], ALU.subtract))
            dve.tensor_copy(info[:, :, 5], gpt[:, 2, :]).then_inc(info_ready, 1)

            link(dve.memset(dtab, 0.0))
            link(dve.tensor_scalar(dtab, dtab, K("gamma_c"), None, ALU.add))
            link(dve.memset(dtab.rearrange("p (e c) -> p e c", c=CB)[:, :, 0:1], 0.0))

            def chunk_states(b):
                for k in range(2):
                    q = 2 * b + k
                    filled(dve, f"ktok{q}")
                    dve.tensor_tensor(kd[:, QT * k:QT * k + QT, :], psum(f"ktok{q}")[:, :].rearrange("p (a b) -> p a b", a=QT),
                                      bc(K("decay_k").unsqueeze(1), [P, QT, P]), ALU.mult).then_inc(bank_emptied[1], 1)
                for c in range(CT):
                    filled(dve, f"KV{b}.{c}")
                    dve.tensor_tensor(kvm.rearrange("p e (t c) -> p e t c", c=CT)[:, :, :, c],
                                      psum(f"KV{b}.{c}")[:, 0:C * TB].rearrange("p (t e) -> p e t", e=C),
                                      bc(K("mask_kv").unsqueeze(2), [P, C, TB]), ALU.mult).then_inc(bank_emptied[2 + c], 1)
                for c in range(CT):
                    moved(dve, f"KV{b}.{c}")
                flat = lambda ap: ap.rearrange("p e c -> p (e c)")
                dve.tensor_tensor_scan(flat(state), dtab, flat(kvm), 0.0, ALU.mult, ALU.add).then_inc(state_ready, 1)

            def chunk_evacuations(q):
                filled(dve, f"QT{q}")
                dve.tensor_copy(q_plain[:, :], psum(f"QT{q}")[:, :])
                dve.tensor_tensor(q_dec[:, :].rearrange("p (c i) -> p c i", c=CQ), psum(f"QT{q}")[:, :].rearrange("p (c i) -> p c i", c=CQ),
                                  bc(K("decay_q").unsqueeze(1), [P, CQ, C]), ALU.mult).then_inc(bank_emptied[1], 1)
                for i in range(QT):
                    name = f"vrep{q}.{i}"
                    filled(dve, name)
                    dve.tensor_tensor(vexp[:, CT * i:CT * i + CT, :], psum(name)[:, :].rearrange("p (c a) -> p c a", c=CT),
                                      bc(K("mask_v").unsqueeze(1), [P, CT, P]), ALU.mult).then_inc(bank_emptied[turn[name][0]], 1)
                for g in range(NG):
                    name = f"R{q}.{g}"
                    filled(dve, name)
                    dve.tensor_tensor(smask[:, g, :].rearrange("p (c i) -> p c i", c=CQ), psum(name)[:, :].rearrange("p (c i) -> p c i", c=CQ),
                                      bc(K("decay_s")[:, C * g:C * g + C].unsqueeze(1), [P, CQ, C]), ALU.mult)\
                        .then_inc(bank_emptied[2 + g], 1)

            chunk_states(0)
            chunk_evacuations(0)
            filled(dve, "y0")
            chunk_evacuations(1)
            filled(dve, "y1")
            filled(dve, "idx")
            dve.tensor_copy(idx_f[:, :, :], psum("idx")[0:CAP, 0:8 * NE].rearrange("p (e k) -> p e k", e=NE)[:, :, 0:6])\
                .then_inc(bank_emptied[6], 1)
            moved(dve, "idx")
            dve.tensor_tensor(idx_t[:, 0, :], idx_f[:, :, 0], idx_f[:, :, 1], ALU.add)
            dve.tensor_scalar(idx_t[:, 1, :], idx_f[:, :, 2], -1.0, 1.0, ALU.mult, ALU.add)
            link(dve.tensor_tensor(gprob[:, :], idx_f[:, :, 3], idx_f[:, :, 4], ALU.add))
            dve.tensor_tensor(gprob[:, :], gprob[:, :], idx_f[:, :, 5], ALU.add)
            dve.tensor_copy(idx_load[:, :], idx_t[:, 0, :])
            link(dve.tensor_tensor(idx_t[:, 2, :], idx_t[:, 1, :], K("oob", CAP), ALU.mult))
            dve.tensor_tensor(idx_store[:, :], idx_t[:, 2, :], idx_t[:, 0, :], ALU.add).then_inc(idx_ready, 1)

            chunk_states(1)
            chunk_evacuations(2)
            filled(dve, "y2")
            chunk_evacuations(3)

            for q in quarters:
                moved(dve, f"y{q}")
                ins = dve.bn_stats(gnst[:, q, :], yT[:, QW * q:QW * q + QW])
            link(ins)
            for b in range(NB):
                gv = lambda a, w=1: gns[:, b, a:a + w]
                dve.bn_aggr(gv(0, 2), gnst[:, 2 * b:2 * b + 2, :].rearrange("p a b -> p (a b)")).then_inc(gn_mean, 1)
            for b in range(NB):
                gv = lambda a, w=1: gns[:, b, a:a + w]
                filled(dve, f"gn{b}")
                dve.tensor_copy(gv(2, 2), psum(f"gn{b}")[:, 0:2]).then_inc(bank_emptied[4], 1)
                moved(dve, f"gn{b}")
                link(dve.tensor_tensor(gv(8), gv(0), gv(2), ALU.subtract))
                dve.tensor_tensor(gv(4), gv(8), gv(8), ALU.mult).then_inc(gn_dev, 1)
            for b in range(NB):
                gv = lambda a, w=1: gns[:, b, a:a + w]
                filled(dve, f"gd{b}")
                dve.tensor_tensor(gv(5), psum(f"gd{b}")[:, 0:1], gv(3), ALU.add).then_inc(bank_emptied[5], 1)
                moved(dve, f"gd{b}")
                n = variances(dve.tensor_copy(gv(9), gv(5)))
                dve.wait_ge(rstd_ready, n)
                link(dve.tensor_tensor(gv(7), gv(6), gnw[:, 0:1], ALU.mult))
                yb = yT[:, SEQ * b:SEQ * b + SEQ]
                link(dve.tensor_scalar(yb, yb, gv(2), gv(7), ALU.subtract, ALU.mult))
                dve.tensor_scalar(yb, yb, gnw[:, 1:2], None, ALU.add).then_inc(yn_ready, 1)

            for h in range(2):
                filled(dve, f"xgT{h}")
                dve.tensor_copy(xgT[:, 4 * h:4 * h + 4, :], psum(f"xgT{h}")[:, 0:4 * CAP].rearrange("p (e c) -> p e c", e=4))\
                    .then_inc(bank_emptied[h], 1)
            for e in range(NE):
                name = f"h{e}"
                filled(dve, name)
                if 4 <= e < 7:
                    dve.wait_ge(h_used, e - 3)
                elif e == 7:
                    filled(dve, "eo0")
                dve.tensor_tensor(hb[:, e % 4], psum(name)[:, 0:FT * CAP].rearrange("p (f c) -> p f c", f=FT),
                                  bc(b1T[:, FT * e:FT * e + FT].unsqueeze(2), [P, FT, CAP]), ALU.add)\
                    .then_inc(bank_emptied[turn[name][0]], 1)
            dve.wait_ge(sg_in, 16 * NE)
            dve.wait_ge(moe_in, 16 * 3)
            for h in range(2):
                es = slice(4 * h, 4 * h + 4)
                filled(dve, f"eo{h}")
                dve.tensor_tensor(eo[:, es, :], psum(f"eo{h}")[0:CAP, :].rearrange("p (e d) -> p e d", e=4), b2r[:, es, :], ALU.add)\
                    .then_inc(bank_emptied[4 + h], 1)
                moved(dve, f"eo{h}")
                dve.tensor_tensor(eo[:, es, :], eo[:, es, :], bc(gprob[:, es].unsqueeze(2), [CAP, 4, D]), ALU.mult).then_inc(eo_ready, 1)
                dve.wait_ge(silu2_ready, h + 1)
                link(dve.tensor_tensor(eo[:, es, :], eo[:, es, :], sg[:, es, :], ALU.mult))
                dve.tensor_tensor(eo[:, es, :], eo[:, es, :], xg[:, es, 0:D], ALU.add).then_inc(fin_ready, 1)


def constants():
    import numpy as np
    p = np.arange(P)
    gamma = 1.0 - 2.0 ** (-5.0 - np.arange(H))
    c = {k: np.zeros((P, w)) for k, (_, w) in CONST_COLS.items()}
    c["ident"][:] = np.eye(P)
    c["tri"][:] = p[:, None] <= p[None, :]
    c["ones"][:] = 1
    c["avg8"][:] = (p[:, None] // DH == p[None, :] // DH) / DH
    m, j, i = p // C, p % C, np.arange(C)
    for g in range(NG):
        dist = i[None, :] - j[:, None]
        c["decay_s"][:, C * g:C * g + C] = np.where(dist >= 0, gamma[GH * g + m][:, None] ** np.maximum(dist, 0), 0) / np.sqrt(DH)
    c["mask_v"][:] = m[:, None] == (p[None, :] // DH) % GH
    c["mask_kv"][:] = (p[:, None] // DH) % GH == np.arange(C)[None, :] // DH
    c["mask_k"][:] = (p[:, None] // DH) % GH == np.arange(GH)[None, :]
    c["decay_k"][:] = gamma[p // DH][None, :] ** (C - j)[:, None]
    c["decay_q"][:] = gamma[p // DH][:, None] ** i[None, :] / np.sqrt(DH)
    c["gamma_c"][:] = gamma[p // DH][:, None] ** C
    c["thr"][:] = [-1] + list(range(1, NKNOT - 1)) + [1e30]
    c["rev"][:] = np.arange(NE, 0, -1)
    c["slot0"][:] = CAP * np.arange(NE) - 1
    c["iota"][:] = np.arange(SLOTS)
    c["ids"][:, 0::2] = p[:, None]
    c["ids"][:, 1::2] = P * np.arange(NT)
    c["neghalf"][:] = -0.5
    c["oob"][:] = NOWHERE + p[:, None] * NE + np.arange(NE)
    c["reset"][:] = np.arange(NE * NT) % NT != 0
    for k in range(CT):
        c["repeat"][:, P * k:P * k + P] = p[:, None] == C * k + (p % C)[None, :]
    return np.concatenate([c[k] for k in CONST_COLS], axis=1).astype(np.float32)


_INS = ['L0_attn_x', 'L0_ffn_signatures_raw', 'L0_ffn_knot_values', 'L0_ffn_temperature', 'L0_ffn_compress_w1',
        'L0_ffn_compress_b1', 'L0_ffn_compress_w2', 'L0_ffn_compress_b2', 'L0_ffn_spline_w1', 'L0_ffn_spline_b1',
        'L0_ffn_spline_w2', 'L0_ffn_spline_b2', 'L0_ffn_directions', 'L0_ffn_norm_gamma', 'L0_ffn_norm_beta',
        'L0_ffn_output_scale', 'L1_attn_W_q', 'L1_attn_W_k', 'L1_attn_W_v', 'L1_attn_W_o', 'L1_attn_gn_weight',
        'L1_attn_gn_bias', 'L1_ffn_gate_w', 'L1_ffn_gate_b', 'L1_ffn_w1', 'L1_ffn_b1', 'L1_ffn_w2', 'L1_ffn_b2']


def kernel(**inputs):
    import numpy as _np
    import concourse.bacc as _bacc
    from concourse import mybir as _mybir
    from concourse.bass_utils import run_bass_kernel_spmd as _run

    nc = _bacc.Bacc("TRN2", target_bir_lowering=False, num_devices=1)
    arrays, args = {}, []
    for name in _INS:
        a = _np.ascontiguousarray(inputs[name])
        arrays[f"in_{name}"] = a
        args.append(nc.dram_tensor(f"in_{name}", a.shape, _mybir.dt.from_np(a.dtype), kind="ExternalInput").ap())
    a = constants()
    arrays["in_consts"] = a
    args.append(nc.dram_tensor("in_consts", a.shape, _mybir.dt.from_np(a.dtype), kind="ExternalInput").ap())
    args.append(nc.dram_tensor("out_0", (NB, SEQ, D), F32, kind="ExternalOutput").ap())
    kernel_program(nc, *args)
    r = _run(nc, [arrays], core_ids=[0])
    return r.results[0]["out_0"]
```

```python
from contextlib import ExitStack

import concourse.bass as bass
from concourse import mybir

F32 = mybir.dt.float32
BF16 = mybir.dt.bfloat16
U32 = mybir.dt.uint32
ALU = mybir.AluOpType
ACT = mybir.ActivationFunctionType
AX = mybir.AxisListType

P = 128
D = 128
NB, SEQ = 2, 1024
N = NB * SEQ
NT = N // P
TB = SEQ // P
QT = 4
NQ = NT // QT
QW = QT * P
EPS = 1e-5

NTILES, TPC = 64, 8
NCL = NTILES // TPC
NKNOT = 8
COMP, GRID = 32, 16
NSC = NTILES + NCL
TW1, TB1, TW2, TB2, TDIR = 0, 2 * GRID, 3 * GRID, 4 * GRID, 4 * GRID + 1
TABW = TDIR + D

H, DH = 16, 8
C = 32
CT, CQ, CB = P // C, QW // C, SEQ // C
NG, GH = 4, 4

NE, CAP, F = 8, 80, 512
FT = F // P
SLOTS = NE * CAP
NOWHERE = 2 * N

CONST_COLS = {}


def _layout():
    at = 0
    for name, width in (("ident", P), ("tri", P), ("ones", P), ("avg8", P), ("decay_s", NG * C),
                        ("mask_v", P), ("mask_kv", C), ("mask_k", GH), ("mask_q", NG), ("decay_k", P), ("decay_q", C),
                        ("gamma_c", 1), ("thr", NKNOT), ("rev", NE), ("slot0", NE), ("iota", SLOTS),
                        ("ids", NT * 2), ("neghalf", NT), ("oob", NE), ("reset", NE * NT), ("repeat", CT * P)):
        CONST_COLS[name] = (at, width)
        at += width
    return at


CONST_W = _layout()


def kernel_program(nc, L0_attn_x, L0_ffn_signatures_raw, L0_ffn_knot_values, L0_ffn_temperature,
                   L0_ffn_compress_w1, L0_ffn_compress_b1, L0_ffn_compress_w2, L0_ffn_compress_b2,
                   L0_ffn_spline_w1, L0_ffn_spline_b1, L0_ffn_spline_w2, L0_ffn_spline_b2,
                   L0_ffn_directions, L0_ffn_norm_gamma, L0_ffn_norm_beta, L0_ffn_output_scale,
                   L1_attn_W_q, L1_attn_W_k, L1_attn_W_v, L1_attn_W_o, L1_attn_gn_weight, L1_attn_gn_bias,
                   L1_ffn_gate_w, L1_ffn_gate_b, L1_ffn_w1, L1_ffn_b1, L1_ffn_w2, L1_ffn_b2, consts, out):
    rows_xn2 = nc.dram_tensor("rows_xn2", (N, D), F32, kind="Internal").ap()
    rows_g = nc.dram_tensor("rows_g", (N, D), F32, kind="Internal").ap()
    out_rows = out.rearrange("b t d -> (b t) d")

    with ExitStack() as ctx:
        def sb(name, shape, dt=F32):
            return ctx.enter_context(nc.sbuf_tensor(name, shape, dt))

        def sem(name):
            return ctx.enter_context(nc.semaphore(name))

        bank = [ctx.enter_context(nc.psum_tensor(f"bank{i}", [P, 512], F32)) for i in range(8)]
        bank_filled = [sem(f"bank{i}_filled") for i in range(8)]
        bank_emptied = [sem(f"bank{i}_emptied") for i in range(8)]

        cst = sb("cst", [P, CONST_W])

        def K(name, parts=P):
            at, w = CONST_COLS[name]
            return cst[0:parts, at:at + w]

        x = sb("x", [P, NT, D])
        xn = sb("xn", [P, NT, D + 1])
        prob = sb("prob", [P, NT, D])
        xnT = sb("xnT", [P, N])
        pT = sb("pT", [P, N])
        ebuf = sb("ebuf", [P, 2, TB, QW])
        stats = sb("stats", [P, NT, 6])
        mv = sb("mv", [P, NT, 2])
        veps = sb("veps", [P, NT])
        rstd = sb("rstd", [P, NT])
        sumexp = sb("sumexp", [P, NT])
        rsum = sb("rsum", [P, NT])
        lse = sb("lse", [P, NT])
        nlse = sb("nlse", [P, NT])
        negent = sb("negent", [P, NT])
        nexp = sb("nexp", [P, NT])
        s0 = sb("s0", [P, NT, D + 1])
        ratio = sb("ratio", [P, NT])
        sig = sb("sig", [NTILES, 3, D])
        sigT = sb("sigT", [P, NSC])
        clsum = sb("clsum", [P, 2 * NCL])
        sc = sb("sc", [P, NT, NSC])
        knots = sb("knots", [P, NKNOT])
        dknots = sb("dknots", [P, NKNOT])
        temp = sb("temp", [P, 2])
        cw1 = sb("cw1", [P, COMP])
        cb1 = sb("cb1", [COMP, 1])
        cw2 = sb("cw2", [COMP, 2])
        cb2 = sb("cb2", [P, 2])
        hT_room = sb("hT_room", [P, N])
        hT = hT_room[0:COMP, :]
        comp = sb("comp", [P, NT, 2])
        table = sb("table", [NTILES, TABW])
        gamma = sb("gamma", [P, D])
        beta = sb("beta", [P, D])
        oscale = sb("oscale", [P, 1])
        picked_room = sb("picked_room", [P, NT * SLOTS // 2])
        picked = picked_room[:, 0:NT * TABW].rearrange("p (t w) -> p t w", t=NT)
        oneT_room = sb("oneT_room", [P, N])
        oneT = oneT_room[0:NTILES, :]
        cal_b = oneT_room[:, 0:NT * 8 * 7].rearrange("p (t a b) -> p t a b", t=NT, a=8)
        onehot = sb("onehot", [P, NT, NTILES])
        sel8 = sb("sel8", [P, NT, 8])
        gate8 = sb("gate8", [P, NT, 8])
        ohc = sb("ohc", [P, NT, 8])
        ohl = sb("ohl", [P, NT, 8])
        cal_a = sb("cal_a", [P, NT, 8, 8])
        small = sb("small", [P, 6, NT * 8])
        row16 = sb("row16", [P, 4, NT])
        spl = sb("spl", [P, 2, NT, GRID])
        y = sb("y", [P, NT, D])
        xn2 = sb("xn2", [P, NT, D])
        wT = sb("wT", [P, 4, P])
        wraw = xn2[:, 0:4, :]
        gnw = sb("gnw", [P, 2])
        gate_w = sb("gate_w", [P, NE])
        gate_b = sb("gate_b", [P, NE])
        b1raw = sb("b1raw", [NE * FT, P])
        b1T = sb("b1T", [P, NE * FT])
        b2r = sb("b2r", [CAP, NE, D])
        slotv = sb("slotv", [P, NT])
        info = sb("info", [P, NT, 6], BF16)
        gpt = sb("gpt", [P, 3, NT])
        idx_f = sb("idx_f", [CAP, NE, 6])
        idx_t = sb("idx_t", [CAP, 3, NE])
        idx_load = sb("idx_load", [CAP, NE], U32)
        idx_store = sb("idx_store", [CAP, NE], U32)
        gprob = sb("gprob", [CAP, NE])
        zeros = sb("zeros", [P, D])
        gns = sb("gns", [P, NB, 16])
        gnst = sb("gnst", [P, NQ, 6])

        xn2T = xnT
        w1 = sb("w1", [P, NE, F])
        w2 = sb("w2", [P, NE, FT, D])
        kexp = pT[:, :].rearrange("p (c a) -> p c a", c=CQ)
        qexp = ebuf[:, 0].rearrange("p a b -> p (a b)")[:, NG * QW:2 * NG * QW].rearrange("p (c a) -> p c a", c=CQ)
        vexp = [hT_room[:, :].rearrange("p (c a) -> p c a", c=CQ),
                xn[:, :, :].rearrange("p a b -> p (a b)")[:, 0:N].rearrange("p (c a) -> p c a", c=CQ)]
        smask = ebuf[:, 0].rearrange("p a b -> p (a b)")[:, 0:NG * QW].rearrange("p (c g i) -> p c g i", c=CQ, g=NG)
        moe_room = ebuf[:, 1].rearrange("p a b -> p (a b)")
        HB0, EO0 = NE * D + SLOTS, NE * D + SLOTS + 4 * FT * CAP
        xg = moe_room[0:CAP, 0:NE * D].rearrange("p (e d) -> p e d", e=NE)
        xgT = moe_room[:, NE * D:HB0].rearrange("p (e c) -> p e c", e=NE)
        hb = moe_room[:, HB0:EO0].rearrange("p (n f c) -> p n f c", n=4, f=FT)
        eo = moe_room[0:CAP, EO0:EO0 + NE * D].rearrange("p (e d) -> p e d", e=NE)

        def q_keep(q):
            return cal_a[:, :, :, :].rearrange("p a b c -> p (a b c)")[:, QW * (q % 2):QW * (q % 2) + QW]

        kd = y[:, 0:TB, :]
        vtok = y[:, TB:NT, :]
        kvm = prob[:, 0:TB, :].rearrange("p a b -> p (a b)").rearrange("p (e c) -> p e c", e=C)
        state = prob[:, TB:NT, :].rearrange("p a b -> p (a b)").rearrange("p (e c) -> p e c", e=C)
        dtab = s0[:, :, :].rearrange("p a b -> p (a b)")[:, 0:C * CB]
        yT = oneT_room
        slot_mask = picked_room[:, :].bitcast(BF16).rearrange("p (t s) -> p t s", t=NT)
        g_tok = picked_room[:, 0:NT * D].rearrange("p (t d) -> p t d", t=NT)

        ident_in = sem("ident_in")
        consts_in = sem("consts_in")
        x_in = [sem(f"x_in{q}") for q in range(NQ)]
        sig_in = sem("sig_in")
        ffn_in = sem("ffn_in")
        w_in = sem("w_in")
        moe_in = sem("moe_in")
        dve_step = sem("dve_step")
        pool_step = sem("pool_step")
        var_ready = sem("var_ready")
        rstd_ready = sem("rstd_ready")
        xn_ready = sem("xn_ready")
        exp_ready = sem("exp_ready")
        sum_ready = sem("sum_ready")
        lse_ready = sem("lse_ready")
        p_ready = sem("p_ready")
        negent_ready = sem("negent_ready")
        nexp_ready = sem("nexp_ready")
        sig_ready = sem("sig_ready")
        sigT_ready = sem("sigT_ready")
        comp_ready = sem("comp_ready")
        cal_in = sem("cal_in")
        cal_exp = sem("cal_exp")
        onehot_ready = sem("onehot_ready")
        yhat_ready = sem("yhat_ready")
        yaff_ready = sem("yaff_ready")
        silu_ready = sem("silu_ready")
        x2_ready = sem("x2_ready")
        xn2_ready = sem("xn2_ready")
        rows_stored = sem("rows_stored")
        zeros_ready = sem("zeros_ready")
        zeros_stored = sem("zeros_stored")
        qexp_ready = sem("qexp_ready")
        lg_ready = sem("lg_ready")
        lgexp_ready = sem("lgexp_ready")
        exp_mask_ready = sem("exp_mask_ready")
        slotmask_ready = sem("slotmask_ready")
        info_ready = sem("info_ready")
        idx_ready = sem("idx_ready")
        xg_in = sem("xg_in")
        state_ready = sem("state_ready")
        gn_mean = sem("gn_mean")
        gn_dev = sem("gn_dev")
        yn_ready = sem("yn_ready")
        g_stored = sem("g_stored")
        g_in = [sem(f"g_in{q}") for q in range(NQ)]
        h_ready = sem("h_ready")
        eo_ready = sem("eo_ready")
        silu2_ready = sem("silu2_ready")
        fin_ready = sem("fin_ready")
        out_stored = sem("out_stored")

        quarters = range(NQ)
        turns = {
            0: [f"xnT{q}" for q in quarters] + ["sigT"] + [f"oneT{q}" for q in quarters]
               + [f"xn2T{q}" for q in quarters] + ["b1T"]
               + [n for q in (0, 1, 2) for n in (f"QT{q}", f"vrep{q}.1", f"vrep{q}.3")]
               + ["eo0", "eo1", "QT3", "vrep3.1", "vrep3.3", "eo2", "eo3"],
            1: [f"pT{q}" for q in quarters] + ["wT"] + [f"pick{i}" for i in range(0, NT // 2, 2)]
               + ["ktok0", "ktok1", "KT0", "KT1", "ktok2", "ktok3", "KT2", "xgT0", "h0", "h2", "h4", "h6", "KT3", "s2_1"],
            6: [f"sc{q}" for q in quarters] + ["comp", "lg", "cum"]
               + [f"vrep{q}.{i}" for q in (0, 1) for i in (0, 2)] + ["idx", "vrep2.0", "vrep2.2", "xgT1", "h1", "h3", "gn0", "gd0",
                                                                 "h5", "h7", "vrep3.0", "vrep3.2", "s2_0"],
            7: [f"h0_{q}" for q in quarters] + [f"pick{i}" for i in range(1, NT // 2, 2)]
               + ["vtok0", "vtok1", "tot", "y0", "vtok2", "vtok3", "y1", "y2", "y3"],
        }
        last = {2: ["s2_2"], 3: ["s2_3"], 4: ["gn1"], 5: ["gd1"]}
        for i in range(NG):
            if i < 2:
                head = [f"S{b}.{h}.{j}" for b in range(NB) for h in range(2) for j in range(i, TB, 2)]
            else:
                head = [f"A{t}" for t in range(i - 2, NT, 2)]
            turns[2 + i] = head + [f"KV0.{i}", f"R0.{i}", f"R1.{i}", f"KV1.{i}", f"R2.{i}", f"R3.{i}"] + last[2 + i]
        turn = {name: (b, n) for b, names in turns.items() for n, name in enumerate(names)}
        in_order = {b: list(names) for b, names in turns.items()}

        def psum(name):
            return bank[turn[name][0]]

        def free(pe, name):
            b, n = turn[name]
            assert in_order[b].pop(0) == name, name
            if n:
                pe.wait_ge(bank_emptied[b], n)
            return bank[b]

        def filled(eng, name):
            b, n = turn[name]
            eng.wait_ge(bank_filled[b], n + 1)
            return bank[b]

        def moved(eng, name):
            b, n = turn[name]
            eng.wait_ge(bank_emptied[b], n + 1)

        block = ctx.enter_context(nc.Block())

        def bc(ap, shape):
            return ap.to_broadcast(shape)

        @block.sync
        def _(sp):
            i0, iw = CONST_COLS["ident"]
            sp.dma_start(cst[:, i0:i0 + iw], consts[:, i0:i0 + iw]).then_inc(ident_in, 16)
            xr = L0_attn_x.rearrange("b (t p) d -> p (b t) d", p=P)
            for q in range(NQ):
                sp.dma_start(x[:, QT * q:QT * q + QT, :], xr[:, QT * q:QT * q + QT, :]).then_inc(x_in[q], 16)
            sp.dma_start(cst[:, iw:], consts[:, iw:]).then_inc(consts_in, 16)
            for j, w in enumerate((L1_attn_W_q, L1_attn_W_k, L1_attn_W_v, L1_attn_W_o)):
                sp.dma_start(wraw[:, j, :], w).then_inc(w_in, 16)
            sp.dma_start(gnw[:, 0:1], L1_attn_gn_weight.unsqueeze(1)).then_inc(w_in, 16)
            sp.dma_start(gnw[:, 1:2], L1_attn_gn_bias.unsqueeze(1)).then_inc(w_in, 16)
            sp.dma_start(gate_w[:, :], L1_ffn_gate_w).then_inc(w_in, 16)
            sp.dma_start(gate_b[:, :], L1_ffn_gate_b.partition_broadcast(P)).then_inc(w_in, 16)
            sp.dma_start(b1raw[:, :], L1_ffn_b1.rearrange("e (f p) -> (e f) p", p=P)).then_inc(w_in, 16)
            sp.dma_start(b2r[:, :, :], L1_ffn_b2.partition_broadcast(CAP)).then_inc(moe_in, 16)
            sp.dma_start(w1[:, :, :], L1_ffn_w1.rearrange("e d f -> d e f")).then_inc(moe_in, 16)
            sp.dma_start(w2[:, :, :, :], L1_ffn_w2.rearrange("e (f p) d -> p e f d", p=P)).then_inc(moe_in, 16)
            sp.wait_ge(zeros_ready, 1)
            sp.dma_start(rows_g.rearrange("(t p) d -> p t d", p=P), bc(zeros[:, :].unsqueeze(1), [P, NT, D])).then_inc(zeros_stored, 16)
            rows = rows_xn2.rearrange("(t p) w -> p t w", p=P)
            for b in range(NB):
                ts = slice(TB * b, TB * b + TB)
                sp.wait_ge(xn2_ready, b + 1)
                sp.dma_start(rows[:, ts, :], xn2[:, ts, :]).then_inc(rows_stored, 16)
            sp.wait_ge(g_stored, 16 * NE)
            growv = rows_g.rearrange("(t p) d -> p t d", p=P)
            for q in range(NQ):
                sp.dma_start(g_tok[:, QT * q:QT * q + QT, :], growv[:, QT * q:QT * q + QT, :]).then_inc(g_in[q], 16)
            outr = out_rows.rearrange("(t p) d -> p t d", p=P)
            for q in range(NQ):
                sp.wait_ge(fin_ready, q + 1)
                sp.dma_start(outr[:, QT * q:QT * q + QT, :], x[:, QT * q:QT * q + QT, :]).then_inc(out_stored, 16)
            sp.wait_ge(rows_stored, 16 * NB)
            sp.wait_ge(zeros_stored, 16)
            sp.wait_ge(out_stored, 16 * NQ)

        @block.gpsimd
        def _(pool):
            n_step = [0]

            def link(ins):
                n_step[0] += 1
                ins.then_inc(pool_step, 1)
                pool.wait_ge(pool_step, n_step[0])

            uses = [0]

            def inv_sqrt(out_ap, var_ap, n, parts=P):
                uses[0] += 1
                pool.wait_ge(var_ready, uses[0])
                link(pool.tensor_scalar(veps[0:parts, 0:n], var_ap, EPS, None, ALU.add))
                pool.tensor_tensor(out_ap, veps[0:parts, 0:n], K("neghalf")[0:parts, 0:n], ALU.pow).then_inc(rstd_ready, 1)
                pool.wait_ge(rstd_ready, uses[0])

            pool.memset(xn[:, :, D:D + 1], 1.0).then_inc(xn_ready, 1)
            pool.memset(zeros[:, :], 0.0).then_inc(zeros_ready, 1)
            pool.wait_ge(consts_in, 16)
            for q in range(NQ):
                ts = slice(QT * q, QT * q + QT)
                inv_sqrt(rstd[:, ts], mv[:, ts, 1], QT)
            for b in range(NB):
                ts = slice(TB * b, TB * b + TB)
                inv_sqrt(rstd[:, ts], mv[:, ts, 1], TB)
                pool.wait_ge(yhat_ready, b + 1)
                link(pool.tensor_tensor(y[:, ts, :], y[:, ts, :], bc(gamma[:, :].unsqueeze(1), [P, TB, D]), ALU.mult))
                pool.tensor_tensor(y[:, ts, :], y[:, ts, :], bc(beta[:, :].unsqueeze(1), [P, TB, D]), ALU.add)\
                    .then_inc(yaff_ready, 1)
            for b in range(NB):
                ts = slice(TB * b, TB * b + TB)
                inv_sqrt(rstd[:, ts], mv[:, ts, 1], TB)
            pool.wait_ge(idx_ready, 1)
            pool.wait_ge(rows_stored, 16 * NB)
            for e in range(NE):
                pool.indirect_dma_start(xg[:, e, :], None, rows_xn2, bass.IndirectOffsetOnAxis(ap=idx_load[:, e:e + 1], axis=0))\
                    .then_inc(xg_in, 16)
            inv_sqrt(gns[:, 0, 6:7], gns[:, 0, 5:6], 1)
            pool.wait_ge(silu2_ready, 1)
            pool.wait_ge(zeros_stored, 16)
            for e in range(NE):
                pool.indirect_dma_start(rows_g, bass.IndirectOffsetOnAxis(ap=idx_store[:, e:e + 1], axis=0),
                                        eo[:, e, :], None, bounds_check=N - 1, oob_is_err=False).then_inc(g_stored, 16)
            inv_sqrt(gns[:, 1, 6:7], gns[:, 1, 5:6], 1)

        @block.scalar
        def _(act):
            act.dma_start(sig[:, 0, :], L0_ffn_signatures_raw).then_inc(sig_in, 16)
            for dst, src in ((cw1[:, :], L0_ffn_compress_w1), (cb1[:, :], L0_ffn_compress_b1.unsqueeze(1)),
                             (cw2[:, :], L0_ffn_compress_w2), (cb2[:, :], L0_ffn_compress_b2.partition_broadcast(P)),
                             (knots[:, :], L0_ffn_knot_values.partition_broadcast(P)),
                             (temp[:, 0:1], L0_ffn_temperature.partition_broadcast(P)),
                             (oscale[:, :], L0_ffn_output_scale.partition_broadcast(P)),
                             (gamma[:, :], L0_ffn_norm_gamma.partition_broadcast(P)),
                             (beta[:, :], L0_ffn_norm_beta.partition_broadcast(P)),
                             (table[:, TW1:TB1], L0_ffn_spline_w1.rearrange("t i g -> t (i g)")),
                             (table[:, TB1:TW2], L0_ffn_spline_b1),
                             (table[:, TW2:TB2], L0_ffn_spline_w2.rearrange("t g o -> t (g o)")),
                             (table[:, TB2:TDIR], L0_ffn_spline_b2),
                             (table[:, TDIR:TABW], L0_ffn_directions)):
                act.dma_start(dst, src).then_inc(ffn_in, 16)
            act.preload_act_table(ACT.Ln)
            for q in range(NQ):
                ts = slice(QT * q, QT * q + QT)
                act.wait_ge(xn_ready, q + 2)
                act.activation(prob[:, ts, :], xn[:, ts, 0:D], ACT.Exp).then_inc(exp_ready, 1)
                filled(act, f"xnT{q}")
                act.activation(xnT[:, QW * q:QW * q + QW], psum(f"xnT{q}")[:, :], ACT.Copy).then_inc(bank_emptied[0], 1)
                act.wait_ge(sum_ready, q + 1)
                act.activation(lse[:, ts], sumexp[:, ts], ACT.Ln).then_inc(lse_ready, 1)
            act.wait_ge(negent_ready, NQ)
            act.activation(nexp[:, :], negent[:, :], ACT.Exp, scale=-1.0).then_inc(nexp_ready, 1)
            filled(act, "sigT")
            act.activation(sigT[:, 0:NTILES], psum("sigT")[:, 0:NTILES], ACT.Copy).then_inc(bank_emptied[0], 1)
            filled(act, "wT")
            act.activation(wT[:, :, :].rearrange("p a b -> p (a b)"), psum("wT")[:, :], ACT.Copy).then_inc(bank_emptied[1], 1)
            act.wait_ge(ffn_in, 16 * 14)
            for q in range(NQ):
                filled(act, f"h0_{q}")
                act.activation(hT[:, QW * q:QW * q + QW], psum(f"h0_{q}")[0:COMP, :], ACT.Gelu, bias=cb1[:, 0:1])\
                    .then_inc(bank_emptied[7], 1)
            moved(act, "comp")
            cflat = comp[:, :, :].rearrange("p a b -> p (a b)")
            act.activation(cflat, cflat, ACT.Tanh).then_inc(comp_ready, 1)

            def calibrate_exp(n):
                act.wait_ge(cal_in, n + 1)
                act.activation(small[:, 0, :], sel8[:, :, :].rearrange("p a b -> p (a b)"), ACT.Exp,
                               scale=temp[:, 1:2]).then_inc(cal_exp, 1)

            calibrate_exp(0)

            def attention_exps(b, h):
                half = 2 * b + h
                if half >= 2:
                    filled(act, f"A{QT * (half - 1) - 1}")
                for j in range(TB):
                    filled(act, f"S{b}.{h}.{j}")
                    act.activation(ebuf[:, half % 2, j, :], psum(f"S{b}.{h}.{j}")[:, :], ACT.Exp,
                                   bias=nlse[:, TB * b + j:TB * b + j + 1]).then_inc(bank_emptied[2 + j % 2], 1)
                    if half == 0 and j == 5:
                        calibrate_exp(1)

            def attention_copy(h):
                for i in range(QT):
                    t = QT * h + i
                    filled(act, f"A{t}")
                    act.activation(s0[:, t, :], psum(f"A{t}")[:, 0:D + 1], ACT.Copy).then_inc(bank_emptied[4 + t % 2], 1)

            act.wait_ge(p_ready, NQ)
            attention_exps(0, 0)
            attention_exps(0, 1)
            attention_copy(0)
            for i in range(8):
                filled(act, f"pick{i}")
                act.activation(picked[:, 2 * i:2 * i + 2, :], psum(f"pick{i}")[:, 0:2 * TABW].rearrange("p (a b) -> p a b", a=2),
                               ACT.Copy).then_inc(bank_emptied[turn[f"pick{i}"][0]], 1)
            attention_copy(1)
            attention_exps(1, 0)
            attention_exps(1, 1)
            attention_copy(2)
            attention_copy(3)
            for b in range(NB):
                act.wait_ge(yaff_ready, b + 1)
                ts = slice(TB * b, TB * b + TB)
                act.activation(y[:, ts, :], y[:, ts, :], ACT.Silu).then_inc(silu_ready, 1)
            for q in range(NQ):
                filled(act, f"xn2T{q}")
                act.activation(xn2T[:, QW * q:QW * q + QW], psum(f"xn2T{q}")[:, :], ACT.Copy).then_inc(bank_emptied[0], 1)
            filled(act, "b1T")
            act.activation(b1T[:, :], psum("b1T")[:, 0:NE * FT], ACT.Copy).then_inc(bank_emptied[0], 1)
            act.wait_ge(lg_ready, 1)
            act.activation(small[:, 1, :], small[:, 0, :], ACT.Exp).then_inc(lgexp_ready, 1)

            def output_copy(q):
                filled(act, f"y{q}")
                act.activation(yT[:, QW * q:QW * q + QW], psum(f"y{q}")[:, :], ACT.Copy).then_inc(bank_emptied[7], 1)

            def value_copies(b):
                for k in range(2):
                    q = 2 * b + k
                    filled(act, f"vtok{q}")
                    act.activation(vtok[:, QT * k:QT * k + QT, :], psum(f"vtok{q}")[:, :].rearrange("p (a b) -> p a b", a=QT),
                                   ACT.Copy).then_inc(bank_emptied[7], 1)

            def spread(q):
                filled(act, f"KT{q}")
                if q:
                    filled(act, f"R{q - 1}.{NG - 1}")
                for m in range(GH):
                    ins = act.activation(kexp[:, :, C * m:C * m + C], psum(f"KT{q}")[:, :].rearrange("p (c j) -> p c j", c=CQ),
                                         ACT.Copy, scale=K("mask_k")[:, m:m + 1])
                ins.then_inc(bank_emptied[1], 1)
                moved(act, f"QT{q}")
                for g in range(NG):
                    ins = act.activation(qexp[:, :, C * g:C * g + C], q_keep(q).rearrange("p (c i) -> p c i", c=CQ),
                                         ACT.Copy, scale=K("mask_q")[:, g:g + 1])
                ins.then_inc(qexp_ready, 1)

            def hidden_gelu(e):
                moved(act, f"h{e}")
                hv = hb[:, e % 4].rearrange("p f c -> p (f c)")
                act.activation(hv, hv, ACT.Gelu_apprx_tanh).then_inc(h_ready, 1)

            value_copies(0)
            spread(0)
            spread(1)
            output_copy(0)
            value_copies(1)
            spread(2)
            output_copy(1)
            for e in range(4):
                hidden_gelu(e)
            output_copy(2)
            for e in range(4, NE):
                hidden_gelu(e)
            spread(3)
            act.wait_ge(eo_ready, 1)
            ev = eo[:, :, :].rearrange("p e d -> p (e d)")
            act.activation(ev, ev, ACT.Silu).then_inc(silu2_ready, 1)
            output_copy(3)

        @block.tensor
        def _(pe):
            idt = K("ident")
            pe.wait_ge(ident_in, 16)

            def done(ins, name):
                ins.then_inc(bank_filled[turn[name][0]], 1)

            def transposes(name, srcs, rows=P):
                out_bank = free(pe, name)
                for i, src in enumerate(srcs):
                    ins = pe.transpose(out_bank[0:src.shape[1], P * i:P * i + src.shape[0]], src, idt[0:src.shape[0], 0:src.shape[0]])
                done(ins, name)

            for q in range(NQ):
                pe.wait_ge(xn_ready, q + 2)
                transposes(f"xnT{q}", [xn[:, QT * q + i, 0:D] for i in range(QT)])
                pe.wait_ge(p_ready, q + 1)
                transposes(f"pT{q}", [prob[:, QT * q + i, :] for i in range(QT)])
            pe.wait_ge(sig_ready, 1)
            transposes("sigT", [sig[:, 2, :]])
            pe.wait_ge(w_in, 16 * 9)
            transposes("wT", [wraw[:, j, :] for j in range(4)])
            pe.wait_ge(ffn_in, 16 * 14)
            pe.wait_ge(sigT_ready, 1)
            for q in range(NQ):
                moved(pe, f"xnT{q}")
                ob = free(pe, f"h0_{q}")
                done(pe.matmul(ob[0:COMP, :], cw1[:, :], xnT[:, QW * q:QW * q + QW], start=True, stop=True), f"h0_{q}")
                ob = free(pe, f"sc{q}")
                for i in range(QT):
                    t = QT * q + i
                    ins = pe.matmul(ob[:, P * i:P * i + NSC], xnT[:, P * t:P * t + P], sigT[:, :], start=True, stop=True)
                done(ins, f"sc{q}")
            ob = free(pe, "comp")
            for t in range(NT):
                if t % QT == 0:
                    moved(pe, f"h0_{t // QT}")
                ins = pe.matmul(ob[:, 2 * t:2 * t + 2], hT[:, P * t:P * t + P], cw2[:, :], start=True, stop=True)
            done(ins, "comp")

            moved(pe, f"pT{NQ - 1}")

            def scores(b, h):
                for j in range(TB):
                    name = f"S{b}.{h}.{j}"
                    ob = free(pe, name)
                    t = TB * b + j
                    done(pe.matmul(ob[:, :], xnT[:, P * t:P * t + P], pT[:, SEQ * b + QW * h:SEQ * b + QW * h + QW],
                                   start=True, stop=True), name)

            def values(b, h):
                half = 2 * b + h
                for i in range(QT):
                    t = QT * half + i
                    ob = free(pe, f"A{t}")
                    for j in range(TB):
                        if i == 0:
                            moved(pe, f"S{b}.{h}.{j}")
                        ins = pe.matmul(ob[:, 0:D + 1], ebuf[:, half % 2, j, P * i:P * i + P], xn[:, TB * b + j, :],
                                        start=(j == 0), stop=(j == TB - 1))
                    done(ins, f"A{t}")

            def pick_rows():
                for q in range(NQ):
                    pe.wait_ge(onehot_ready, 1)
                    transposes(f"oneT{q}", [onehot[:, QT * q + i, :] for i in range(QT)])
                for i in range(NT // 2):
                    name = f"pick{i}"
                    ob = free(pe, name)
                    moved(pe, f"oneT{2 * i // QT}")
                    for k in range(2):
                        t = 2 * i + k
                        ins = pe.matmul(ob[:, TABW * k:TABW * k + TABW], oneT[:, P * t:P * t + P], table[:, :], start=True, stop=True)
                    done(ins, name)

            scores(0, 0)
            scores(0, 1)
            values(0, 0)
            pick_rows()
            values(0, 1)
            scores(1, 0)
            scores(1, 1)
            values(1, 0)
            values(1, 1)

            for q in range(NQ):
                pe.wait_ge(xn2_ready, q // 2 + 1)
                transposes(f"xn2T{q}", [xn2[:, QT * q + i, :] for i in range(QT)])
            transposes("b1T", [b1raw[:, :]])
            ob = free(pe, "lg")
            for t in range(NT):
                if t % QT == 0:
                    moved(pe, f"xn2T{t // QT}")
                ins = pe.matmul(ob[:, NE * t:NE * t + NE], xn2T[:, P * t:P * t + P], gate_w[:, :], start=True, stop=True)
            done(ins, "lg")

            def key_value_states(b):
                for name, w in (("ktok", 1), ("vtok", 2)):
                    for k in range(2):
                        q = 2 * b + k
                        ob = free(pe, f"{name}{q}")
                        for i in range(QT):
                            t = QT * q + i
                            ins = pe.matmul(ob[:, P * i:P * i + P], xn2T[:, P * t:P * t + P], wT[:, w, :], start=True, stop=True)
                        done(ins, f"{name}{q}")
                moved(pe, f"ktok{2 * b + 1}")
                moved(pe, f"vtok{2 * b + 1}")
                for c in range(CT):
                    ob = free(pe, f"KV{b}.{c}")
                    rows = slice(C * c, C * c + C)
                    for t in range(TB):
                        for g in range(NG):
                            cols = slice(C * g, C * g + C)
                            ins = pe.matmul(ob[cols, C * t:C * t + C], kd[rows, t, cols], vtok[rows, t, cols],
                                            start=True, stop=True, tile_position=(C * c, C * g))
                    done(ins, f"KV{b}.{c}")

            def chunk_inputs(q):
                for name, w in (("KT", 1), ("QT", 0)):
                    ob = free(pe, f"{name}{q}")
                    done(pe.matmul(ob[:, :], wT[:, w, :], xn2T[:, QW * q:QW * q + QW], start=True, stop=True), f"{name}{q}")
                for i in range(QT):
                    ob = free(pe, f"vrep{q}.{i}")
                    for c in range(CT):
                        ins = pe.matmul(ob[:, P * c:P * c + P], K("repeat")[:, P * c:P * c + P],
                                        vtok[:, QT * (q % 2) + i, :], start=True, stop=True)
                    done(ins, f"vrep{q}.{i}")

            def chunk_scores(q):
                moved(pe, f"KT{q}")
                pe.wait_ge(qexp_ready, q + 1)
                for k in range(QT):
                    ob = free(pe, f"R{q}.{k}")
                    for c in range(CT):
                        ins = pe.matmul(ob[:, P * c:P * c + P], kexp[:, CT * k + c, :], qexp[:, CT * k + c, :], start=True, stop=True)
                    done(ins, f"R{q}.{k}")

            def chunk_outputs(q):
                b = q // 2
                moved(pe, f"vrep{q}.2")
                moved(pe, f"vrep{q}.3")
                pe.wait_ge(state_ready, b + 1)
                ob = free(pe, f"y{q}")
                for c in range(CQ):
                    if c % CT == 0:
                        moved(pe, f"R{q}.{c // CT}")
                    for g in range(NG):
                        rows = slice(C * g, C * g + C)
                        cb = CQ * (q % 2) + c
                        cols = slice(C * c, C * c + C)
                        ins = pe.matmul(ob[rows, cols], vexp[q % 2][:, c, rows], smask[:, c, g, :], start=True, stop=(cb == 0))
                        if cb:
                            ins = pe.matmul(ob[rows, cols], state[rows, :, cb - 1], q_keep(q)[rows, cols], start=False, stop=True,
                                            tile_position=(C * g, C * g))
                done(ins, f"y{q}")

            def count_experts():
                pe.wait_ge(exp_mask_ready, 1)
                m8 = ohc[:, :, :].rearrange("p a b -> p (a b)")
                ob = free(pe, "cum")
                done(pe.matmul(ob[:, 0:NT * NE], K("tri"), m8, start=True, stop=True), "cum")
                ob = free(pe, "tot")
                done(pe.matmul(ob[:, 0:NT * NE], K("ones"), m8, start=True, stop=True), "tot")

            def slot_tokens():
                pe.wait_ge(slotmask_ready, NT)
                pe.wait_ge(info_ready, 1)
                ob = free(pe, "idx")
                for e in range(NE):
                    for t in range(NT):
                        ins = pe.matmul(ob[0:CAP, 8 * e:8 * e + 6], slot_mask[:, t, CAP * e:CAP * e + CAP], info[:, t, :],
                                        start=(t == 0), stop=(t == NT - 1))
                done(ins, "idx")

            def norm_sums(name, srcs, b):
                ob = free(pe, name)
                done(pe.matmul(ob[:, 0:srcs.shape[1]], K("avg8"), srcs, start=True, stop=True), name)

            def norm_means(b):
                pe.wait_ge(gn_mean, b + 1)
                norm_sums(f"gn{b}", gns[:, b, 0:2], b)

            def norm_devs(b):
                pe.wait_ge(gn_dev, b + 1)
                norm_sums(f"gd{b}", gns[:, b, 4:5], b)

            def slot_rows():
                pe.wait_ge(xg_in, 16 * NE)
                for h in range(2):
                    ob = free(pe, f"xgT{h}")
                    for k in range(4):
                        ins = pe.transpose(ob[:, CAP * k:CAP * k + CAP], xg[:, 4 * h + k, :], idt[0:CAP, 0:CAP])
                    done(ins, f"xgT{h}")
                pe.wait_ge(moe_in, 16 * 3)

            def expert_hidden(e):
                ob = free(pe, f"h{e}")
                moved(pe, f"xgT{e // 4}")
                for f in range(FT):
                    ins = pe.matmul(ob[:, CAP * f:CAP * f + CAP], w1[:, e, P * f:P * f + P], xgT[:, e, :], start=True, stop=True)
                done(ins, f"h{e}")

            def expert_out(e):
                name = f"eo{e // 2}"
                ob = free(pe, name) if e % 2 == 0 else psum(name)
                pe.wait_ge(h_ready, e + 1)
                for f in range(FT):
                    ins = pe.matmul(ob[0:CAP, D * (e % 2):D * (e % 2) + D], hb[:, e % 4, f, :], w2[:, e, f, :],
                                    start=(f == 0), stop=(f == FT - 1))
                if e % 2:
                    done(ins, name)

            def project(q):
                pe.wait_ge(yn_ready, q // 2 + 1)
                ob = free(pe, f"s2_{q}")
                for i in range(QT):
                    t = QT * q + i
                    ins = pe.matmul(ob[:, P * i:P * i + P], yT[:, P * t:P * t + P], wT[:, 3, :], start=True, stop=True)
                done(ins, f"s2_{q}")

            key_value_states(0)
            count_experts()
            chunk_inputs(0)
            chunk_scores(0)
            chunk_inputs(1)
            chunk_outputs(0)
            chunk_scores(1)
            slot_tokens()
            key_value_states(1)
            chunk_inputs(2)
            chunk_outputs(1)
            slot_rows()
            chunk_scores(2)
            for e in range(4):
                expert_hidden(e)
            norm_means(0)
            chunk_outputs(2)
            norm_devs(0)
            for e in range(4):
                expert_out(e)
            for e in range(4, NE):
                expert_hidden(e)
            chunk_inputs(3)
            for e in range(4, NE):
                expert_out(e)
            chunk_scores(3)
            chunk_outputs(3)
            project(0)
            project(1)
            norm_means(1)
            norm_devs(1)
            project(2)
            project(3)
            assert not any(in_order.values())

        @block.vector
        def _(dve):
            n_step = [0]

            def link(ins):
                n_step[0] += 1
                ins.then_inc(dve_step, 1)
                dve.wait_ge(dve_step, n_step[0])

            n_var = [0]

            def variances(ins):
                n_var[0] += 1
                ins.then_inc(var_ready, 1)
                return n_var[0]

            def tile_stats(src, ts):
                for t in ts:
                    ins = dve.bn_stats(stats[:, t, :], src[:, t, 0:D])
                link(ins)
                for t in ts:
                    ins = dve.bn_aggr(mv[:, t, :], stats[:, t, :])
                return variances(ins)

            dve.wait_ge(sig_in, 16)
            raw = sig[:, 0, :]
            dve.tensor_scalar(sig[:, 1, :], raw, 0.3, None, ALU.is_gt)
            link(dve.tensor_scalar(sig[:, 2, :], raw, -0.3, None, ALU.is_lt))
            link(dve.tensor_tensor(sig[:, 1, :], sig[:, 1, :], sig[:, 2, :], ALU.subtract))
            link(dve.tensor_tensor(sig[:, 1, :], sig[:, 1, :], raw, ALU.subtract))
            dve.tensor_tensor(sig[:, 2, :], sig[:, 1, :], raw, ALU.add).then_inc(sig_ready, 1)

            for q in quarters:
                dve.wait_ge(x_in[q], 16)
                tile_stats(x, range(QT * q, QT * q + QT))
            for q in quarters:
                dve.wait_ge(rstd_ready, q + 1)
                for t in range(QT * q, QT * q + QT):
                    ins = dve.tensor_scalar(xn[:, t, 0:D], x[:, t, :], mv[:, t, 0:1], rstd[:, t:t + 1], ALU.subtract, ALU.mult)
                ins.then_inc(xn_ready, 1)
            for q in quarters:
                ts = slice(QT * q, QT * q + QT)
                dve.wait_ge(exp_ready, q + 1)
                dve.tensor_reduce(sumexp[:, ts], prob[:, ts, :], AX.X, ALU.add).then_inc(sum_ready, 1)
                dve.wait_ge(sum_ready, q + 1)
                link(dve.reciprocal(rsum[:, ts], sumexp[:, ts]))
                link(dve.tensor_tensor(prob[:, ts, :], prob[:, ts, :], bc(rsum[:, ts].unsqueeze(2), [P, QT, D]), ALU.mult))
                dve.wait_ge(lse_ready, q + 1)
                dve.tensor_scalar(nlse[:, ts], lse[:, ts], -1.0, None, ALU.mult).then_inc(p_ready, 1)
                for t in range(QT * q, QT * q + QT):
                    ins = dve.scalar_tensor_tensor(out=y[:, t, :], in0=xn[:, t, 0:D], scalar=lse[:, t:t + 1], in1=prob[:, t, :],
                                                   op0=ALU.subtract, op1=ALU.mult, accum_out=negent[:, t:t + 1])
                ins.then_inc(negent_ready, 1)
                filled(dve, f"pT{q}")
                dve.tensor_copy(pT[:, QW * q:QW * q + QW], psum(f"pT{q}")[:, :]).then_inc(bank_emptied[1], 1)

            moved(dve, "sigT")
            link(dve.tensor_reduce(clsum[:, 0:NCL], sigT[:, 0:NTILES].rearrange("p (c l) -> p c l", c=NCL), AX.X, ALU.add))
            link(dve.tensor_scalar(clsum[:, NCL:2 * NCL], clsum[:, 0:NCL], 0.0, None, ALU.is_lt))
            dve.scalar_tensor_tensor(out=sigT[:, NTILES:NSC], in0=clsum[:, 0:NCL], scalar=0.0, in1=clsum[:, NCL:2 * NCL],
                                     op0=ALU.is_gt, op1=ALU.subtract).then_inc(sigT_ready, 1)
            dve.wait_ge(ffn_in, 16 * 14)
            link(dve.tensor_scalar(temp[:, 0:1], temp[:, 0:1], 1e-6, None, ALU.add))
            link(dve.reciprocal(temp[:, 1:2], temp[:, 0:1]))
            link(dve.tensor_scalar(temp[:, 1:2], temp[:, 1:2], -1.0, None, ALU.mult))
            link(dve.tensor_tensor(dknots[:, 0:7], knots[:, 1:8], knots[:, 0:7], ALU.subtract))

            for q in quarters:
                filled(dve, f"sc{q}")
                dve.tensor_copy(sc[:, QT * q:QT * q + QT, :],
                                psum(f"sc{q}")[:, :].rearrange("p (a b) -> p a b", a=QT)[:, :, 0:NSC]).then_inc(bank_emptied[6], 1)
            filled(dve, "comp")
            dve.tensor_tensor(comp[:, :, :], psum("comp")[:, 0:2 * NT].rearrange("p (a b) -> p a b", b=2),
                              bc(cb2[:, :].unsqueeze(1), [P, NT, 2]), ALU.add).then_inc(bank_emptied[6], 1)
            moved(dve, "sc3")
            dve.tensor_copy(sel8[:, :, :], sc[:, :, NTILES:NSC]).then_inc(cal_in, 1)

            W = NT * 8
            rows = lambda i: small[:, i, :]
            r3 = lambda i: small[:, i, :].rearrange("p (a b) -> p a b", b=8)

            def calibrate(n):
                dve.wait_ge(cal_exp, n + 1)
                link(dve.tensor_scalar(rows(1), rows(0), 1.0, None, ALU.add))
                link(dve.reciprocal(rows(1), rows(1)))
                link(dve.tensor_scalar(rows(1), rows(1), float(NKNOT - 1), None, ALU.mult))
                ge = cal_a[:, :, :, :].rearrange("p t a b -> p (t a) b")
                hot = cal_b[:, :, :, :].rearrange("p t a b -> p (t a) b")
                part = cal_a[:, :, :, :].rearrange("p t a b -> p (t a) b")[:, :, 0:7]
                link(dve.tensor_tensor(ge, bc(rows(1).unsqueeze(2), [P, W, 8]), bc(K("thr").unsqueeze(1), [P, W, 8]), ALU.is_ge))
                link(dve.tensor_tensor(hot, ge[:, :, 0:7], ge[:, :, 1:8], ALU.subtract))
                link(dve.tensor_reduce(rows(2), ge[:, :, 1:7], AX.X, ALU.add))
                link(dve.tensor_tensor(rows(1), rows(1), rows(2), ALU.subtract))
                link(dve.tensor_tensor(part, hot, bc(dknots[:, 0:7].unsqueeze(1), [P, W, 7]), ALU.mult))
                link(dve.tensor_reduce(rows(2), part, AX.X, ALU.add))
                link(dve.tensor_tensor(part, hot, bc(knots[:, 0:7].unsqueeze(1), [P, W, 7]), ALU.mult))
                link(dve.tensor_reduce(rows(3), part, AX.X, ALU.add))
                link(dve.tensor_tensor(rows(1), rows(1), rows(2), ALU.mult))
                link(dve.tensor_tensor(gate8[:, :, :].rearrange("p a b -> p (a b)"), rows(1), rows(3), ALU.add))

            def first_max(out8, values):
                link(dve.tensor_reduce(row16[:, 0, :], values, AX.X, ALU.max))
                link(dve.tensor_tensor(r3(4), values, bc(row16[:, 0, :].unsqueeze(2), [P, NT, 8]), ALU.is_equal))
                link(dve.tensor_tensor(r3(4), r3(4), bc(K("rev").unsqueeze(1), [P, NT, 8]), ALU.mult))
                link(dve.tensor_reduce(row16[:, 0, :], r3(4), AX.X, ALU.max))
                return dve.tensor_tensor(out8, r3(4), bc(row16[:, 0, :].unsqueeze(2), [P, NT, 8]), ALU.is_equal)

            calibrate(0)
            link(first_max(ohc[:, :, :], gate8[:, :, :]))
            link(dve.tensor_tensor(cal_a[:, :, :, :], sc[:, :, 0:NTILES].rearrange("p t (c l) -> p t c l", c=NCL),
                                   bc(ohc[:, :, :].unsqueeze(3), [P, NT, NCL, TPC]), ALU.mult))
            dve.tensor_reduce(sel8[:, :, :], cal_a[:, :, :, :].rearrange("p t c l -> p t l c"), AX.X, ALU.add).then_inc(cal_in, 1)
            calibrate(1)
            link(first_max(ohl[:, :, :], gate8[:, :, :]))
            dve.tensor_tensor(onehot[:, :, :].rearrange("p t (c l) -> p t c l", c=NCL),
                              bc(ohc[:, :, :].unsqueeze(3), [P, NT, NCL, TPC]),
                              bc(ohl[:, :, :].unsqueeze(2), [P, NT, NCL, TPC]), ALU.mult).then_inc(onehot_ready, 1)
            for q in quarters:
                filled(dve, f"oneT{q}")
                dve.tensor_copy(oneT[:, QW * q:QW * q + QW], psum(f"oneT{q}")[0:NTILES, :]).then_inc(bank_emptied[0], 1)

            for i in (6, 7):
                moved(dve, f"pick{i}")
            dve.wait_ge(comp_ready, 1)
            col = lambda at: picked[:, :, at:at + GRID]
            dve.tensor_tensor(spl[:, 0], col(TW1), bc(comp[:, :, 0:1], [P, NT, GRID]), ALU.mult)
            link(dve.tensor_tensor(spl[:, 1], col(TW1 + GRID), bc(comp[:, :, 1:2], [P, NT, GRID]), ALU.mult))
            link(dve.tensor_tensor(spl[:, 0], spl[:, 0], spl[:, 1], ALU.add))
            link(dve.tensor_tensor(spl[:, 0], spl[:, 0], col(TB1), ALU.add))
            link(dve.scalar_tensor_tensor(out=spl[:, 1], in0=spl[:, 0], scalar=0.0, in1=col(TW2), op0=ALU.max, op1=ALU.mult))
            link(dve.tensor_reduce(row16[:, 1, :], spl[:, 1], AX.X, ALU.add))
            link(dve.tensor_tensor(row16[:, 1, :], row16[:, 1, :], picked[:, :, TB2], ALU.add))
            link(dve.tensor_scalar(row16[:, 1, :], row16[:, 1, :], oscale[:, 0:1], None, ALU.mult))
            dve.wait_ge(negent_ready, NQ)
            for b in range(NB):
                tr = range(TB * b, TB * b + TB)
                for t in tr:
                    ins = dve.scalar_tensor_tensor(out=y[:, t, :], in0=picked[:, t, TDIR:TABW], scalar=row16[:, 1, t:t + 1],
                                                   in1=xn[:, t, 0:D], op0=ALU.mult, op1=ALU.add)
                link(ins)
                n = tile_stats(y, tr)
                dve.wait_ge(rstd_ready, n)
                for t in tr:
                    ins = dve.tensor_scalar(y[:, t, :], y[:, t, :], mv[:, t, 0:1], rstd[:, t:t + 1], ALU.subtract, ALU.mult)
                ins.then_inc(yhat_ready, 1)

            dve.wait_ge(nexp_ready, 1)
            for b in range(NB):
                ts = slice(TB * b, TB * b + TB)
                for t in (TB * b + TB - 2, TB * b + TB - 1):
                    moved(dve, f"A{t}")
                link(dve.tensor_tensor(ratio[:, ts], s0[:, ts, D], nexp[:, ts], ALU.mult))
                link(dve.reciprocal(ratio[:, ts], ratio[:, ts]))
                link(dve.tensor_tensor(ratio[:, ts], ratio[:, ts], nexp[:, ts], ALU.mult))
                link(dve.tensor_tensor(s0[:, ts, 0:D], s0[:, ts, 0:D], bc(ratio[:, ts].unsqueeze(2), [P, TB, D]), ALU.mult))
                dve.wait_ge(silu_ready, b + 1)
                link(dve.tensor_tensor(s0[:, ts, 0:D], s0[:, ts, 0:D], y[:, ts, :], ALU.mult))
                dve.tensor_tensor(x[:, ts, :], x[:, ts, :], s0[:, ts, 0:D], ALU.add).then_inc(x2_ready, 1)
                dve.wait_ge(x2_ready, b + 1)
                n = tile_stats(x, range(TB * b, TB * b + TB))
                dve.wait_ge(rstd_ready, n)
                for t in range(TB * b, TB * b + TB):
                    ins = dve.tensor_scalar(xn2[:, t, :], x[:, t, :], mv[:, t, 0:1], rstd[:, t:t + 1], ALU.subtract, ALU.mult)
                ins.then_inc(xn2_ready, 1)

            filled(dve, "lg")
            dve.tensor_tensor(r3(2), psum("lg")[:, 0:W].rearrange("p (a b) -> p a b", b=NE),
                              bc(gate_b[:, :].unsqueeze(1), [P, NT, NE]), ALU.add).then_inc(bank_emptied[6], 1)
            moved(dve, "lg")
            link(dve.tensor_reduce(row16[:, 2, :], r3(2), AX.X, ALU.max))
            dve.tensor_tensor(r3(0), r3(2), bc(row16[:, 2, :].unsqueeze(2), [P, NT, NE]), ALU.subtract).then_inc(lg_ready, 1)
            dve.wait_ge(lg_ready, 1)
            first_max(ohc[:, :, :], r3(0)).then_inc(exp_mask_ready, 1)

            link(dve.memset(dtab, 0.0))
            link(dve.tensor_scalar(dtab, dtab, K("gamma_c"), None, ALU.add))
            link(dve.memset(dtab.rearrange("p (e c) -> p e c", c=CB)[:, :, 0:1], 0.0))

            def chunk_products(b):
                for k in range(2):
                    q = 2 * b + k
                    filled(dve, f"ktok{q}")
                    dve.tensor_tensor(kd[:, QT * k:QT * k + QT, :], psum(f"ktok{q}")[:, :].rearrange("p (a b) -> p a b", a=QT),
                                      bc(K("decay_k").unsqueeze(1), [P, QT, P]), ALU.mult).then_inc(bank_emptied[1], 1)
                for c in range(CT):
                    filled(dve, f"KV{b}.{c}")
                    dve.tensor_tensor(kvm.rearrange("p e (t c) -> p e t c", c=CT)[:, :, :, c],
                                      psum(f"KV{b}.{c}")[:, 0:C * TB].rearrange("p (t e) -> p e t", e=C),
                                      bc(K("mask_kv").unsqueeze(2), [P, C, TB]), ALU.mult).then_inc(bank_emptied[2 + c], 1)

            def chunk_states(b):
                for c in range(CT):
                    moved(dve, f"KV{b}.{c}")
                flat = lambda ap: ap.rearrange("p e c -> p (e c)")
                dve.tensor_tensor_scan(flat(state), dtab, flat(kvm), 0.0, ALU.mult, ALU.add).then_inc(state_ready, 1)

            def chunk_operands(q):
                filled(dve, f"QT{q}")
                if q >= 2:
                    filled(dve, f"y{q - 2}")
                dve.tensor_tensor(q_keep(q).rearrange("p (c i) -> p c i", c=CQ), psum(f"QT{q}")[:, :].rearrange("p (c i) -> p c i", c=CQ),
                                  bc(K("decay_q").unsqueeze(1), [P, CQ, C]), ALU.mult).then_inc(bank_emptied[0], 1)
                moved(dve, f"QT{q}")
                for i in range(QT):
                    name = f"vrep{q}.{i}"
                    filled(dve, name)
                    dve.tensor_tensor(vexp[q % 2][:, CT * i:CT * i + CT, :], psum(name)[:, :].rearrange("p (c a) -> p c a", c=CT),
                                      bc(K("mask_v").unsqueeze(1), [P, CT, P]), ALU.mult).then_inc(bank_emptied[turn[name][0]], 1)

            def chunk_decays(q):
                if q:
                    filled(dve, f"y{q - 1}")
                for k in range(QT):
                    name = f"R{q}.{k}"
                    filled(dve, name)
                    dve.tensor_tensor(smask[:, CT * k:CT * k + CT, :, :].rearrange("p c g i -> p c (g i)"),
                                      psum(name)[:, :].rearrange("p (c a) -> p c a", c=CT),
                                      bc(K("decay_s").unsqueeze(1), [P, CT, P]), ALU.mult).then_inc(bank_emptied[2 + k], 1)

            def dispatch_positions():
                filled(dve, "tot")
                dve.tensor_copy(rows(3).rearrange("p (e t) -> p e t", e=NE),
                                psum("tot")[:, 0:W].rearrange("p (t e) -> p e t", e=NE)).then_inc(bank_emptied[7], 1)
                moved(dve, "tot")
                link(dve.tensor_tensor_scan(rows(4), K("reset"), rows(3), 0.0, ALU.mult, ALU.add))
                link(dve.tensor_tensor(rows(5), rows(4), rows(3), ALU.subtract))
                filled(dve, "cum")
                dve.tensor_tensor(r3(2), psum("cum")[:, 0:W].rearrange("p (t e) -> p t e", e=NE),
                                  rows(5).rearrange("p (e t) -> p t e", e=NE), ALU.add).then_inc(bank_emptied[6], 1)
                moved(dve, "cum")
                link(dve.tensor_tensor(r3(2), r3(2), ohc[:, :, :], ALU.mult))
                link(dve.tensor_reduce(row16[:, 3, :], r3(2), AX.X, ALU.add))
                link(dve.tensor_tensor(r3(3), ohc[:, :, :], bc(K("slot0").unsqueeze(1), [P, NT, NE]), ALU.mult))
                link(dve.tensor_reduce(slotv[:, :], r3(3), AX.X, ALU.add))
                link(dve.tensor_tensor(slotv[:, :], slotv[:, :], row16[:, 3, :], ALU.add))
                link(dve.tensor_scalar(row16[:, 3, :], row16[:, 3, :], float(CAP), float(NOWHERE), ALU.is_gt, ALU.mult))
                link(dve.tensor_tensor(slotv[:, :], slotv[:, :], row16[:, 3, :], ALU.add))

            def slot_masks():
                for t in range(NT):
                    dve.tensor_scalar(slot_mask[:, t, :], K("iota"), slotv[:, t:t + 1], None, ALU.is_equal).then_inc(slotmask_ready, 1)
                dve.wait_ge(lgexp_ready, 1)
                link(dve.tensor_reduce(gpt[:, 0, :], r3(1), AX.X, ALU.add))
                link(dve.reciprocal(gpt[:, 0, :], gpt[:, 0, :]))
                dve.tensor_copy(info[:, :, 0:2], K("ids").rearrange("p (t k) -> p t k", k=2))
                dve.memset(info[:, :, 2:3], 1.0)
                link(dve.tensor_copy(info[:, :, 3], gpt[:, 0, :]))
                link(dve.tensor_tensor(gpt[:, 1, :], gpt[:, 0, :], info[:, :, 3], ALU.subtract))
                link(dve.tensor_copy(info[:, :, 4], gpt[:, 1, :]))
                link(dve.tensor_tensor(gpt[:, 2, :], gpt[:, 1, :], info[:, :, 4], ALU.subtract))
                dve.tensor_copy(info[:, :, 5], gpt[:, 2, :]).then_inc(info_ready, 1)

            def slot_indices():
                filled(dve, "idx")
                dve.tensor_copy(idx_f[:, :, :], psum("idx")[0:CAP, 0:8 * NE].rearrange("p (e k) -> p e k", e=NE)[:, :, 0:6])\
                    .then_inc(bank_emptied[6], 1)
                moved(dve, "idx")
                dve.tensor_tensor(idx_t[:, 0, :], idx_f[:, :, 0], idx_f[:, :, 1], ALU.add)
                dve.tensor_scalar(idx_t[:, 1, :], idx_f[:, :, 2], -1.0, 1.0, ALU.mult, ALU.add)
                link(dve.tensor_tensor(gprob[:, :], idx_f[:, :, 3], idx_f[:, :, 4], ALU.add))
                dve.tensor_tensor(gprob[:, :], gprob[:, :], idx_f[:, :, 5], ALU.add)
                dve.tensor_copy(idx_load[:, :], idx_t[:, 0, :])
                link(dve.tensor_tensor(idx_t[:, 2, :], idx_t[:, 1, :], K("oob", CAP), ALU.mult))
                dve.tensor_tensor(idx_store[:, :], idx_t[:, 2, :], idx_t[:, 0, :], ALU.add).then_inc(idx_ready, 1)

            def norm_begin(b):
                for q in (2 * b, 2 * b + 1):
                    moved(dve, f"y{q}")
                    ins = dve.bn_stats(gnst[:, q, :], yT[:, QW * q:QW * q + QW])
                link(ins)
                dve.bn_aggr(gns[:, b, 0:2], gnst[:, 2 * b:2 * b + 2, :].rearrange("p a b -> p (a b)")).then_inc(gn_mean, 1)

            def norm_middle(b):
                gv = lambda a, w=1: gns[:, b, a:a + w]
                filled(dve, f"gn{b}")
                dve.tensor_copy(gv(2, 2), psum(f"gn{b}")[:, 0:2]).then_inc(bank_emptied[turn[f"gn{b}"][0]], 1)
                moved(dve, f"gn{b}")
                link(dve.tensor_tensor(gv(8), gv(0), gv(2), ALU.subtract))
                dve.tensor_tensor(gv(4), gv(8), gv(8), ALU.mult).then_inc(gn_dev, 1)

            def norm_end(b):
                gv = lambda a, w=1: gns[:, b, a:a + w]
                filled(dve, f"gd{b}")
                dve.tensor_tensor(gv(5), psum(f"gd{b}")[:, 0:1], gv(3), ALU.add).then_inc(bank_emptied[turn[f"gd{b}"][0]], 1)
                moved(dve, f"gd{b}")
                n = variances(dve.tensor_copy(gv(9), gv(5)))
                dve.wait_ge(rstd_ready, n)
                link(dve.tensor_tensor(gv(7), gv(6), gnw[:, 0:1], ALU.mult))
                yb = yT[:, SEQ * b:SEQ * b + SEQ]
                link(dve.tensor_scalar(yb, yb, gv(2), gv(7), ALU.subtract, ALU.mult))
                dve.tensor_scalar(yb, yb, gnw[:, 1:2], None, ALU.add).then_inc(yn_ready, 1)

            def gather_copies():
                for h in range(2):
                    filled(dve, f"xgT{h}")
                    dve.tensor_copy(xgT[:, 4 * h:4 * h + 4, :], psum(f"xgT{h}")[:, 0:4 * CAP].rearrange("p (e c) -> p e c", e=4))\
                        .then_inc(bank_emptied[turn[f"xgT{h}"][0]], 1)

            def hidden_sum(e):
                name = f"h{e}"
                filled(dve, name)
                dve.tensor_tensor(hb[:, e % 4], psum(name)[:, 0:FT * CAP].rearrange("p (f c) -> p f c", f=FT),
                                  bc(b1T[:, FT * e:FT * e + FT].unsqueeze(2), [P, FT, CAP]), ALU.add)\
                    .then_inc(bank_emptied[turn[name][0]], 1)

            def expert_sum(h):
                es = slice(2 * h, 2 * h + 2)
                filled(dve, f"eo{h}")
                dve.tensor_tensor(eo[:, es, :], psum(f"eo{h}")[0:CAP, 0:2 * D].rearrange("p (e d) -> p e d", e=2), b2r[:, es, :], ALU.add)\
                    .then_inc(bank_emptied[0], 1)
                moved(dve, f"eo{h}")
                ins = dve.tensor_tensor(eo[:, es, :], eo[:, es, :], bc(gprob[:, es].unsqueeze(2), [CAP, 2, D]), ALU.mult)
                if h == 3:
                    ins.then_inc(eo_ready, 1)
                else:
                    link(ins)

            def finish(q):
                ts = slice(QT * q, QT * q + QT)
                filled(dve, f"s2_{q}")
                dve.wait_ge(g_in[q], 16)
                dve.tensor_tensor(g_tok[:, ts, :], psum(f"s2_{q}")[:, :].rearrange("p (a b) -> p a b", a=QT), g_tok[:, ts, :], ALU.mult)\
                    .then_inc(bank_emptied[turn[f"s2_{q}"][0]], 1)
                moved(dve, f"s2_{q}")
                dve.tensor_tensor(x[:, ts, :], x[:, ts, :], g_tok[:, ts, :], ALU.add).then_inc(fin_ready, 1)

            chunk_products(0)
            chunk_states(0)
            dispatch_positions()
            chunk_operands(0)
            chunk_decays(0)
            chunk_operands(1)
            slot_masks()
            chunk_decays(1)
            slot_indices()
            chunk_products(1)
            chunk_operands(2)
            filled(dve, "y1")
            chunk_states(1)
            gather_copies()
            chunk_decays(2)
            norm_begin(0)
            for e in range(4):
                hidden_sum(e)
            norm_middle(0)
            for e in range(4, NE):
                if e == 4:
                    norm_end(0)
                    expert_sum(0)
                    expert_sum(1)
                hidden_sum(e)
            chunk_operands(3)
            expert_sum(2)
            expert_sum(3)
            chunk_decays(3)
            norm_begin(1)
            norm_middle(1)
            norm_end(1)
            for q in quarters:
                finish(q)


def constants():
    import numpy as np
    p = np.arange(P)
    gamma = 1.0 - 2.0 ** (-5.0 - np.arange(H))
    c = {k: np.zeros((P, w)) for k, (_, w) in CONST_COLS.items()}
    c["ident"][:] = np.eye(P)
    c["tri"][:] = p[:, None] <= p[None, :]
    c["ones"][:] = 1
    c["avg8"][:] = (p[:, None] // DH == p[None, :] // DH) / DH
    m, j, i = p // C, p % C, np.arange(C)
    for g in range(NG):
        c["decay_s"][:, C * g:C * g + C] = np.where(i[None, :] >= j[:, None], gamma[GH * g + m][:, None] ** -j[:, None], 0)
    c["mask_v"][:] = m[:, None] == (p[None, :] // DH) % GH
    c["mask_kv"][:] = (p[:, None] // DH) % GH == np.arange(C)[None, :] // DH
    c["mask_q"][:] = (p[:, None] // C) == np.arange(NG)[None, :]
    c["mask_k"][:] = (p[:, None] // DH) % GH == np.arange(GH)[None, :]
    c["decay_k"][:] = gamma[p // DH][None, :] ** (C - j)[:, None]
    c["decay_q"][:] = gamma[p // DH][:, None] ** i[None, :] / np.sqrt(DH)
    c["gamma_c"][:] = gamma[p // DH][:, None] ** C
    c["thr"][:] = [-1] + list(range(1, NKNOT - 1)) + [1e30]
    c["rev"][:] = np.arange(NE, 0, -1)
    c["slot0"][:] = CAP * np.arange(NE) - 1
    c["iota"][:] = np.arange(SLOTS)
    c["ids"][:, 0::2] = p[:, None]
    c["ids"][:, 1::2] = P * np.arange(NT)
    c["neghalf"][:] = -0.5
    c["oob"][:] = NOWHERE + p[:, None] * NE + np.arange(NE)
    c["reset"][:] = np.arange(NE * NT) % NT != 0
    for k in range(CT):
        c["repeat"][:, P * k:P * k + P] = p[:, None] == C * k + (p % C)[None, :]
    return np.concatenate([c[k] for k in CONST_COLS], axis=1).astype(np.float32)


_INS = ['L0_attn_x', 'L0_ffn_signatures_raw', 'L0_ffn_knot_values', 'L0_ffn_temperature', 'L0_ffn_compress_w1',
        'L0_ffn_compress_b1', 'L0_ffn_compress_w2', 'L0_ffn_compress_b2', 'L0_ffn_spline_w1', 'L0_ffn_spline_b1',
        'L0_ffn_spline_w2', 'L0_ffn_spline_b2', 'L0_ffn_directions', 'L0_ffn_norm_gamma', 'L0_ffn_norm_beta',
        'L0_ffn_output_scale', 'L1_attn_W_q', 'L1_attn_W_k', 'L1_attn_W_v', 'L1_attn_W_o', 'L1_attn_gn_weight',
        'L1_attn_gn_bias', 'L1_ffn_gate_w', 'L1_ffn_gate_b', 'L1_ffn_w1', 'L1_ffn_b1', 'L1_ffn_w2', 'L1_ffn_b2']


def kernel(**inputs):
    import numpy as _np
    import concourse.bacc as _bacc
    from concourse import mybir as _mybir
    from concourse.bass_utils import run_bass_kernel_spmd as _run

    nc = _bacc.Bacc("TRN2", target_bir_lowering=False, num_devices=1)
    arrays, args = {}, []
    for name in _INS:
        a = _np.ascontiguousarray(inputs[name])
        arrays[f"in_{name}"] = a
        args.append(nc.dram_tensor(f"in_{name}", a.shape, _mybir.dt.from_np(a.dtype), kind="ExternalInput").ap())
    a = constants()
    arrays["in_consts"] = a
    args.append(nc.dram_tensor("in_consts", a.shape, _mybir.dt.from_np(a.dtype), kind="ExternalInput").ap())
    args.append(nc.dram_tensor("out_0", (NB, SEQ, D), F32, kind="ExternalOutput").ap())
    kernel_program(nc, *args)
    r = _run(nc, [arrays], core_ids=[0])
    return r.results[0]["out_0"]
```

```python
from contextlib import ExitStack

import concourse.bass as bass
from concourse import mybir

F32 = mybir.dt.float32
BF16 = mybir.dt.bfloat16
F16 = mybir.dt.float16
U32 = mybir.dt.uint32
ALU = mybir.AluOpType
ACT = mybir.ActivationFunctionType
AX = mybir.AxisListType

P = 128
D = 128
NB, SEQ = 2, 1024
N = NB * SEQ
NT = N // P
TB = SEQ // P
QT = 4
NQ = NT // QT
QW = QT * P
EPS = 1e-5
PSCALE = 2.0 ** 15

NTILES, TPC = 64, 8
NCL = NTILES // TPC
NKNOT = 8
COMP, GRID = 32, 16
NSC = NTILES + NCL
TW1, TB1, TW2, TB2, TDIR = 0, 2 * GRID, 3 * GRID, 4 * GRID, 4 * GRID + 1
TABW = TDIR + D

H, DH = 16, 8
C = 32
CT, CQ, CB = P // C, QW // C, SEQ // C
NG, GH = 4, 4

NE, CAP, F = 8, 80, 512
FT = F // P
SLOTS = NE * CAP
NOWHERE = 2 * N

CONST_COLS = {}


def _layout():
    at = 0
    for name, width in (("ident", P), ("tri", P), ("ones", P), ("avg8", P), ("decay_s", NG * C),
                        ("mask_v", P), ("mask_kv", C), ("mask_k", GH), ("mask_q", NG), ("decay_k", P), ("decay_q", C),
                        ("gamma_c", 1), ("thr", NKNOT), ("rev", NE), ("slot0", NE), ("iota", SLOTS),
                        ("ids", NT * 2), ("oob", NE), ("reset", NE * NT), ("repeat", CT * P)):
        CONST_COLS[name] = (at, width)
        at += width
    return at


CONST_W = _layout()


def kernel_program(nc, L0_attn_x, L0_ffn_signatures_raw, L0_ffn_knot_values, L0_ffn_temperature,
                   L0_ffn_compress_w1, L0_ffn_compress_b1, L0_ffn_compress_w2, L0_ffn_compress_b2,
                   L0_ffn_spline_w1, L0_ffn_spline_b1, L0_ffn_spline_w2, L0_ffn_spline_b2,
                   L0_ffn_directions, L0_ffn_norm_gamma, L0_ffn_norm_beta, L0_ffn_output_scale,
                   L1_attn_W_q, L1_attn_W_k, L1_attn_W_v, L1_attn_W_o, L1_attn_gn_weight, L1_attn_gn_bias,
                   L1_ffn_gate_w, L1_ffn_gate_b, L1_ffn_w1, L1_ffn_b1, L1_ffn_w2, L1_ffn_b2, consts, out):
    rows_xn2 = nc.dram_tensor("rows_xn2", (N, D), F32, kind="Internal").ap()
    rows_g = nc.dram_tensor("rows_g", (N, D), F32, kind="Internal").ap()
    out_rows = out.rearrange("b t d -> (b t) d")

    with ExitStack() as ctx:
        def sb(name, shape, dt=F32):
            return ctx.enter_context(nc.sbuf_tensor(name, shape, dt))

        def sem(name):
            return ctx.enter_context(nc.semaphore(name))

        bank = [ctx.enter_context(nc.psum_tensor(f"bank{i}", [P, 512], F32)) for i in range(8)]
        bank_filled = [sem(f"bank{i}_filled") for i in range(8)]
        bank_emptied = [sem(f"bank{i}_emptied") for i in range(8)]

        cst = sb("cst", [P, CONST_W])

        def K(name, parts=P):
            at, w = CONST_COLS[name]
            return cst[0:parts, at:at + w]

        x = sb("x", [P, NT, D])
        xn = sb("xn", [P, NT, D + 1])
        prob = sb("prob", [P, NT, D])
        xnT = sb("xnT", [P, N])
        pT = sb("pT", [P, N])
        ebuf = sb("ebuf", [P, 2, TB, QW])
        stats = sb("stats", [P, NT, 6])
        mv = sb("mv", [P, NT, 2])
        veps = sb("veps", [P, NT])
        rstd = sb("rstd", [P, NT])
        nmean = sb("nmean", [P, NT])
        sumexp = sb("sumexp", [P, NT])
        rsum = sb("rsum", [P, NT])
        lse = sb("lse", [P, NT])
        nlse = sb("nlse", [P, NT])
        negent = sb("negent", [P, NT])
        nexp = sb("nexp", [P, NT])
        s0 = sb("s0", [P, NT, D + 1])
        ratio = sb("ratio", [P, NT])
        sig = sb("sig", [NTILES, 3, D])
        sigT = sb("sigT", [P, NSC])
        clsum = sb("clsum", [P, 2 * NCL])
        sc = sb("sc", [P, NT, NSC])
        knots = sb("knots", [P, NKNOT])
        dknots = sb("dknots", [P, NKNOT])
        temp = sb("temp", [P, 2])
        cw1 = sb("cw1", [P, COMP])
        cb1 = sb("cb1", [COMP, 1])
        cw2 = sb("cw2", [COMP, 2])
        cb2 = sb("cb2", [P, 2])
        hT_room = sb("hT_room", [P, N])
        hT = hT_room[0:COMP, :]
        comp = sb("comp", [P, NT, 2])
        table = sb("table", [NTILES, TABW])
        gamma = sb("gamma", [P, D])
        beta = sb("beta", [P, D])
        oscale = sb("oscale", [P, 1])
        picked_room = sb("picked_room", [P, NT * SLOTS // 2])
        picked = picked_room[:, 0:NT * TABW].rearrange("p (t w) -> p t w", t=NT)
        oneT_room = sb("oneT_room", [P, N])
        oneT = oneT_room[0:NTILES, :]
        cal_b = oneT_room[:, 0:NT * 8 * 7].rearrange("p (t a b) -> p t a b", t=NT, a=8)
        onehot = sb("onehot", [P, NT, NTILES])
        sel8 = sb("sel8", [P, NT, 8])
        gate8 = sb("gate8", [P, NT, 8])
        ohc = sb("ohc", [P, NT, 8])
        ohl = sb("ohl", [P, NT, 8])
        cal_a = sb("cal_a", [P, NT, 8, 8])
        small = sb("small", [P, 6, NT * 8])
        row16 = sb("row16", [P, 4, NT])
        spl = sb("spl", [P, 2, NT, GRID])
        y = sb("y", [P, NT, D])
        xn2 = sb("xn2", [P, NT, D])
        wT = sb("wT", [P, 4, P])
        wraw = xn2[:, 0:4, :]
        gnw = sb("gnw", [P, 2])
        wkg = sb("wkg", [P, P + NE])
        gate_b = sb("gate_b", [P, NE])
        b1raw = sb("b1raw", [NE * FT, P])
        b1T = sb("b1T", [P, NE * FT])
        b2r = sb("b2r", [CAP, NE, D])
        slotv = sb("slotv", [P, NT])
        info = sb("info", [P, NT, 6], BF16)
        gpt = sb("gpt", [P, 3, NT])
        idx_f = sb("idx_f", [CAP, NE, 6])
        idx_t = sb("idx_t", [CAP, 3, NE])
        idx_load = sb("idx_load", [CAP, NE], U32)
        idx_store = sb("idx_store", [CAP, NE], U32)
        gprob = sb("gprob", [CAP, NE])
        neghalf = sb("neghalf", [P, NT])
        zeros = sb("zeros", [P, D])
        gns = sb("gns", [P, NB, 16])
        gnst = sb("gnst", [P, NQ, 6])

        xn2T = xnT
        w1 = sb("w1", [P, NE, F])
        w2 = sb("w2", [P, NE, FT, D])
        kexp = pT[:, :].rearrange("p (c a) -> p c a", c=CQ)
        qexp = ebuf[:, 0].rearrange("p a b -> p (a b)")[:, NG * QW:2 * NG * QW].rearrange("p (c a) -> p c a", c=CQ)
        vexp = [hT_room[:, :].rearrange("p (c a) -> p c a", c=CQ),
                xn[:, :, :].rearrange("p a b -> p (a b)")[:, 0:N].rearrange("p (c a) -> p c a", c=CQ)]
        smask = ebuf[:, 0].rearrange("p a b -> p (a b)")[:, 0:NG * QW].rearrange("p (c g i) -> p c g i", c=CQ, g=NG)
        moe_room = ebuf[:, 1].rearrange("p a b -> p (a b)")
        HB0, EO0 = NE * D + SLOTS, NE * D + SLOTS + 4 * FT * CAP
        xg = moe_room[0:CAP, 0:NE * D].rearrange("p (e d) -> p e d", e=NE)
        xgT = moe_room[:, NE * D:HB0].rearrange("p (e c) -> p e c", e=NE)
        hb = moe_room[:, HB0:EO0].rearrange("p (n f c) -> p n f c", n=4, f=FT)
        eo = moe_room[0:CAP, EO0:EO0 + NE * D].rearrange("p (e d) -> p e d", e=NE)

        def q_keep(q):
            return cal_a[:, :, :, :].rearrange("p a b c -> p (a b c)")[:, QW * (q % 2):QW * (q % 2) + QW]

        kd = [y[:, TB * b:TB * b + TB, :] for b in range(NB)]
        idxT = small[:, :, :].rearrange("p a b -> p (a b)")[0:6, 0:SLOTS]
        vtok = sc[:, :, :].rearrange("p a b -> p (a b)")[:, 0:TB * D].rearrange("p (t d) -> p t d", t=TB)
        kvm = prob[:, 0:TB, :].rearrange("p a b -> p (a b)").rearrange("p (e c) -> p e c", e=C)
        state = prob[:, TB:NT, :].rearrange("p a b -> p (a b)").rearrange("p (e c) -> p e c", e=C)
        dtab = s0[:, :, :].rearrange("p a b -> p (a b)")[:, 0:C * CB]
        yT = oneT_room
        slot_mask = picked_room[:, :].bitcast(BF16).rearrange("p (t s) -> p t s", t=NT)
        g_tok = picked_room[:, 0:NT * D].rearrange("p (t d) -> p t d", t=NT)

        parts = w1[:, :, :].rearrange("p e f -> p (e f)").bitcast(F16).rearrange("p (k n) -> p k n", k=4)
        xn_hi, xn_lo, p_hi, p_lo = (parts[:, k, :] for k in range(4))

        ident_in = sem("ident_in")
        consts_in = sem("consts_in")
        x_in = [sem(f"x_in{q}") for q in range(NQ)]
        sig_in = sem("sig_in")
        hidden_in = sem("hidden_in")
        ffn_in = sem("ffn_in")
        w_in = sem("w_in")
        moe_in = sem("moe_in")
        dve_step = sem("dve_step")
        pool_step = sem("pool_step")
        var_ready = sem("var_ready")
        rstd_ready = sem("rstd_ready")
        xn_ready = sem("xn_ready")
        exp_ready = sem("exp_ready")
        rsum_ready = sem("rsum_ready")
        lse_ready = sem("lse_ready")
        nlse_ready = sem("nlse_ready")
        p_ready = sem("p_ready")
        negent_ready = sem("negent_ready")
        nexp_ready = sem("nexp_ready")
        temp_in = sem("temp_in")
        temp_ready = sem("temp_ready")
        xn_split = sem("xn_split")
        p_split = sem("p_split")
        sig_ready = sem("sig_ready")
        sigT_ready = sem("sigT_ready")
        comp_ready = sem("comp_ready")
        cal_in = sem("cal_in")
        cal_exp = sem("cal_exp")
        onehot_ready = sem("onehot_ready")
        yhat_ready = sem("yhat_ready")
        yaff_ready = sem("yaff_ready")
        silu_ready = sem("silu_ready")
        x2_ready = sem("x2_ready")
        nmr_ready = sem("nmr_ready")
        xn2_ready = [sem(f"xn2_ready{q}") for q in range(NQ)]
        rows_stored = sem("rows_stored")
        zeros_ready = sem("zeros_ready")
        zeros_stored = sem("zeros_stored")
        qexp_ready = sem("qexp_ready")
        lg_ready = sem("lg_ready")
        lgexp_ready = sem("lgexp_ready")
        exp_mask_ready = sem("exp_mask_ready")
        wkg_ready = sem("wkg_ready")
        dtab_ready = sem("dtab_ready")
        slotmask_ready = sem("slotmask_ready")
        info_ready = sem("info_ready")
        idx_ready = sem("idx_ready")
        xg_in = sem("xg_in")
        state_ready = sem("state_ready")
        gn_mean = sem("gn_mean")
        gn_dev = sem("gn_dev")
        yn_ready = sem("yn_ready")
        g_stored = sem("g_stored")
        g_in = [sem(f"g_in{q}") for q in range(NQ)]
        h_ready = sem("h_ready")
        eo_ready = sem("eo_ready")
        silu2_ready = sem("silu2_ready")
        fin_ready = sem("fin_ready")
        out_stored = sem("out_stored")

        quarters = range(NQ)
        turns = {
            0: ["xnT0", "xnT2", "oneT0", "oneT2"] + [f"S1.{h}.{j}" for h in range(2) for j in (2, 6)] + ["xn2T0", "xn2T2", "QT0", "vrep0.1", "vrep0.3", "b1T", "QT1", "vrep1.1", "vrep1.3",
                "QT2", "vrep2.1", "vrep2.3", "QT3", "eo0", "eo1", "vrep3.1", "vrep3.3", "eo2", "eo3"],
            1: ["xnT1", "xnT3", "pT0", "pT2", "wT", "oneT1", "oneT3"] + [f"S1.{h}.{j}" for h in range(2) for j in (3, 7)] + ["xn2T1", "xn2T3", "KT0", "KT1", "vtok3", "KT2",
                "xgT0", "h0", "h2", "KT3", "h4", "h6", "s2_1"],
            6: ["sc0", "sc2", "h0_0", "h0_2", "comp"] + [f"pick{i}" for i in range(0, NT // 2, 2)]
               + ["ktok1.1", "vrep0.0", "vrep0.2", "cum", "vrep1.0", "vrep1.2", "idxT0", "idx", "vrep2.0", "vrep2.2", "xgT1", "h1", "h3", "gn0",
                  "vrep3.0", "vrep3.2", "h5", "h7", "s2_0"],
            7: ["sigT", "sc1", "sc3", "h0_1", "h0_3"] + [f"pick{i}" for i in range(1, NT // 2, 2)]
               + ["vtok0", "ktok1.0", "tot", "y0", "vtok2", "idxT1", "y1", "y2", "y3"],
        }
        extra = {2: ["ktok0.0", "ktok1.2"], 3: ["ktok0.1"], 4: ["vtok1"], 5: ["ktok0.2"]}
        last = {2: ["s2_2"], 3: ["s2_3.0"], 4: ["gn1", "s2_3.1"], 5: ["gd1"]}
        for i in range(NG):
            if i < 2:
                head = [f"S0.{h}.{j}" for h in range(2) for j in range(i, TB, 2)] + [f"S1.{h}.{j}" for h in range(2) for j in (i, i + 4)]
            else:
                head = [f"pT{2 * i - 3}"] + [f"A{t}" for t in range(i - 2, NT, 2)]
            turns[2 + i] = head + extra[2 + i] + [f"KV0.{i}", f"R0.{i}", f"R1.{i}", f"KV1.{i}", f"R2.{i}"] + (["gd0"] if i == 3 else []) + [f"R3.{i}"] + last[2 + i]
        turn = {name: (b, n) for b, names in turns.items() for n, name in enumerate(names)}
        in_order = {b: list(names) for b, names in turns.items()}

        def psum(name):
            return bank[turn[name][0]]

        def free(pe, name):
            b, n = turn[name]
            assert in_order[b].pop(0) == name, name
            if n:
                pe.wait_ge(bank_emptied[b], n)
            return bank[b]

        def filled(eng, name):
            b, n = turn[name]
            eng.wait_ge(bank_filled[b], n + 1)
            return bank[b]

        def moved(eng, name):
            b, n = turn[name]
            eng.wait_ge(bank_emptied[b], n + 1)

        block = ctx.enter_context(nc.Block())

        def bc(ap, shape):
            return ap.to_broadcast(shape)

        @block.sync
        def _(sp):
            i0, iw = CONST_COLS["ident"]
            xr = L0_attn_x.rearrange("b (t p) d -> p (b t) d", p=P)
            for q in range(NQ):
                sp.dma_start(x[:, QT * q:QT * q + QT, :], xr[:, QT * q:QT * q + QT, :]).then_inc(x_in[q], 16)
                if q == 0:
                    sp.dma_start(cst[:, i0:i0 + iw], consts[:, i0:i0 + iw]).then_inc(ident_in, 16)
            sp.dma_start(cst[:, iw:], consts[:, iw:]).then_inc(consts_in, 16)
            for dst, src in ((cw2[:, :], L0_ffn_compress_w2), (cb2[:, :], L0_ffn_compress_b2.partition_broadcast(P)),
                             (oscale[:, :], L0_ffn_output_scale.partition_broadcast(P)),
                             (gamma[:, :], L0_ffn_norm_gamma.partition_broadcast(P)),
                             (beta[:, :], L0_ffn_norm_beta.partition_broadcast(P)),
                             (table[:, TW1:TB1], L0_ffn_spline_w1.rearrange("t i g -> t (i g)")),
                             (table[:, TB1:TW2], L0_ffn_spline_b1),
                             (table[:, TW2:TB2], L0_ffn_spline_w2.rearrange("t g o -> t (g o)")),
                             (table[:, TB2:TDIR], L0_ffn_spline_b2),
                             (table[:, TDIR:TABW], L0_ffn_directions)):
                sp.dma_start(dst, src).then_inc(ffn_in, 16)
            for j, w in enumerate((L1_attn_W_q, L1_attn_W_k, L1_attn_W_v, L1_attn_W_o)):
                sp.dma_start(wraw[:, j, :], w).then_inc(w_in, 16)
            sp.dma_start(gnw[:, 0:1], L1_attn_gn_weight.unsqueeze(1)).then_inc(w_in, 16)
            sp.dma_start(gnw[:, 1:2], L1_attn_gn_bias.unsqueeze(1)).then_inc(w_in, 16)
            sp.dma_start(wkg[:, P:P + NE], L1_ffn_gate_w).then_inc(w_in, 16)
            sp.dma_start(gate_b[:, :], L1_ffn_gate_b.partition_broadcast(P)).then_inc(w_in, 16)
            sp.dma_start(b1raw[:, :], L1_ffn_b1.rearrange("e (f p) -> (e f) p", p=P)).then_inc(w_in, 16)
            sp.dma_start(b2r[:, :, :], L1_ffn_b2.partition_broadcast(CAP)).then_inc(moe_in, 16)
            sp.dma_start(w2[:, :, :, :], L1_ffn_w2.rearrange("e (f p) d -> p e f d", p=P)).then_inc(moe_in, 16)
            sp.wait_ge(zeros_ready, 1)
            sp.dma_start(rows_g.rearrange("(t p) d -> p t d", p=P), bc(zeros[:, :].unsqueeze(1), [P, NT, D])).then_inc(zeros_stored, 16)
            for j in (TB - 2, TB - 1):
                filled(sp, f"S{NB - 1}.1.{j}")
            sp.dma_start(w1[:, :, :], L1_ffn_w1.rearrange("e d f -> d e f")).then_inc(moe_in, 16)
            rows = rows_xn2.rearrange("(t p) w -> p t w", p=P)
            for q in range(NQ):
                ts = slice(QT * q, QT * q + QT)
                sp.wait_ge(xn2_ready[q], 1)
                sp.dma_start(rows[:, ts, :], xn2[:, ts, :]).then_inc(rows_stored, 16)
            sp.wait_ge(g_stored, 16 * NE)
            growv = rows_g.rearrange("(t p) d -> p t d", p=P)
            for q in range(NQ):
                sp.dma_start(g_tok[:, QT * q:QT * q + QT, :], growv[:, QT * q:QT * q + QT, :]).then_inc(g_in[q], 16)
            outr = out_rows.rearrange("(t p) d -> p t d", p=P)
            at = 0
            for n, tiles in enumerate([QT] * (NQ - 1) + [QT // 2] * 2):
                sp.wait_ge(fin_ready, n + 1)
                sp.dma_start(outr[:, at:at + tiles, :], x[:, at:at + tiles, :]).then_inc(out_stored, 16)
                at += tiles
            sp.wait_ge(rows_stored, 16 * NQ)
            sp.wait_ge(zeros_stored, 16)
            sp.wait_ge(out_stored, 16 * (NQ + 1))

        @block.gpsimd
        def _(pool):
            n_step = [0]

            def link(ins):
                n_step[0] += 1
                ins.then_inc(pool_step, 1)
                pool.wait_ge(pool_step, n_step[0])

            uses = [0]

            def inv_sqrt(out_ap, var_ap, n, parts=P):
                uses[0] += 1
                pool.wait_ge(var_ready, uses[0])
                link(pool.tensor_scalar(veps[0:parts, 0:n], var_ap, EPS, None, ALU.add))
                pool.tensor_tensor(out_ap, veps[0:parts, 0:n], neghalf[0:parts, 0:n], ALU.pow).then_inc(rstd_ready, 1)
                pool.wait_ge(rstd_ready, uses[0])

            link(pool.memset(neghalf[:, :], -0.5))
            pool.memset(xn[:, :, D:D + 1], 1.0).then_inc(xn_ready, 1)
            pool.memset(zeros[:, :], 0.0).then_inc(zeros_ready, 1)
            for q in range(NQ):
                ts = slice(QT * q, QT * q + QT)
                inv_sqrt(rstd[:, ts], mv[:, ts, 1], QT)
            for q in range(NQ):
                ts = slice(QT * q, QT * q + QT)
                pool.wait_ge(rsum_ready, q + 1)
                pool.tensor_tensor(prob[:, ts, :], prob[:, ts, :], bc(rsum[:, ts].unsqueeze(2), [P, QT, D]), ALU.mult).then_inc(p_ready, 1)

            def split(hi, lo, whole, ready):
                pool.tensor_copy(hi, whole).then_inc(ready, 1)
                pool.wait_ge(ready, 2 * n_split[ready.name] + 1)
                pool.tensor_tensor(lo, whole, hi, ALU.subtract).then_inc(ready, 1)
                n_split[ready.name] += 1

            n_split = {xn_split.name: 0, p_split.name: 0}
            cols = lambda q: slice(QW * q, QW * q + QW)
            for q in range(NQ):
                moved(pool, f"xnT{q}")
                split(xn_hi[:, cols(q)], xn_lo[:, cols(q)], xnT[:, cols(q)], xn_split)
                if q:
                    moved(pool, f"pT{q}")
                    split(p_hi[:, cols(q)], p_lo[:, cols(q)], pT[:, cols(q)], p_split)
            for b in range(NB):
                ts = slice(TB * b, TB * b + TB)
                inv_sqrt(rstd[:, ts], mv[:, ts, 1], TB)
                pool.wait_ge(yhat_ready, b + 1)
                link(pool.tensor_tensor(y[:, ts, :], y[:, ts, :], bc(gamma[:, :].unsqueeze(1), [P, TB, D]), ALU.mult))
                pool.tensor_tensor(y[:, ts, :], y[:, ts, :], bc(beta[:, :].unsqueeze(1), [P, TB, D]), ALU.add)\
                    .then_inc(yaff_ready, 1)
            for q in range(NQ):
                ts = slice(QT * q, QT * q + QT)
                inv_sqrt(rstd[:, ts], mv[:, ts, 1], QT)
                if q < 2:
                    pool.tensor_tensor(nmean[:, ts], nmean[:, ts], rstd[:, ts], ALU.mult).then_inc(nmr_ready, 1)
            pool.wait_ge(consts_in, 16)
            pool.wait_ge(x2_ready, 2)
            link(pool.memset(dtab, 0.0))
            link(pool.tensor_scalar(dtab, dtab, K("gamma_c"), None, ALU.add))
            pool.memset(dtab.rearrange("p (e c) -> p e c", c=CB)[:, :, 0:1], 0.0).then_inc(dtab_ready, 1)
            pool.wait_ge(idx_ready, 1)
            pool.wait_ge(rows_stored, 16 * NQ)
            for e in range(NE):
                pool.indirect_dma_start(xg[:, e, :], None, rows_xn2, bass.IndirectOffsetOnAxis(ap=idx_load[:, e:e + 1], axis=0))\
                    .then_inc(xg_in, 16)
            pool.wait_ge(zeros_stored, 16)
            for h in range(2):
                pool.wait_ge(silu2_ready, h + 1)
                for e in range(4 * h, 4 * h + 4):
                    pool.indirect_dma_start(rows_g, bass.IndirectOffsetOnAxis(ap=idx_store[:, e:e + 1], axis=0),
                                            eo[:, e, :], None, bounds_check=N - 1, oob_is_err=False).then_inc(g_stored, 16)
                if h == 0:
                    inv_sqrt(gns[:, 0, 6:7], gns[:, 0, 5:6], 1)
            inv_sqrt(gns[:, 1, 6:7], gns[:, 1, 5:6], 1)

        @block.scalar
        def _(act):
            act.dma_start(sig[:, 0, :], L0_ffn_signatures_raw).then_inc(sig_in, 16)
            act.dma_start(temp[:, 0:1], L0_ffn_temperature.partition_broadcast(P)).then_inc(temp_in, 16)
            act.dma_start(knots[:, :], L0_ffn_knot_values.partition_broadcast(P)).then_inc(temp_in, 16)
            act.dma_start(cw1[:, :], L0_ffn_compress_w1).then_inc(hidden_in, 16)
            act.dma_start(cb1[:, :], L0_ffn_compress_b1.unsqueeze(1)).then_inc(hidden_in, 16)
            act.preload_act_table(ACT.Exp)
            for q in range(NQ):
                ts = slice(QT * q, QT * q + QT)
                act.wait_ge(xn_ready, q + 2)
                act.activation(prob[:, ts, :], xn[:, ts, 0:D], ACT.Exp).then_inc(exp_ready, 1)
                filled(act, f"xnT{q}")
                act.activation(xnT[:, QW * q:QW * q + QW], psum(f"xnT{q}")[:, :], ACT.Copy).then_inc(bank_emptied[turn[f"xnT{q}"][0]], 1)
            for q in range(NQ):
                filled(act, f"sc{q}")
                act.activation(sc[:, QT * q:QT * q + QT, :], psum(f"sc{q}")[:, :].rearrange("p (a b) -> p a b", a=QT)[:, :, 0:NSC],
                               ACT.Copy).then_inc(bank_emptied[turn[f"sc{q}"][0]], 1)
            act.wait_ge(temp_ready, 1)
            moved(act, "sc3")
            act.activation(small[:, 0, :].rearrange("p (a b) -> p a b", b=8), sc[:, :, NTILES:NSC], ACT.Exp,
                           scale=temp[:, 1:2]).then_inc(cal_exp, 1)

            act.wait_ge(rsum_ready, NQ)
            act.activation(lse[:, :], sumexp[:, :], ACT.Ln).then_inc(lse_ready, 1)
            act.wait_ge(lse_ready, 1)
            act.activation(nlse[:, :], lse[:, :], ACT.Copy, scale=-1.0).then_inc(nlse_ready, 1)
            act.wait_ge(nlse_ready, 1)

            def hidden_gelu0(q):
                filled(act, f"h0_{q}")
                act.activation(hT[:, QW * q:QW * q + QW], psum(f"h0_{q}")[0:COMP, :], ACT.Gelu, bias=cb1[:, 0:1])\
                    .then_inc(bank_emptied[turn[f"h0_{q}"][0]], 1)

            def probability_copy(q):
                filled(act, f"pT{q}")
                act.activation(pT[:, QW * q:QW * q + QW], psum(f"pT{q}")[:, :], ACT.Copy, scale=PSCALE).then_inc(bank_emptied[turn[f"pT{q}"][0]], 1)

            act.wait_ge(hidden_in, 16 * 2)
            hidden_gelu0(0)
            hidden_gelu0(1)
            probability_copy(0)
            probability_copy(1)
            hidden_gelu0(2)
            hidden_gelu0(3)

            def attention_exps(b, h):
                half = 2 * b + h
                if half >= 2:
                    filled(act, f"A{QT * (half - 1) - 1}")
                for j in range(TB):
                    filled(act, f"S{b}.{h}.{j}")
                    act.activation(ebuf[:, half % 2, j, :], psum(f"S{b}.{h}.{j}")[:, :], ACT.Exp,
                                   bias=nlse[:, TB * b + j:TB * b + j + 1], scale=1.0 / PSCALE).then_inc(bank_emptied[turn[f"S{b}.{h}.{j}"][0]], 1)

            def attention_copy(h, tiles=range(QT)):
                for i in tiles:
                    t = QT * h + i
                    filled(act, f"A{t}")
                    act.activation(s0[:, t, :], psum(f"A{t}")[:, 0:D + 1], ACT.Copy).then_inc(bank_emptied[4 + t % 2], 1)

            def ffn_silu(b):
                act.wait_ge(yaff_ready, b + 1)
                ts = slice(TB * b, TB * b + TB)
                act.activation(y[:, ts, :], y[:, ts, :], ACT.Silu).then_inc(silu_ready, 1)

            attention_exps(0, 0)
            probability_copy(2)
            probability_copy(3)
            act.wait_ge(cal_in, 1)
            act.activation(small[:, 0, :], sel8[:, :, :].rearrange("p a b -> p (a b)"), ACT.Exp, scale=temp[:, 1:2]).then_inc(cal_exp, 1)
            filled(act, "wT")
            act.activation(wT[:, :, :].rearrange("p a b -> p (a b)"), psum("wT")[:, :], ACT.Copy).then_inc(bank_emptied[1], 1)
            moved(act, "wT")
            act.activation(wkg[:, 0:P], wT[:, 1, :], ACT.Copy).then_inc(wkg_ready, 1)
            attention_copy(0)
            attention_exps(0, 1)
            moved(act, "comp")
            cflat = comp[:, :, :].rearrange("p a b -> p (a b)")
            act.activation(cflat, cflat, ACT.Tanh).then_inc(comp_ready, 1)
            for i in range(8):
                filled(act, f"pick{i}")
                act.activation(picked[:, 2 * i:2 * i + 2, :], psum(f"pick{i}")[:, 0:2 * TABW].rearrange("p (a b) -> p a b", a=2),
                               ACT.Copy).then_inc(bank_emptied[turn[f"pick{i}"][0]], 1)
            act.wait_ge(negent_ready, 1)
            act.activation(nexp[:, :], negent[:, :], ACT.Exp, scale=-1.0).then_inc(nexp_ready, 1)
            attention_copy(1)
            attention_exps(1, 0)
            attention_exps(1, 1)
            ffn_silu(0)
            def normalize2(q):
                act.wait_ge(nmr_ready, q + 1)
                for t in range(QT * q, QT * q + QT):
                    ins = act.activation(xn2[:, t, :], x[:, t, :], ACT.Identity, bias=nmean[:, t:t + 1], scale=rstd[:, t:t + 1])
                ins.then_inc(xn2_ready[q], 1)

            attention_copy(2)
            ffn_silu(1)
            normalize2(0)
            attention_copy(3, range(2))
            normalize2(1)
            attention_copy(3, range(2, QT))
            def transposed_copy(q):
                filled(act, f"xn2T{q}")
                act.activation(xn2T[:, QW * q:QW * q + QW], psum(f"xn2T{q}")[:, :], ACT.Copy).then_inc(bank_emptied[turn[f"xn2T{q}"][0]], 1)

            def output_copy(q):
                filled(act, f"y{q}")
                act.activation(yT[:, QW * q:QW * q + QW], psum(f"y{q}")[:, :], ACT.Copy).then_inc(bank_emptied[7], 1)

            def value_copies(b):
                for k in range(2):
                    q = 2 * b + k
                    filled(act, f"vtok{q}")
                    act.activation(vtok[:, QT * k:QT * k + QT, :], psum(f"vtok{q}")[:, :].rearrange("p (a b) -> p a b", a=QT),
                                   ACT.Copy).then_inc(bank_emptied[turn[f"vtok{q}"][0]], 1)

            def spread(q):
                filled(act, f"KT{q}")
                if q:
                    filled(act, f"R{q - 1}.{NG - 1}")
                for m in range(GH):
                    ins = act.activation(kexp[:, :, C * m:C * m + C], psum(f"KT{q}")[:, :].rearrange("p (c j) -> p c j", c=CQ),
                                         ACT.Copy, scale=K("mask_k")[:, m:m + 1])
                ins.then_inc(bank_emptied[1], 1)
                moved(act, f"QT{q}")
                for g in range(NG):
                    ins = act.activation(qexp[:, :, C * g:C * g + C], q_keep(q).rearrange("p (c i) -> p c i", c=CQ),
                                         ACT.Copy, scale=K("mask_q")[:, g:g + 1])
                ins.then_inc(qexp_ready, 1)

            def expert_silu(h):
                act.wait_ge(eo_ready, h + 1)
                ev = eo[:, 4 * h:4 * h + 4, :].rearrange("p e d -> p (e d)")
                act.activation(ev, ev, ACT.Silu).then_inc(silu2_ready, 1)

            def hidden_gelu(e):
                moved(act, f"h{e}")
                hv = hb[:, e % 4].rearrange("p f c -> p (f c)")
                act.activation(hv, hv, ACT.Gelu_apprx_tanh).then_inc(h_ready, 1)

            transposed_copy(0)
            transposed_copy(1)
            value_copies(0)
            transposed_copy(2)
            transposed_copy(3)
            act.wait_ge(lg_ready, 1)
            act.activation(small[:, 1, :], small[:, 0, :], ACT.Exp).then_inc(lgexp_ready, 1)
            spread(0)
            filled(act, "b1T")
            act.activation(b1T[:, :], psum("b1T")[:, 0:NE * FT], ACT.Copy).then_inc(bank_emptied[0], 1)
            spread(1)
            output_copy(0)
            value_copies(1)
            for h in range(2):
                filled(act, f"idxT{h}")
                act.activation(idxT[:, SLOTS // 2 * h:SLOTS // 2 * h + SLOTS // 2], psum(f"idxT{h}")[0:6, 0:SLOTS // 2], ACT.Copy)\
                    .then_inc(bank_emptied[turn[f"idxT{h}"][0]], 1)
            spread(2)
            output_copy(1)
            for e in range(4):
                hidden_gelu(e)
            spread(3)
            expert_silu(0)
            for e in range(4, NE):
                hidden_gelu(e)
            output_copy(2)
            expert_silu(1)
            output_copy(3)

        @block.tensor
        def _(pe):
            idt = K("ident")
            pe.wait_ge(ident_in, 16)

            def done(ins, name):
                ins.then_inc(bank_filled[turn[name][0]], 1)

            def transposes(name, srcs, rows=P):
                out_bank = free(pe, name)
                for i, src in enumerate(srcs):
                    ins = pe.transpose(out_bank[0:src.shape[1], P * i:P * i + src.shape[0]], src, idt[0:src.shape[0], 0:src.shape[0]])
                done(ins, name)

            pe.wait_ge(sig_ready, 1)
            transposes("sigT", [sig[:, 2, :]])

            def signature_scores(q):
                moved(pe, f"xnT{q}")
                ob = free(pe, f"sc{q}")
                for i in range(QT):
                    t = QT * q + i
                    ins = pe.matmul(ob[:, P * i:P * i + NSC], xnT[:, P * t:P * t + P], sigT[:, :], start=True, stop=True)
                done(ins, f"sc{q}")

            for q in range(NQ):
                pe.wait_ge(xn_ready, q + 2)
                transposes(f"xnT{q}", [xn[:, QT * q + i, 0:D] for i in range(QT)])
                if q == 1:
                    pe.wait_ge(sigT_ready, 1)
                if q:
                    signature_scores(q - 1)
            signature_scores(NQ - 1)
            def probabilities(q):
                pe.wait_ge(p_ready, q + 1)
                transposes(f"pT{q}", [prob[:, QT * q + i, :] for i in range(QT)])

            def hidden(q):
                ob = free(pe, f"h0_{q}")
                done(pe.matmul(ob[0:COMP, :], cw1[:, :], xnT[:, QW * q:QW * q + QW], start=True, stop=True), f"h0_{q}")

            def component(t):
                ob = free(pe, "comp") if t == 0 else psum("comp")
                if t % QT == 0:
                    moved(pe, f"h0_{t // QT}")
                ins = pe.matmul(ob[:, 2 * t:2 * t + 2], hT[:, P * t:P * t + P], cw2[:, :], start=True, stop=True)
                if t == NT - 1:
                    done(ins, "comp")

            def scores(b, h, between=None):
                for j in range(TB):
                    name = f"S{b}.{h}.{j}"
                    ob = free(pe, name)
                    keys = slice(P * (TB * b + j), P * (TB * b + j) + P)
                    queries = slice(SEQ * b + QW * h, SEQ * b + QW * h + QW)
                    if (b, h) == (0, 0):
                        done(pe.matmul(ob[:, :], xnT[:, keys], pT[:, queries], start=True, stop=True), name)
                    else:
                        if j == 0:
                            pe.wait_ge(xn_split, 2 * 2 * (b + 1))
                            pe.wait_ge(p_split, 2 * (2 * b + h))
                        pe.matmul(ob[:, :], xn_hi[:, keys], p_lo[:, queries], start=True, stop=False)
                        pe.matmul(ob[:, :], xn_hi[:, keys], p_hi[:, queries], start=False, stop=False)
                        done(pe.matmul(ob[:, :], xn_lo[:, keys], p_hi[:, queries], start=False, stop=True), name)
                    if between:
                        between(j)

            def values(b, h):
                half = 2 * b + h
                for i in range(QT):
                    t = QT * half + i
                    ob = free(pe, f"A{t}")
                    for j in range(TB):
                        if i == 0:
                            moved(pe, f"S{b}.{h}.{j}")
                        ins = pe.matmul(ob[:, 0:D + 1], ebuf[:, half % 2, j, P * i:P * i + P], xn[:, TB * b + j, :],
                                        start=(j == 0), stop=(j == TB - 1))
                    done(ins, f"A{t}")

            def pick_rows():
                pe.wait_ge(onehot_ready, 1)
                for q in range(NQ):
                    transposes(f"oneT{q}", [onehot[:, QT * q + i, :] for i in range(QT)])
                for i in range(NT // 2):
                    name = f"pick{i}"
                    ob = free(pe, name)
                    moved(pe, f"oneT{2 * i // QT}")
                    for k in range(2):
                        t = 2 * i + k
                        ins = pe.matmul(ob[:, TABW * k:TABW * k + TABW], oneT[:, P * t:P * t + P], table[:, :], start=True, stop=True)
                    done(ins, name)

            pe.wait_ge(hidden_in, 16 * 2)
            hidden(0)
            hidden(1)
            probabilities(0)
            probabilities(1)
            hidden(2)
            hidden(3)
            moved(pe, "pT1")
            scores(0, 0)
            probabilities(2)
            probabilities(3)
            pe.wait_ge(w_in, 16 * 9)
            transposes("wT", [wraw[:, j, :] for j in range(4)])
            values(0, 0)
            pe.wait_ge(ffn_in, 16 * 10)

            def two_components(j):
                component(2 * j)
                component(2 * j + 1)

            scores(0, 1, two_components)
            pick_rows()
            values(0, 1)
            moved(pe, "pT3")
            scores(1, 0)
            scores(1, 1)
            values(1, 0)
            values(1, 1)

            def layer1_input(b):
                for q in (2 * b, 2 * b + 1):
                    pe.wait_ge(xn2_ready[q], 1)
                    transposes(f"xn2T{q}", [xn2[:, QT * q + i, :] for i in range(QT)])

            def token_product(name, q, w, i):
                if i == 0:
                    moved(pe, f"xn2T{q}")
                ob = free(pe, f"{name}{q}") if i == 0 else psum(f"{name}{q}")
                t = QT * q + i
                ins = pe.matmul(ob[:, P * i:P * i + P], xn2T[:, P * t:P * t + P], wT[:, w, :], start=True, stop=True)
                if i == QT - 1:
                    done(ins, f"{name}{q}")

            def keys_and_logits(b):
                if b == 0:
                    pe.wait_ge(wkg_ready, 1)
                for i in range(TB):
                    t = TB * b + i
                    if i % QT == 0:
                        moved(pe, f"xn2T{t // QT}")
                    name = f"ktok{b}.{i // 3}"
                    ob = free(pe, name) if i % 3 == 0 else psum(name)
                    at = (P + NE) * (i % 3)
                    ins = pe.matmul(ob[:, at:at + P + NE], xn2T[:, P * t:P * t + P], wkg[:, :], start=True, stop=True)
                    if i % 3 == 2 or i == TB - 1:
                        done(ins, name)

            def token_values(b, between=None):
                for q in (2 * b, 2 * b + 1):
                    for i in range(QT):
                        token_product("vtok", q, 2, i)
                        if between:
                            between(QT * (q % 2) + i)

            def chunk_product(b, c):
                for j in range(3):
                    moved(pe, f"ktok{b}.{j}")
                for k in range(2):
                    moved(pe, f"vtok{2 * b + k}")
                ob = free(pe, f"KV{b}.{c}")
                rows = slice(C * c, C * c + C)
                for t in range(TB):
                    for g in range(NG):
                        cols = slice(C * g, C * g + C)
                        ins = pe.matmul(ob[cols, C * t:C * t + C], kd[b][rows, t, cols], vtok[rows, t, cols],
                                        start=True, stop=True, tile_position=(C * c, C * g))
                done(ins, f"KV{b}.{c}")

            def chunk_keys_queries(q):
                for name, w in (("KT", 1), ("QT", 0)):
                    ob = free(pe, f"{name}{q}")
                    done(pe.matmul(ob[:, :], wkg[:, 0:P] if w == 1 else wT[:, w, :], xn2T[:, QW * q:QW * q + QW], start=True, stop=True), f"{name}{q}")

            def chunk_value(q, i):
                ob = free(pe, f"vrep{q}.{i}")
                for c in range(CT):
                    ins = pe.matmul(ob[:, P * c:P * c + P], K("repeat")[:, P * c:P * c + P],
                                    vtok[:, QT * (q % 2) + i, :], start=True, stop=True)
                done(ins, f"vrep{q}.{i}")

            def chunk_values(q):
                for i in range(QT):
                    chunk_value(q, i)

            def chunk_score(q, c):
                if c == 0:
                    moved(pe, f"KT{q}")
                    pe.wait_ge(qexp_ready, q + 1)
                name = f"R{q}.{c // CT}"
                ob = free(pe, name) if c % CT == 0 else psum(name)
                at = P * (c % CT)
                ins = pe.matmul(ob[:, at:at + P], kexp[:, c, :], qexp[:, c, :], start=True, stop=True)
                if c % CT == CT - 1:
                    done(ins, name)

            def tile_scores(q, k):
                for c in range(CT * k, CT * k + CT):
                    chunk_score(q, c)

            def tile_outputs(q, k):
                if k == 0:
                    moved(pe, f"vrep{q}.2")
                    moved(pe, f"vrep{q}.3")
                    pe.wait_ge(state_ready, q // 2 + 1)
                ob = free(pe, f"y{q}") if k == 0 else psum(f"y{q}")
                moved(pe, f"R{q}.{k}")
                for c in range(CT * k, CT * k + CT):
                    for g in range(NG):
                        rows = slice(C * g, C * g + C)
                        cb = CQ * (q % 2) + c
                        cols = slice(C * c, C * c + C)
                        ins = pe.matmul(ob[rows, cols], vexp[q % 2][:, c, rows], smask[:, c, g, :], start=True, stop=(cb == 0))
                        if cb:
                            ins = pe.matmul(ob[rows, cols], state[rows, :, cb - 1], q_keep(q)[rows, cols], start=False, stop=True,
                                            tile_position=(C * g, C * g))
                    if c == CQ - 1:
                        done(ins, f"y{q}")

            def outputs_and_scores(q):
                for k in range(QT):
                    tile_outputs(q, k)
                for k in range(QT):
                    tile_scores(q + 1, k)

            def count_experts():
                pe.wait_ge(exp_mask_ready, 1)
                m8 = ohc[:, :, :].rearrange("p a b -> p (a b)")
                ob = free(pe, "cum")
                done(pe.matmul(ob[:, 0:NT * NE], K("tri"), m8, start=True, stop=True), "cum")
                ob = free(pe, "tot")
                done(pe.matmul(ob[:, 0:NT * NE], K("ones"), m8, start=True, stop=True), "tot")

            def slot_tokens():
                pe.wait_ge(slotmask_ready, NT)
                pe.wait_ge(info_ready, 1)
                for h in range(2):
                    ob = free(pe, f"idxT{h}")
                    for t in range(NT):
                        ins = pe.matmul(ob[0:6, 0:SLOTS // 2], info[:, t, :], slot_mask[:, t, SLOTS // 2 * h:SLOTS // 2 * h + SLOTS // 2],
                                        start=(t == 0), stop=(t == NT - 1))
                    done(ins, f"idxT{h}")

            def slot_columns():
                ob = free(pe, "idx")
                for h in range(2):
                    moved(pe, f"idxT{h}")
                for e in range(NE):
                    ins = pe.transpose(ob[0:CAP, 8 * e:8 * e + 6], idxT[:, CAP * e:CAP * e + CAP], idt[0:6, 0:6])
                done(ins, "idx")

            def norm_sums(name, srcs, b):
                ob = free(pe, name)
                done(pe.matmul(ob[:, 0:srcs.shape[1]], K("avg8"), srcs, start=True, stop=True), name)

            def norm_means(b):
                pe.wait_ge(gn_mean, b + 1)
                norm_sums(f"gn{b}", gns[:, b, 0:2], b)

            def norm_devs(b):
                pe.wait_ge(gn_dev, b + 1)
                norm_sums(f"gd{b}", gns[:, b, 4:5], b)

            def slot_rows():
                pe.wait_ge(xg_in, 16 * NE)
                for h in range(2):
                    ob = free(pe, f"xgT{h}")
                    for k in range(4):
                        ins = pe.transpose(ob[:, CAP * k:CAP * k + CAP], xg[:, 4 * h + k, :], idt[0:CAP, 0:CAP])
                    done(ins, f"xgT{h}")
                pe.wait_ge(moe_in, 16 * 3)

            def expert_hidden(e):
                ob = free(pe, f"h{e}")
                moved(pe, f"xgT{e // 4}")
                for f in range(FT):
                    ins = pe.matmul(ob[:, CAP * f:CAP * f + CAP], w1[:, e, P * f:P * f + P], xgT[:, e, :], start=True, stop=True)
                done(ins, f"h{e}")

            def expert_out(e):
                name = f"eo{e // 2}"
                ob = free(pe, name) if e % 2 == 0 else psum(name)
                pe.wait_ge(h_ready, e + 1)
                for f in range(FT):
                    ins = pe.matmul(ob[0:CAP, D * (e % 2):D * (e % 2) + D], hb[:, e % 4, f, :], w2[:, e, f, :],
                                    start=(f == 0), stop=(f == FT - 1))
                if e % 2:
                    done(ins, name)

            def project(q, i):
                if i == 0:
                    pe.wait_ge(yn_ready, q + 1)
                name, first, final = (f"s2_{q}", 0, QT - 1) if q < NQ - 1 else (f"s2_{q}.{i // 2}", i // 2 * 2, i // 2 * 2 + 1)
                ob = free(pe, name) if i == first else psum(name)
                t = QT * q + i
                ins = pe.matmul(ob[:, P * i:P * i + P], yT[:, P * t:P * t + P], wT[:, 3, :], start=True, stop=True)
                if i == final:
                    done(ins, name)

            layer1_input(0)
            keys_and_logits(0)
            token_values(0)
            layer1_input(1)
            keys_and_logits(1)
            chunk_keys_queries(0)
            for c in range(CT):
                chunk_product(0, c)
                chunk_value(0, c)
            count_experts()
            transposes("b1T", [b1raw[:, :]])
            for k in range(QT):
                tile_scores(0, k)
            chunk_keys_queries(1)
            chunk_values(1)
            outputs_and_scores(0)
            token_values(1)
            slot_tokens()
            slot_columns()
            chunk_keys_queries(2)
            for c in range(CT):
                chunk_product(1, c)
                chunk_value(2, c)
            outputs_and_scores(1)
            slot_rows()
            for e in range(4):
                expert_hidden(e)
            chunk_keys_queries(3)
            for e in range(4):
                if e == 2:
                    norm_means(0)
                expert_out(e)
            chunk_values(3)
            for e in range(4, NE):
                expert_hidden(e)
            norm_devs(0)
            for k in range(QT):
                tile_outputs(2, k)
                expert_out(4 + k)
            for k in range(QT):
                tile_scores(3, k)
            for k in range(QT):
                tile_outputs(3, k)
            for q in (0, 1):
                for i in range(QT):
                    project(q, i)
            norm_means(1)
            norm_devs(1)
            for q in (2, 3):
                for i in range(QT):
                    project(q, i)
            assert not any(in_order.values())

        @block.vector
        def _(dve):
            n_step = [0]

            def link(ins):
                n_step[0] += 1
                ins.then_inc(dve_step, 1)
                dve.wait_ge(dve_step, n_step[0])

            n_var = [0]

            def variances(ins):
                n_var[0] += 1
                ins.then_inc(var_ready, 1)
                return n_var[0]

            def tile_stats(src, ts):
                for t in ts:
                    ins = dve.bn_stats(stats[:, t, :], src[:, t, 0:D])
                link(ins)
                for t in ts:
                    ins = dve.bn_aggr(mv[:, t, :], stats[:, t, :])
                return variances(ins)

            def normalize(q):
                dve.wait_ge(rstd_ready, q + 1)
                for t in range(QT * q, QT * q + QT):
                    ins = dve.tensor_scalar(xn[:, t, 0:D], x[:, t, :], mv[:, t, 0:1], rstd[:, t:t + 1], ALU.subtract, ALU.mult)
                ins.then_inc(xn_ready, 1)

            def quarter_stats(q):
                dve.wait_ge(x_in[q], 16)
                tile_stats(x, range(QT * q, QT * q + QT))

            quarter_stats(0)
            dve.wait_ge(sig_in, 16)
            raw = sig[:, 0, :]
            dve.tensor_scalar(sig[:, 1, :], raw, 0.3, None, ALU.is_gt)
            link(dve.tensor_scalar(sig[:, 2, :], raw, -0.3, None, ALU.is_lt))
            link(dve.tensor_tensor(sig[:, 1, :], sig[:, 1, :], sig[:, 2, :], ALU.subtract))
            link(dve.tensor_tensor(sig[:, 1, :], sig[:, 1, :], raw, ALU.subtract))
            dve.tensor_tensor(sig[:, 2, :], sig[:, 1, :], raw, ALU.add).then_inc(sig_ready, 1)
            quarter_stats(1)
            normalize(0)
            filled(dve, "sigT")
            dve.tensor_copy(sigT[:, 0:NTILES], psum("sigT")[:, 0:NTILES]).then_inc(bank_emptied[7], 1)
            moved(dve, "sigT")
            link(dve.tensor_reduce(clsum[:, 0:NCL], sigT[:, 0:NTILES].rearrange("p (c l) -> p c l", c=NCL), AX.X, ALU.add))
            link(dve.tensor_scalar(clsum[:, NCL:2 * NCL], clsum[:, 0:NCL], 0.0, None, ALU.is_lt))
            dve.scalar_tensor_tensor(out=sigT[:, NTILES:NSC], in0=clsum[:, 0:NCL], scalar=0.0, in1=clsum[:, NCL:2 * NCL],
                                     op0=ALU.is_gt, op1=ALU.subtract).then_inc(sigT_ready, 1)
            quarter_stats(2)
            normalize(1)
            quarter_stats(3)
            normalize(2)
            normalize(3)
            dve.wait_ge(temp_in, 16 * 2)
            link(dve.tensor_scalar(temp[:, 0:1], temp[:, 0:1], 1e-6, None, ALU.add))
            link(dve.reciprocal(temp[:, 1:2], temp[:, 0:1]))
            dve.tensor_scalar(temp[:, 1:2], temp[:, 1:2], -1.0, None, ALU.mult).then_inc(temp_ready, 1)
            link(dve.tensor_tensor(dknots[:, 0:7], knots[:, 1:8], knots[:, 0:7], ALU.subtract))
            for q in quarters:
                ts = slice(QT * q, QT * q + QT)
                dve.wait_ge(exp_ready, q + 1)
                link(dve.tensor_reduce(sumexp[:, ts], prob[:, ts, :], AX.X, ALU.add))
                dve.reciprocal(rsum[:, ts], sumexp[:, ts]).then_inc(rsum_ready, 1)

            W = NT * 8
            rows = lambda i: small[:, i, :]
            r3 = lambda i: small[:, i, :].rearrange("p (a b) -> p a b", b=8)

            def calibrate(n):
                dve.wait_ge(cal_exp, n + 1)
                dve.wait_ge(consts_in, 16)
                link(dve.tensor_scalar(rows(1), rows(0), 1.0, None, ALU.add))
                link(dve.reciprocal(rows(1), rows(1)))
                link(dve.tensor_scalar(rows(1), rows(1), float(NKNOT - 1), None, ALU.mult))
                ge = cal_a[:, :, :, :].rearrange("p t a b -> p (t a) b")
                hot = cal_b[:, :, :, :].rearrange("p t a b -> p (t a) b")
                part = cal_a[:, :, :, :].rearrange("p t a b -> p (t a) b")[:, :, 0:7]
                link(dve.tensor_tensor(ge, bc(rows(1).unsqueeze(2), [P, W, 8]), bc(K("thr").unsqueeze(1), [P, W, 8]), ALU.is_ge))
                link(dve.tensor_tensor(hot, ge[:, :, 0:7], ge[:, :, 1:8], ALU.subtract))
                link(dve.tensor_reduce(rows(2), ge[:, :, 1:7], AX.X, ALU.add))
                link(dve.tensor_tensor(rows(1), rows(1), rows(2), ALU.subtract))
                link(dve.tensor_tensor(part, hot, bc(dknots[:, 0:7].unsqueeze(1), [P, W, 7]), ALU.mult))
                link(dve.tensor_reduce(rows(2), part, AX.X, ALU.add))
                link(dve.tensor_tensor(part, hot, bc(knots[:, 0:7].unsqueeze(1), [P, W, 7]), ALU.mult))
                link(dve.tensor_reduce(rows(3), part, AX.X, ALU.add))
                link(dve.tensor_tensor(rows(1), rows(1), rows(2), ALU.mult))
                link(dve.tensor_tensor(gate8[:, :, :].rearrange("p a b -> p (a b)"), rows(1), rows(3), ALU.add))

            def first_max(out8, values):
                link(dve.tensor_reduce(row16[:, 0, :], values, AX.X, ALU.max))
                link(dve.tensor_tensor(r3(4), values, bc(row16[:, 0, :].unsqueeze(2), [P, NT, 8]), ALU.is_equal))
                link(dve.tensor_tensor(r3(4), r3(4), bc(K("rev").unsqueeze(1), [P, NT, 8]), ALU.mult))
                link(dve.tensor_reduce(row16[:, 0, :], r3(4), AX.X, ALU.max))
                return dve.tensor_tensor(out8, r3(4), bc(row16[:, 0, :].unsqueeze(2), [P, NT, 8]), ALU.is_equal)

            calibrate(0)
            link(first_max(ohc[:, :, :], gate8[:, :, :]))
            link(dve.tensor_tensor(cal_a[:, :, :, :], sc[:, :, 0:NTILES].rearrange("p t (c l) -> p t c l", c=NCL),
                                   bc(ohc[:, :, :].unsqueeze(3), [P, NT, NCL, TPC]), ALU.mult))
            dve.tensor_reduce(sel8[:, :, :], cal_a[:, :, :, :].rearrange("p t c l -> p t l c"), AX.X, ALU.add).then_inc(cal_in, 1)
            calibrate(1)
            link(first_max(ohl[:, :, :], gate8[:, :, :]))
            dve.tensor_tensor(onehot[:, :, :].rearrange("p t (c l) -> p t c l", c=NCL),
                              bc(ohc[:, :, :].unsqueeze(3), [P, NT, NCL, TPC]),
                              bc(ohl[:, :, :].unsqueeze(2), [P, NT, NCL, TPC]), ALU.mult).then_inc(onehot_ready, 1)
            filled(dve, "comp")
            dve.tensor_tensor(comp[:, :, :], psum("comp")[:, 0:2 * NT].rearrange("p (a b) -> p a b", b=2),
                              bc(cb2[:, :].unsqueeze(1), [P, NT, 2]), ALU.add).then_inc(bank_emptied[6], 1)
            for q in quarters:
                filled(dve, f"oneT{q}")
                dve.tensor_copy(oneT[:, QW * q:QW * q + QW], psum(f"oneT{q}")[0:NTILES, :]).then_inc(bank_emptied[q % 2], 1)

            dve.wait_ge(p_ready, NQ)
            dve.wait_ge(lse_ready, 1)
            for t in range(NT):
                ins = dve.scalar_tensor_tensor(out=xn2[:, t, :], in0=xn[:, t, 0:D], scalar=lse[:, t:t + 1], in1=prob[:, t, :],
                                               op0=ALU.subtract, op1=ALU.mult, accum_out=negent[:, t:t + 1])
            ins.then_inc(negent_ready, 1)

            for i in (6, 7):
                moved(dve, f"pick{i}")
            dve.wait_ge(comp_ready, 1)
            col = lambda at: picked[:, :, at:at + GRID]
            dve.tensor_tensor(spl[:, 0], col(TW1), bc(comp[:, :, 0:1], [P, NT, GRID]), ALU.mult)
            link(dve.tensor_tensor(spl[:, 1], col(TW1 + GRID), bc(comp[:, :, 1:2], [P, NT, GRID]), ALU.mult))
            link(dve.tensor_tensor(spl[:, 0], spl[:, 0], spl[:, 1], ALU.add))
            link(dve.tensor_tensor(spl[:, 0], spl[:, 0], col(TB1), ALU.add))
            link(dve.scalar_tensor_tensor(out=spl[:, 1], in0=spl[:, 0], scalar=0.0, in1=col(TW2), op0=ALU.max, op1=ALU.mult))
            link(dve.tensor_reduce(row16[:, 1, :], spl[:, 1], AX.X, ALU.add))
            link(dve.tensor_tensor(row16[:, 1, :], row16[:, 1, :], picked[:, :, TB2], ALU.add))
            link(dve.tensor_scalar(row16[:, 1, :], row16[:, 1, :], oscale[:, 0:1], None, ALU.mult))
            for b in range(NB):
                tr = range(TB * b, TB * b + TB)
                for t in tr:
                    ins = dve.scalar_tensor_tensor(out=y[:, t, :], in0=picked[:, t, TDIR:TABW], scalar=row16[:, 1, t:t + 1],
                                                   in1=xn[:, t, 0:D], op0=ALU.mult, op1=ALU.add)
                link(ins)
                n = tile_stats(y, tr)
                dve.wait_ge(rstd_ready, n)
                for t in tr:
                    ins = dve.tensor_scalar(y[:, t, :], y[:, t, :], mv[:, t, 0:1], rstd[:, t:t + 1], ALU.subtract, ALU.mult)
                ins.then_inc(yhat_ready, 1)

            def decayed_keys(b):
                for j in range(3):
                    n = min(3, TB - 3 * j)
                    name = f"ktok{b}.{j}"
                    filled(dve, name)
                    both = psum(name)[:, 0:(P + NE) * n].rearrange("p (a b) -> p a b", a=n)
                    dve.tensor_tensor(kd[b][:, 3 * j:3 * j + n, :], both[:, :, 0:P],
                                      bc(K("decay_k").unsqueeze(1), [P, n, P]), ALU.mult)
                    t = TB * b + 3 * j
                    ins = dve.tensor_tensor(r3(2)[:, t:t + n, :], both[:, :, P:P + NE],
                                            bc(gate_b[:, :].unsqueeze(1), [P, n, NE]), ALU.add).then_inc(bank_emptied[turn[name][0]], 1)

            dve.wait_ge(negent_ready, 1)
            dve.wait_ge(nexp_ready, 1)
            def residual(q):
                ts = slice(QT * q, QT * q + QT)
                for t in (QT * q + QT - 2, QT * q + QT - 1):
                    moved(dve, f"A{t}")
                link(dve.tensor_tensor(ratio[:, ts], s0[:, ts, D], nexp[:, ts], ALU.mult))
                link(dve.reciprocal(ratio[:, ts], ratio[:, ts]))
                link(dve.tensor_tensor(ratio[:, ts], ratio[:, ts], nexp[:, ts], ALU.mult))
                dve.wait_ge(silu_ready, q // 2 + 1)
                for t in range(QT * q, QT * q + QT):
                    ins = dve.scalar_tensor_tensor(out=s0[:, t, 0:D], in0=s0[:, t, 0:D], scalar=ratio[:, t:t + 1], in1=y[:, t, :],
                                                   op0=ALU.mult, op1=ALU.mult)
                link(ins)
                dve.tensor_tensor(x[:, ts, :], x[:, ts, :], s0[:, ts, 0:D], ALU.add).then_inc(x2_ready, 1)
                dve.wait_ge(x2_ready, q + 1)
                if q >= 2:
                    return tile_stats(x, range(QT * q, QT * q + QT))
                for t in range(QT * q, QT * q + QT):
                    ins = dve.bn_stats(stats[:, t, :], x[:, t, :])
                link(ins)
                for t in range(QT * q, QT * q + QT):
                    ins = dve.bn_aggr(mv[:, t, :], stats[:, t, :])
                link(ins)
                return variances(dve.tensor_scalar(nmean[:, ts], mv[:, ts, 0], -1.0, None, ALU.mult))

            def normalize2(q, n):
                dve.wait_ge(rstd_ready, n)
                for t in range(QT * q, QT * q + QT):
                    ins = dve.tensor_scalar(xn2[:, t, :], x[:, t, :], mv[:, t, 0:1], rstd[:, t:t + 1], ALU.subtract, ALU.mult)
                ins.then_inc(xn2_ready[q], 1)

            for q in range(2):
                residual(q)
            nth = [residual(q) for q in (2, 3)]
            for q in (2, 3):
                normalize2(q, nth[q - 2])
            decayed_keys(0)

            decayed_keys(1)
            for b in range(NB):
                for j in range(3):
                    moved(dve, f"ktok{b}.{j}")
            link(dve.tensor_reduce(row16[:, 2, :], r3(2), AX.X, ALU.max))
            dve.tensor_tensor(r3(0), r3(2), bc(row16[:, 2, :].unsqueeze(2), [P, NT, NE]), ALU.subtract).then_inc(lg_ready, 1)
            dve.wait_ge(lg_ready, 1)
            first_max(ohc[:, :, :], r3(0)).then_inc(exp_mask_ready, 1)

            def chunk_product(b, c):
                filled(dve, f"KV{b}.{c}")
                dve.tensor_tensor(kvm.rearrange("p e (t c) -> p e t c", c=CT)[:, :, :, c],
                                  psum(f"KV{b}.{c}")[:, 0:C * TB].rearrange("p (t e) -> p e t", e=C),
                                  bc(K("mask_kv").unsqueeze(2), [P, C, TB]), ALU.mult).then_inc(bank_emptied[2 + c], 1)

            def chunk_states(b):
                for c in range(CT):
                    moved(dve, f"KV{b}.{c}")
                dve.wait_ge(dtab_ready, 1)
                flat = lambda ap: ap.rearrange("p e c -> p (e c)")
                dve.tensor_tensor_scan(flat(state), dtab, flat(kvm), 0.0, ALU.mult, ALU.add).then_inc(state_ready, 1)

            def chunk_queries(q):
                filled(dve, f"QT{q}")
                if q >= 2:
                    filled(dve, f"y{q - 2}")
                dve.tensor_tensor(q_keep(q).rearrange("p (c i) -> p c i", c=CQ), psum(f"QT{q}")[:, :].rearrange("p (c i) -> p c i", c=CQ),
                                  bc(K("decay_q").unsqueeze(1), [P, CQ, C]), ALU.mult).then_inc(bank_emptied[0], 1)

            def chunk_value(q, i):
                if q >= 2 and i == 0:
                    filled(dve, f"y{q - 2}")
                name = f"vrep{q}.{i}"
                filled(dve, name)
                dve.tensor_tensor(vexp[q % 2][:, CT * i:CT * i + CT, :], psum(name)[:, :].rearrange("p (c a) -> p c a", c=CT),
                                  bc(K("mask_v").unsqueeze(1), [P, CT, P]), ALU.mult).then_inc(bank_emptied[turn[name][0]], 1)

            def chunk_operands(q):
                chunk_queries(q)
                for i in range(QT):
                    chunk_value(q, i)

            def chunk_decay(q, k):
                if q and k == 0:
                    filled(dve, f"y{q - 1}")
                name = f"R{q}.{k}"
                filled(dve, name)
                dve.tensor_tensor(smask[:, CT * k:CT * k + CT, :, :].rearrange("p c g i -> p c (g i)"),
                                  psum(name)[:, :].rearrange("p (c a) -> p c a", c=CT),
                                  bc(K("decay_s").unsqueeze(1), [P, CT, P]), ALU.mult).then_inc(bank_emptied[2 + k], 1)

            def chunk_decays(q):
                for k in range(QT):
                    chunk_decay(q, k)

            def dispatch_positions():
                filled(dve, "tot")
                dve.tensor_copy(rows(3).rearrange("p (e t) -> p e t", e=NE),
                                psum("tot")[:, 0:W].rearrange("p (t e) -> p e t", e=NE)).then_inc(bank_emptied[7], 1)
                moved(dve, "tot")
                link(dve.tensor_tensor_scan(rows(4), K("reset"), rows(3), 0.0, ALU.mult, ALU.add))
                link(dve.tensor_tensor(rows(5), rows(4), rows(3), ALU.subtract))
                filled(dve, "cum")
                dve.tensor_tensor(r3(2), psum("cum")[:, 0:W].rearrange("p (t e) -> p t e", e=NE),
                                  rows(5).rearrange("p (e t) -> p t e", e=NE), ALU.add).then_inc(bank_emptied[6], 1)
                moved(dve, "cum")
                link(dve.tensor_tensor(r3(2), r3(2), ohc[:, :, :], ALU.mult))
                link(dve.tensor_reduce(row16[:, 3, :], r3(2), AX.X, ALU.add))
                link(dve.tensor_tensor(r3(3), ohc[:, :, :], bc(K("slot0").unsqueeze(1), [P, NT, NE]), ALU.mult))
                link(dve.tensor_reduce(slotv[:, :], r3(3), AX.X, ALU.add))
                link(dve.tensor_tensor(slotv[:, :], slotv[:, :], row16[:, 3, :], ALU.add))
                link(dve.tensor_scalar(row16[:, 3, :], row16[:, 3, :], float(CAP), float(NOWHERE), ALU.is_gt, ALU.mult))
                link(dve.tensor_tensor(slotv[:, :], slotv[:, :], row16[:, 3, :], ALU.add))

            def slot_masks():
                for t in range(NT):
                    dve.tensor_scalar(slot_mask[:, t, :], K("iota"), slotv[:, t:t + 1], None, ALU.is_equal).then_inc(slotmask_ready, 1)
                dve.wait_ge(lgexp_ready, 1)
                link(dve.tensor_reduce(gpt[:, 0, :], r3(1), AX.X, ALU.add))
                link(dve.reciprocal(gpt[:, 0, :], gpt[:, 0, :]))
                dve.tensor_copy(info[:, :, 0:2], K("ids").rearrange("p (t k) -> p t k", k=2))
                dve.memset(info[:, :, 2:3], 1.0)
                link(dve.tensor_copy(info[:, :, 3], gpt[:, 0, :]))
                link(dve.tensor_tensor(gpt[:, 1, :], gpt[:, 0, :], info[:, :, 3], ALU.subtract))
                link(dve.tensor_copy(info[:, :, 4], gpt[:, 1, :]))
                link(dve.tensor_tensor(gpt[:, 2, :], gpt[:, 1, :], info[:, :, 4], ALU.subtract))
                dve.tensor_copy(info[:, :, 5], gpt[:, 2, :]).then_inc(info_ready, 1)

            def slot_indices():
                filled(dve, "idx")
                dve.tensor_copy(idx_f[:, :, :], psum("idx")[0:CAP, 0:8 * NE].rearrange("p (e k) -> p e k", e=NE)[:, :, 0:6])\
                    .then_inc(bank_emptied[6], 1)
                moved(dve, "idx")
                dve.tensor_tensor(idx_t[:, 0, :], idx_f[:, :, 0], idx_f[:, :, 1], ALU.add)
                dve.tensor_scalar(idx_t[:, 1, :], idx_f[:, :, 2], -1.0, 1.0, ALU.mult, ALU.add)
                link(dve.tensor_tensor(gprob[:, :], idx_f[:, :, 3], idx_f[:, :, 4], ALU.add))
                dve.tensor_tensor(gprob[:, :], gprob[:, :], idx_f[:, :, 5], ALU.add)
                dve.tensor_copy(idx_load[:, :], idx_t[:, 0, :])
                link(dve.tensor_tensor(idx_t[:, 2, :], idx_t[:, 1, :], K("oob", CAP), ALU.mult))
                dve.tensor_tensor(idx_store[:, :], idx_t[:, 2, :], idx_t[:, 0, :], ALU.add).then_inc(idx_ready, 1)

            def norm_begin(b):
                for q in (2 * b, 2 * b + 1):
                    moved(dve, f"y{q}")
                    ins = dve.bn_stats(gnst[:, q, :], yT[:, QW * q:QW * q + QW])
                link(ins)
                dve.bn_aggr(gns[:, b, 0:2], gnst[:, 2 * b:2 * b + 2, :].rearrange("p a b -> p (a b)")).then_inc(gn_mean, 1)

            def norm_middle(b):
                gv = lambda a, w=1: gns[:, b, a:a + w]
                filled(dve, f"gn{b}")
                dve.tensor_copy(gv(2, 2), psum(f"gn{b}")[:, 0:2]).then_inc(bank_emptied[turn[f"gn{b}"][0]], 1)
                moved(dve, f"gn{b}")
                link(dve.tensor_tensor(gv(8), gv(0), gv(2), ALU.subtract))
                dve.tensor_tensor(gv(4), gv(8), gv(8), ALU.mult).then_inc(gn_dev, 1)

            def norm_end(b):
                gv = lambda a, w=1: gns[:, b, a:a + w]
                filled(dve, f"gd{b}")
                dve.tensor_tensor(gv(5), psum(f"gd{b}")[:, 0:1], gv(3), ALU.add).then_inc(bank_emptied[turn[f"gd{b}"][0]], 1)
                moved(dve, f"gd{b}")
                n = variances(dve.tensor_copy(gv(9), gv(5)))
                dve.wait_ge(rstd_ready, n)
                link(dve.tensor_tensor(gv(7), gv(6), gnw[:, 0:1], ALU.mult))
                link(dve.tensor_tensor(gv(10), gv(2), gv(7), ALU.mult))
                link(dve.tensor_tensor(gv(11), gnw[:, 1:2], gv(10), ALU.subtract))
                for q in (2 * b, 2 * b + 1):
                    yq = yT[:, QW * q:QW * q + QW]
                    dve.tensor_scalar(yq, yq, gv(7), gv(11), ALU.mult, ALU.add).then_inc(yn_ready, 1)

            def gather_copies():
                for h in range(2):
                    filled(dve, f"xgT{h}")
                    dve.tensor_copy(xgT[:, 4 * h:4 * h + 4, :], psum(f"xgT{h}")[:, 0:4 * CAP].rearrange("p (e c) -> p e c", e=4))\
                        .then_inc(bank_emptied[turn[f"xgT{h}"][0]], 1)

            def hidden_sum(e):
                name = f"h{e}"
                filled(dve, name)
                dve.tensor_tensor(hb[:, e % 4], psum(name)[:, 0:FT * CAP].rearrange("p (f c) -> p f c", f=FT),
                                  bc(b1T[:, FT * e:FT * e + FT].unsqueeze(2), [P, FT, CAP]), ALU.add)\
                    .then_inc(bank_emptied[turn[name][0]], 1)

            def expert_sum(h):
                es = slice(2 * h, 2 * h + 2)
                filled(dve, f"eo{h}")
                dve.tensor_tensor(eo[:, es, :], psum(f"eo{h}")[0:CAP, 0:2 * D].rearrange("p (e d) -> p e d", e=2), b2r[:, es, :], ALU.add)\
                    .then_inc(bank_emptied[0], 1)
                moved(dve, f"eo{h}")
                ins = dve.tensor_tensor(eo[:, es, :], eo[:, es, :], bc(gprob[:, es].unsqueeze(2), [CAP, 2, D]), ALU.mult)
                if h % 2:
                    ins.then_inc(eo_ready, 1)
                else:
                    link(ins)

            def finish(q, half=None):
                name = f"s2_{q}" if half is None else f"s2_{q}.{half}"
                i0, n = (0, QT) if half is None else (2 * half, 2)
                ts = slice(QT * q + i0, QT * q + i0 + n)
                filled(dve, name)
                dve.wait_ge(g_in[q], 16)
                dve.tensor_tensor(g_tok[:, ts, :], psum(name)[:, P * i0:P * i0 + P * n].rearrange("p (a b) -> p a b", a=n),
                                  g_tok[:, ts, :], ALU.mult).then_inc(bank_emptied[turn[name][0]], 1)
                moved(dve, name)
                dve.tensor_tensor(x[:, ts, :], x[:, ts, :], g_tok[:, ts, :], ALU.add).then_inc(fin_ready, 1)

            chunk_queries(0)
            for c in range(CT):
                chunk_product(0, c)
                chunk_value(0, c)
            chunk_states(0)
            dispatch_positions()
            chunk_decays(0)
            chunk_operands(1)
            slot_masks()
            chunk_decays(1)
            slot_indices()
            chunk_queries(2)
            for c in range(CT):
                chunk_product(1, c)
                chunk_value(2, c)
            filled(dve, "y1")
            gather_copies()
            chunk_states(1)
            for e in range(4):
                hidden_sum(e)
            chunk_queries(3)
            norm_begin(0)
            norm_middle(0)
            expert_sum(0)
            expert_sum(1)
            for i in range(QT):
                chunk_value(3, i)
                if i < 2:
                    chunk_decay(2, i)
            hidden_sum(4)
            chunk_decay(2, 2)
            hidden_sum(5)
            chunk_decay(2, 3)
            hidden_sum(6)
            hidden_sum(7)
            norm_end(0)
            expert_sum(2)
            expert_sum(3)
            chunk_decays(3)
            norm_begin(1)
            norm_middle(1)
            norm_end(1)
            for q in range(NQ - 1):
                finish(q)
            for half in range(2):
                finish(NQ - 1, half)


def constants():
    import numpy as np
    p = np.arange(P)
    gamma = 1.0 - 2.0 ** (-5.0 - np.arange(H))
    c = {k: np.zeros((P, w)) for k, (_, w) in CONST_COLS.items()}
    c["ident"][:] = np.eye(P)
    c["tri"][:] = p[:, None] <= p[None, :]
    c["ones"][:] = 1
    c["avg8"][:] = (p[:, None] // DH == p[None, :] // DH) / DH
    m, j, i = p // C, p % C, np.arange(C)
    for g in range(NG):
        c["decay_s"][:, C * g:C * g + C] = np.where(i[None, :] >= j[:, None], gamma[GH * g + m][:, None] ** -j[:, None], 0)
    c["mask_v"][:] = m[:, None] == (p[None, :] // DH) % GH
    c["mask_kv"][:] = (p[:, None] // DH) % GH == np.arange(C)[None, :] // DH
    c["mask_q"][:] = (p[:, None] // C) == np.arange(NG)[None, :]
    c["mask_k"][:] = (p[:, None] // DH) % GH == np.arange(GH)[None, :]
    c["decay_k"][:] = gamma[p // DH][None, :] ** (C - j)[:, None]
    c["decay_q"][:] = gamma[p // DH][:, None] ** i[None, :] / np.sqrt(DH)
    c["gamma_c"][:] = gamma[p // DH][:, None] ** C
    c["thr"][:] = [-1] + list(range(1, NKNOT - 1)) + [1e30]
    c["rev"][:] = np.arange(NE, 0, -1)
    c["slot0"][:] = CAP * np.arange(NE) - 1
    c["iota"][:] = np.arange(SLOTS)
    c["ids"][:, 0::2] = p[:, None]
    c["ids"][:, 1::2] = P * np.arange(NT)
    c["oob"][:] = NOWHERE + p[:, None] * NE + np.arange(NE)
    c["reset"][:] = np.arange(NE * NT) % NT != 0
    for k in range(CT):
        c["repeat"][:, P * k:P * k + P] = p[:, None] == C * k + (p % C)[None, :]
    return np.concatenate([c[k] for k in CONST_COLS], axis=1).astype(np.float32)


_INS = ['L0_attn_x', 'L0_ffn_signatures_raw', 'L0_ffn_knot_values', 'L0_ffn_temperature', 'L0_ffn_compress_w1',
        'L0_ffn_compress_b1', 'L0_ffn_compress_w2', 'L0_ffn_compress_b2', 'L0_ffn_spline_w1', 'L0_ffn_spline_b1',
        'L0_ffn_spline_w2', 'L0_ffn_spline_b2', 'L0_ffn_directions', 'L0_ffn_norm_gamma', 'L0_ffn_norm_beta',
        'L0_ffn_output_scale', 'L1_attn_W_q', 'L1_attn_W_k', 'L1_attn_W_v', 'L1_attn_W_o', 'L1_attn_gn_weight',
        'L1_attn_gn_bias', 'L1_ffn_gate_w', 'L1_ffn_gate_b', 'L1_ffn_w1', 'L1_ffn_b1', 'L1_ffn_w2', 'L1_ffn_b2']


def kernel(**inputs):
    import numpy as _np
    import concourse.bacc as _bacc
    from concourse import mybir as _mybir
    from concourse.bass_utils import run_bass_kernel_spmd as _run

    nc = _bacc.Bacc("TRN2", target_bir_lowering=False, num_devices=1)
    arrays, args = {}, []
    for name in _INS:
        a = _np.ascontiguousarray(inputs[name])
        arrays[f"in_{name}"] = a
        args.append(nc.dram_tensor(f"in_{name}", a.shape, _mybir.dt.from_np(a.dtype), kind="ExternalInput").ap())
    a = constants()
    arrays["in_consts"] = a
    args.append(nc.dram_tensor("in_consts", a.shape, _mybir.dt.from_np(a.dtype), kind="ExternalInput").ap())
    args.append(nc.dram_tensor("out_0", (NB, SEQ, D), F32, kind="ExternalOutput").ap())
    kernel_program(nc, *args)
    r = _run(nc, [arrays], core_ids=[0])
    return r.results[0]["out_0"]
```
